# Optimizing a Trainium2 kernel written in Bass

```python
import numpy as np
import jax
import jax.numpy as jnp

def _softmax(x, axis=-1):
    return jax.nn.softmax(x, axis=axis)

def _gelu(x):
    return jax.nn.gelu(x, approximate=True)

def _silu(x):
    return jax.nn.silu(x)

def _sigmoid(x):
    return jax.nn.sigmoid(x)

def _layernorm(x, axis=-1, eps=1e-05):
    m = jnp.mean(x, axis=axis, keepdims=True)
    v = jnp.var(x, axis=axis, keepdims=True)
    return (x - m) / jnp.sqrt(v + eps)

def _scatter_add(tgt, idx, src, axis=0):
    return tgt.at[idx].add(src)

def _segment_sum(src, seg, n):
    return jax.ops.segment_sum(src, seg, n)
kernel_name = 'mk_flamingo_gated_d2_seqx_r4_2f54d1'

def setup_inputs(seed: int=0):
    np.random.seed(seed)
    _w = jnp.asarray

    def _rec_inputs():
        import jax
        import jax.numpy as jnp
        _rk = jax.random.key(seed)
        x = 7.22e-05 + 1 * jax.random.normal(jax.random.fold_in(_rk, 1), (8, 256, 512), jnp.float32)
        _lenS = 256 - jax.random.randint(jax.random.fold_in(_rk, 7), (8,), 0, max(1, 256 // 4) + 1, jnp.int32)
        _lenS2 = 256 - jax.random.randint(jax.random.fold_in(_rk, 8), (8,), 0, max(1, 256 // 4) + 1, jnp.int32)
        _ctx_2048P = jax.random.normal(jax.random.fold_in(_rk, 11), (8, 16, 512), jnp.float32)
        _ctx_2048c = jax.random.dirichlet(jax.random.fold_in(_rk, 511), 0.3 * jnp.ones((16,), jnp.float32), (8, 256))
        _ctx_2048t = jnp.einsum('bsk,bkd->bsd', _ctx_2048c, _ctx_2048P)
        _ctx_2048t = _ctx_2048t * jax.lax.rsqrt(jnp.mean(jnp.square(_ctx_2048t)) + 1e-12) * 0.953939
        ctx_2048 = 4.13588e-05 + 0.999923 * (_ctx_2048t + 0.3 * jax.random.normal(jax.random.fold_in(_rk, 611), (8, 256, 512), jnp.float32))
        _validS = jnp.arange(256)[None, :] < _lenS[:, None]
        _validS2 = jnp.arange(256)[None, :] < _lenS2[:, None]
        _causal = jnp.tril(jnp.ones((256, 256), dtype=bool))
        mask_Bx1xSxS_fk0 = jnp.where(jnp.broadcast_to(_validS[:, None, None, :], (8, 1, 256, 256)), -1000000000.0, 0.0).astype(jnp.float32)
        _g = jax.random.normal(jax.random.fold_in(_rk, 9001), (2, 2), jnp.float32)
        _g = jnp.sign(_g) * jnp.maximum(jnp.abs(_g), 1.0) + (_g == 0) * 1.0
        g_xattn = _g[0]
        g_ffn = _g[1]
        return (x, ctx_2048, mask_Bx1xSxS_fk0, g_xattn, g_ffn)
    x, ctx_2048, mask_Bx1xSxS_fk0, g_xattn, g_ffn = _rec_inputs()

    def _L0_xattn_setup():
        import jax, jax.numpy as jnp
        import numpy as np
        BS, S, DK = (8, 128, 512)
        key = jax.random.key(seed)
        kq, kk, kv = jax.random.split(key, 3)
        q = jax.random.normal(kq, (BS, S, DK), dtype=jnp.float32)
        k = jax.random.normal(kk, (BS, S, DK), dtype=jnp.float32)
        v = jax.random.normal(kv, (BS, S, DK), dtype=jnp.float32)
        return {'q': q, 'k': k, 'v': v}
    _L0_xattn_all = _L0_xattn_setup()
    _L0_xattn_in = {k: v for k, v in _L0_xattn_all.items() if k in ()}
    del _L0_xattn_all

    def _L0_ffn_setup():
        import jax, jax.numpy as jnp
        import numpy as np
        TOP_K = 6
        CAP_FACTOR = 2

        def _shared_swiglu(x, wg, wu, wd):
            return jax.nn.silu(x @ wg.T) * (x @ wu.T) @ wd.T
        key = jax.random.key(seed)
        ks = jax.random.split(key, 8)
        B, S, D, E, F, FS = (4, 512, 512, 64, 352, 704)
        scale = jnp.float32(0.02)
        return {'hidden_states': jax.random.normal(ks[0], (B, S, D), jnp.float32), 'gate_w': jax.random.normal(ks[1], (E, D), jnp.float32) * scale, 'w_gate': jax.random.normal(ks[2], (E, F, D), jnp.float32) * scale, 'w_up': jax.random.normal(ks[3], (E, F, D), jnp.float32) * scale, 'w_down': jax.random.normal(ks[4], (E, D, F), jnp.float32) * scale, 'sh_gate': jax.random.normal(ks[5], (FS, D), jnp.float32) * scale, 'sh_up': jax.random.normal(ks[6], (FS, D), jnp.float32) * scale, 'sh_down': jax.random.normal(ks[7], (D, FS), jnp.float32) * scale}
    _L0_ffn_all = _L0_ffn_setup()
    _L0_ffn_in = {k: v for k, v in _L0_ffn_all.items() if k in ('gate_w', 'w_gate', 'w_up', 'w_down', 'sh_gate', 'sh_up', 'sh_down')}
    del _L0_ffn_all

    def _L1_xattn_setup():
        import jax, jax.numpy as jnp
        import numpy as np
        import math
        B, S, HID, H = (2, 512, 512, 32)
        D = HID // H
        AL = 10

        def _rope_tables(seq_len, dim, dtype):
            inv_freq = 1.0 / 10000.0 ** (np.arange(0, dim, 2, dtype=np.float32) / dim)
            t = np.arange(seq_len, dtype=np.float32)
            freqs = np.outer(t, inv_freq)
            emb = np.concatenate([freqs, freqs], -1)
            return (jnp.asarray(np.cos(emb), dtype), jnp.asarray(np.sin(emb), dtype))

        def _rotate_half(x):
            x1, x2 = jnp.split(x, 2, axis=-1)
            return jnp.concatenate([-x2, x1], axis=-1)
        key = jax.random.key(seed)
        ks = jax.random.split(key, 8)
        hidden_states = jax.random.normal(ks[0], (B, S, HID), dtype=jnp.float32)
        adapter = jax.random.normal(ks[1], (B, AL, HID), dtype=jnp.float32)
        causal = jnp.tril(jnp.ones((S, S), dtype=bool))
        attention_mask = jnp.broadcast_to(jnp.where(causal, 0.0, -1000000000.0).astype(jnp.float32)[None, None], (B, 1, S, S))
        scale = 0.02
        Wq = jax.random.normal(ks[2], (HID, HID), dtype=jnp.float32) * scale
        Wk = jax.random.normal(ks[3], (HID, HID), dtype=jnp.float32) * scale
        Wv = jax.random.normal(ks[4], (HID, HID), dtype=jnp.float32) * scale
        Wo = jax.random.normal(ks[5], (HID, HID), dtype=jnp.float32) * scale
        gate = jax.random.normal(ks[6], (1, H, 1, 1), dtype=jnp.float32) * 0.1
        return {'hidden_states': hidden_states, 'attention_mask': attention_mask, 'adapter': adapter, 'Wq': Wq, 'Wk': Wk, 'Wv': Wv, 'Wo': Wo, 'gate': gate}
    _L1_xattn_all = _L1_xattn_setup()
    _L1_xattn_in = {k: v for k, v in _L1_xattn_all.items() if k in ('Wq', 'Wk', 'Wv', 'Wo', 'gate')}
    del _L1_xattn_all

    def _L1_ffn_setup():
        import jax, jax.numpy as jnp
        import numpy as np
        ALPHA = 1.702
        LIMIT = 7.0
        TOP_K = 2
        E, H, I = (8, 512, 512)
        B, S = (2, 512)
        key = jax.random.key(seed)
        ks = jax.random.split(key, 7)
        return {'hidden_states': jax.random.normal(ks[0], (B, S, H), dtype=jnp.float32), 'router_weight': jax.random.normal(ks[1], (E, H), dtype=jnp.float32) * 0.02, 'router_bias': jax.random.normal(ks[2], (E,), dtype=jnp.float32) * 0.02, 'gate_up_proj': jax.random.normal(ks[3], (E, H, 2 * I), dtype=jnp.float32) * 0.02, 'gate_up_proj_bias': jax.random.normal(ks[4], (E, 2 * I), dtype=jnp.float32) * 0.02, 'down_proj': jax.random.normal(ks[5], (E, I, H), dtype=jnp.float32) * 0.02, 'down_proj_bias': jax.random.normal(ks[6], (E, H), dtype=jnp.float32) * 0.02}
    _L1_ffn_all = _L1_ffn_setup()
    _L1_ffn_in = {k: v for k, v in _L1_ffn_all.items() if k in ('router_weight', 'router_bias', 'gate_up_proj', 'gate_up_proj_bias', 'down_proj', 'down_proj_bias')}
    del _L1_ffn_all
    return {'x': x, 'ctx_2048': ctx_2048, 'mask_Bx1xSxS_fk0': mask_Bx1xSxS_fk0, 'g_xattn': g_xattn, 'g_ffn': g_ffn, 'L0_ffn_gate_w': _L0_ffn_in['gate_w'], 'L0_ffn_w_gate': _L0_ffn_in['w_gate'], 'L0_ffn_w_up': _L0_ffn_in['w_up'], 'L0_ffn_w_down': _L0_ffn_in['w_down'], 'L0_ffn_sh_gate': _L0_ffn_in['sh_gate'], 'L0_ffn_sh_up': _L0_ffn_in['sh_up'], 'L0_ffn_sh_down': _L0_ffn_in['sh_down'], 'L1_xattn_Wq': _L1_xattn_in['Wq'], 'L1_xattn_Wk': _L1_xattn_in['Wk'], 'L1_xattn_Wv': _L1_xattn_in['Wv'], 'L1_xattn_Wo': _L1_xattn_in['Wo'], 'L1_xattn_gate': _L1_xattn_in['gate'], 'L1_ffn_router_weight': _L1_ffn_in['router_weight'], 'L1_ffn_router_bias': _L1_ffn_in['router_bias'], 'L1_ffn_gate_up_proj': _L1_ffn_in['gate_up_proj'], 'L1_ffn_gate_up_proj_bias': _L1_ffn_in['gate_up_proj_bias'], 'L1_ffn_down_proj': _L1_ffn_in['down_proj'], 'L1_ffn_down_proj_bias': _L1_ffn_in['down_proj_bias']}

def reference(x, ctx_2048, mask_Bx1xSxS_fk0, g_xattn, g_ffn, L0_ffn_gate_w, L0_ffn_w_gate, L0_ffn_w_up, L0_ffn_w_down, L0_ffn_sh_gate, L0_ffn_sh_up, L0_ffn_sh_down, L1_xattn_Wq, L1_xattn_Wk, L1_xattn_Wv, L1_xattn_Wo, L1_xattn_gate, L1_ffn_router_weight, L1_ffn_router_bias, L1_ffn_gate_up_proj, L1_ffn_gate_up_proj_bias, L1_ffn_down_proj, L1_ffn_down_proj_bias):
    import jax
    import jax.numpy as jnp

    def _L0_xattn_ref(q, k, v):
        import jax, jax.numpy as jnp
        import numpy as np
        BS, S, DK = (8, 128, 512)
        dk = q.shape[-1]
        scale = 1.0 / jnp.sqrt(jnp.asarray(dk, dtype=q.dtype))
        scaled = jnp.einsum('bsd,bse->bde', q, k) * scale
        attn = jax.nn.softmax(scaled, axis=1)
        out = jnp.einsum('bde,bse->bsd', attn, v)
        return out

    def _L0_ffn_ref(hidden_states, gate_w, w_gate, w_up, w_down, sh_gate, sh_up, sh_down):
        import jax, jax.numpy as jnp
        import numpy as np
        TOP_K = 6
        CAP_FACTOR = 2

        def _shared_swiglu(x, wg, wu, wd):
            return jax.nn.silu(x @ wg.T) * (x @ wu.T) @ wd.T
        B, S, D = hidden_states.shape
        E = gate_w.shape[0]
        x = hidden_states.reshape(-1, D)
        N = x.shape[0]
        A = N * TOP_K
        C = CAP_FACTOR * ((A + E - 1) // E)
        scores = jax.nn.softmax(x @ gate_w.T, axis=-1)
        topk_w, topk_idx = jax.lax.top_k(scores, TOP_K)
        topk_w = topk_w / (topk_w.sum(-1, keepdims=True) + 1e-20)
        flat_e = topk_idx.reshape(-1)
        flat_w = topk_w.reshape(-1)
        order = jnp.argsort(flat_e)
        se = flat_e[order]
        st = order // TOP_K
        sw = flat_w[order]
        counts = jnp.bincount(flat_e, length=E)
        offsets = jnp.cumsum(counts) - counts
        pos = jnp.arange(A) - offsets[se]
        valid = pos < C
        pos_c = jnp.minimum(pos, C - 1)
        buf = jnp.zeros((E, C, D), x.dtype).at[se, pos_c].add(jnp.where(valid[:, None], x[st], jnp.zeros((), x.dtype)))
        g = jnp.einsum('ecd,efd->ecf', buf, w_gate)
        u = jnp.einsum('ecd,efd->ecf', buf, w_up)
        eo = jnp.einsum('ecf,edf->ecd', jax.nn.silu(g) * u, w_down)
        gathered = eo[se, pos_c] * (sw * valid.astype(sw.dtype))[:, None]
        y = jnp.zeros_like(x).at[st].add(gathered).reshape(B, S, D)
        return y + _shared_swiglu(hidden_states, sh_gate, sh_up, sh_down)

    def _L1_xattn_ref(hidden_states, attention_mask, adapter, Wq, Wk, Wv, Wo, gate):
        import jax, jax.numpy as jnp
        import numpy as np
        import math
        B, S, HID, H = (2, 512, 512, 32)
        D = HID // H
        AL = 10

        def _rope_tables(seq_len, dim, dtype):
            inv_freq = 1.0 / 10000.0 ** (np.arange(0, dim, 2, dtype=np.float32) / dim)
            t = np.arange(seq_len, dtype=np.float32)
            freqs = np.outer(t, inv_freq)
            emb = np.concatenate([freqs, freqs], -1)
            return (jnp.asarray(np.cos(emb), dtype), jnp.asarray(np.sin(emb), dtype))

        def _rotate_half(x):
            x1, x2 = jnp.split(x, 2, axis=-1)
            return jnp.concatenate([-x2, x1], axis=-1)
        bsz, q_len, hid = hidden_states.shape
        n_heads = gate.shape[1]
        head_dim = hid // n_heads
        inv_sqrt_d = 1.0 / math.sqrt(head_dim)

        def split_heads(x, length):
            return x.reshape(bsz, length, n_heads, head_dim).transpose(0, 2, 1, 3)
        q = split_heads(hidden_states @ Wq, q_len)
        k = split_heads(hidden_states @ Wk, q_len)
        v = split_heads(hidden_states @ Wv, q_len)
        cos, sin = _rope_tables(q_len, head_dim, q.dtype)
        q = q * cos + _rotate_half(q) * sin
        k = k * cos + _rotate_half(k) * sin
        scores = jnp.einsum('bhqd,bhkd->bhqk', q, k) * inv_sqrt_d
        scores = scores + attention_mask
        scores = jnp.maximum(scores, jnp.finfo(scores.dtype).min)
        w = jax.nn.softmax(scores.astype(jnp.float32), axis=-1).astype(q.dtype)
        attn_output = jnp.einsum('bhqk,bhkd->bhqd', w, v)
        adapter_len = adapter.shape[1]
        a_k = split_heads(adapter @ Wk, adapter_len)
        a_v = split_heads(adapter @ Wv, adapter_len)
        a_scores = jnp.einsum('bhqd,bhkd->bhqk', q, a_k) * inv_sqrt_d
        a_scores = jnp.tanh(gate) * jax.nn.softmax(a_scores.astype(jnp.float32), axis=-1).astype(q.dtype)
        attn_output = attn_output + jnp.einsum('bhqk,bhkd->bhqd', a_scores, a_v)
        attn_output = attn_output.transpose(0, 2, 1, 3).reshape(bsz, q_len, hid)
        return attn_output @ Wo

    def _L1_ffn_ref(hidden_states, router_weight, router_bias, gate_up_proj, gate_up_proj_bias, down_proj, down_proj_bias):
        import jax, jax.numpy as jnp
        import numpy as np
        ALPHA = 1.702
        LIMIT = 7.0
        TOP_K = 2
        E, H, I = (8, 512, 512)
        B, S = (2, 512)
        bsz, seq_len, hidden = hidden_states.shape
        h = hidden_states.reshape(-1, hidden)
        T = h.shape[0]
        logits = h @ router_weight.T + router_bias
        top_vals, top_idx = jax.lax.top_k(logits, TOP_K)
        top_w = jax.nn.softmax(top_vals, axis=-1)
        scores = jnp.zeros_like(logits).at[jnp.arange(T)[:, None], top_idx].set(top_w)
        gate_up = jnp.einsum('th,ehj->etj', h, gate_up_proj) + gate_up_proj_bias[:, None, :]
        gate = gate_up[..., ::2]
        up = gate_up[..., 1::2]
        gate = jnp.minimum(gate, LIMIT)
        up = jnp.clip(up, -LIMIT, LIMIT)
        glu = gate * jax.nn.sigmoid(gate * ALPHA)
        act = (up + 1.0) * glu
        expert_out = jnp.einsum('eti,eih->eth', act, down_proj) + down_proj_bias[:, None, :]
        out = jnp.einsum('te,eth->th', scores, expert_out)
        return out.reshape(bsz, seq_len, hidden)
    x = x + jnp.tanh(g_xattn[0]) * _L0_xattn_ref(_layernorm(x, axis=-1), ctx_2048, ctx_2048)
    x = x + jnp.tanh(g_ffn[0]) * _L0_ffn_ref(_layernorm(x, axis=-1), L0_ffn_gate_w, L0_ffn_w_gate, L0_ffn_w_up, L0_ffn_w_down, L0_ffn_sh_gate, L0_ffn_sh_up, L0_ffn_sh_down)
    x = x + jnp.tanh(g_xattn[1]) * _L1_xattn_ref(_layernorm(x, axis=-1), mask_Bx1xSxS_fk0, ctx_2048, L1_xattn_Wq, L1_xattn_Wk, L1_xattn_Wv, L1_xattn_Wo, L1_xattn_gate)
    x = x + jnp.tanh(g_ffn[1]) * _L1_ffn_ref(_layernorm(x, axis=-1), L1_ffn_router_weight, L1_ffn_router_bias, L1_ffn_gate_up_proj, L1_ffn_gate_up_proj_bias, L1_ffn_down_proj, L1_ffn_down_proj_bias)
    return x

_drawn_inputs = setup_inputs


def setup_inputs(seed=0):
    import zlib

    import numpy as np

    out = dict(_drawn_inputs(seed))
    spreads = {'g_ffn': (-1.0, 0.6)}
    factors = {'L0_ffn_gate_w': 4.101,
     'L0_ffn_w_gate': 3.884,
     'L0_ffn_w_up': 3.892,
     'L0_ffn_w_down': 3.813,
     'L1_xattn_Wq': 6.575,
     'L1_xattn_Wk': 6.814,
     'L1_xattn_gate': 4.721,
     'L1_ffn_router_bias': 4.948,
     'L1_ffn_gate_up_proj_bias': 8.0,
     'L1_ffn_down_proj_bias': 5.045}
    for name, (base, spread) in spreads.items():
        noise = np.random.default_rng([zlib.crc32(name.encode()), seed]).standard_normal(out[name].shape)
        drawn = base * np.exp(spread * noise) if base else spread * noise
        out[name] = jnp.asarray(drawn.astype(out[name].dtype))
    for name, factor in factors.items():
        out[name] = (out[name] * factor).astype(out[name].dtype)
    return out
```

```python
import concourse.bass as bass
from concourse import mybir
from contextlib import ExitStack

F32 = mybir.dt.float32
U32 = mybir.dt.uint32
F32R = mybir.dt.float32r
ALU = mybir.AluOpType
ACT = mybir.ActivationFunctionType
AX = mybir.AxisListType
ds = bass.ds

P = 128
B, S, D = 8, 256, 512
T = B * S
TT = T // P
ST = S // P
DC = D // P
EPS = 1e-5

E0, K0, F0 = 64, 6, 352
CAP = 2 * ((T * K0 + E0 - 1) // E0)
CT = CAP // P
SLOTS = E0 * CAP
FT0 = [(f, min(P, F0 - f)) for f in range(0, F0, P)]
FS = 704
FTS = [(0, P), (P, P), (2 * P, P), (3 * P, P), (4 * P, 96), (4 * P + 96, 96)]
NTOK = 512

NH, HD = 32, 16
E1, I1, K1 = 8, 512, 2
LIMIT, ALPHA = 7.0, 1.702
FMIN = -3.4028234663852886e38
MARK = 3.0e38


class Serial:

    def __init__(self, eng, sem, base, steps):
        self.eng, self.sem, self.base, self.steps, self.n = eng, sem, base, steps, 0

    def __call__(self, ins):
        self.n += 1
        ins.then_inc(self.sem, 1)
        self.eng.wait_ge(self.sem, self.base + self.n)

    def later(self, ins):
        self.n += 1
        ins.then_inc(self.sem, 1)

    def all(self):
        self.eng.wait_ge(self.sem, self.base + self.n)

    def close(self):
        assert self.n == self.steps, self.n


class Phase:

    def __init__(self, nc, ctx, prefix):
        self.nc, self.ctx, self.prefix = nc, ctx, prefix

    def sb(self, name, shape, dt=F32):
        return self.ctx.enter_context(self.nc.sbuf_tensor(self.prefix + name, shape, dt))

    def ps(self, name, shape):
        return self.ctx.enter_context(self.nc.psum_tensor(self.prefix + name, shape, F32))

    def sem(self, name):
        return self.ctx.enter_context(self.nc.semaphore(self.prefix + name))

    def sems(self, names):
        return [self.sem(n) for n in names.split()]


def row(x, i):
    return x[:, ds(i, 1), :].rearrange("p o d -> p (o d)")


def row_stats(dve, step, t, stats6):
    for i in range(TT):
        step(dve.bn_stats(stats6[:, i, :], t.x[:, i, :]))
    for i in range(TT):
        step(dve.bn_aggr(t.mv[:, i, :], stats6[:, i, :]))


ROW_STATS = 2 * TT


def row_rstd(pool, step, t):
    step(pool.tensor_scalar(t.vareps[:, :], t.mv[:, :, 1], EPS, None, ALU.add))
    step(pool.tensor_tensor(t.rstd[:, :], t.vareps[:, :], t.minus_half[:, :], ALU.pow))


class Shared:
    pass


def load_constants(nc, t, d):
    with ExitStack() as ctx:
        ph = Phase(nc, ctx, "i_")
        raw = ph.sb("raw", [P, 4])
        const_in, = ph.sems("const_in")
        block = ctx.enter_context(nc.Block())

        @block.sync
        def _(sp):
            sp.dma_start(t.ident[:, :], d["ident"]).then_inc(const_in, 16)
            sp.dma_start(t.before[:, :], d["before"]).then_inc(const_in, 16)
            sp.dma_start(raw[:, :], d["gates"]).then_inc(const_in, 16)
            sp.dma_start(t.x[:, :, :], d["x"].rearrange("b (t p) d -> p (b t) d", p=P)).then_inc(const_in, 16)
            sp.wait_ge(const_in, 64)

        @block.vector
        def _(dve):
            dve.memset(t.ones[:, :], 1.0)
            dve.memset(t.minus_half[:, :], -0.5)

        @block.scalar
        def _(act):
            act.wait_ge(const_in, 64)
            act.activation(t.gates[:, :], raw[:, :], ACT.Tanh)


def layer0_attention(nc, t, d):
    scale = D ** -0.5
    zrows = 8
    nz = SLOTS // (P * zrows)
    slots_z = d["slots"].rearrange("(n p r) d -> n p (r d)", p=P, r=zrows)
    with ExitStack() as ctx:
        ph = Phase(nc, ctx, "a_")
        cn = [ph.sb(f"cn{p}", [P, ST, D]) for p in range(2)]
        ct = [ph.sb(f"ct{p}", [P, DC, S]) for p in range(2)]
        cts = [ph.sb(f"cts{p}", [P, DC, S]) for p in range(2)]
        q = [ph.sb(f"q{p}", [P, ST, D]) for p in range(2)]
        prob = [ph.sb(f"prob{p}", [P, DC, D]) for p in range(2)]
        stats6 = ph.sb("stats6", [P, TT, 6])
        nmax = ph.sb("nmax", [P, DC])
        nb = [ph.sb(f"nb{p}", [P, DC]) for p in range(2)]
        ssum = [ph.sb(f"ssum{p}", [P, DC]) for p in range(2)]
        rsum = ph.sb("rsum", [P, DC])
        zero = ph.sb("zero", [P, zrows * D])
        score = [ph.ps(f"score{e}", [P, D]) for e in range(DC)]
        out = [ph.ps(f"out{s}", [P, D]) for s in range(ST)]
        ctx_in = [ph.sem(f"ctx_in{p}") for p in range(2)]
        stats_ready, rstd_ready, q_ready, score_ready, bias_ready, prob_ready = ph.sems(
            "stats_ready rstd_ready q_ready score_ready bias_ready prob_ready")
        ctx_scaled, out_ready, x_added, batch_done, dve_step, pool_step, zero_ready, zeroed = ph.sems(
            "ctx_scaled out_ready x_added batch_done dve_step pool_step zero_ready zeroed")
        block = ctx.enter_context(nc.Block())

        @block.sync
        def _(sp):
            with sp.Fori(0, B // 2) as j:
                for p in range(2):
                    b = 2 * j + p
                    sp.wait_ge(batch_done, b + 1)
                    sp.dma_start(cn[p][:, :, :], d["ctx"][ds(b, 1), :, :].rearrange("o (t p) d -> p (o t) d", p=P)).then_inc(ctx_in[p], 16)
                    sp.dma_start(ct[p][:, :, :], d["ctx_t"][ds(b, 1), :, :].rearrange("o (c p) s -> p (o c) s", p=P)).then_inc(ctx_in[p], 16)

        @block.gpsimd
        def _(pool):
            pool.sem_inc(batch_done, 2)
            pool.memset(zero[:, :], 0.0).then_inc(zero_ready, 1)
            pool.wait_ge(stats_ready, 1)
            row_rstd(pool, Serial(pool, pool_step, 0, 2), t)
            pool.sem_inc(rstd_ready, 1)

        @block.vector
        def _(dve):
            row_stats(dve, Serial(dve, dve_step, 0, ROW_STATS), t, stats6)
            dve.sem_inc(stats_ready, 1)
            dve.wait_ge(rstd_ready, 1)
            steps = 2 * DC
            with dve.Fori(0, B // 2) as j:
                for p in range(2):
                    b = 2 * j + p
                    step = Serial(dve, dve_step, ROW_STATS + b * steps, steps)
                    dve.wait_ge(batch_done, b + 1)
                    for s in range(ST):
                        dve.tensor_scalar(q[p][:, s, :], row(t.x, ST * b + s), t.mv_at(ST * b + s, 0), t.rstd_at(ST * b + s),
                                          ALU.subtract, ALU.mult).then_inc(q_ready, 1)
                    dve.wait_ge(ctx_in[p], 32 * (j + 1))
                    for e in range(DC):
                        dve.wait_ge(score_ready, DC * b + e + 1)
                        step(dve.reduce_max(nmax[:, e:e + 1], score[e][:, :], axis=AX.X))
                        dve.tensor_scalar(nb[p][:, e:e + 1], nmax[:, e:e + 1], -scale, None, ALU.mult).then_inc(bias_ready, 1)
                    for e in range(DC):
                        dve.wait_ge(prob_ready, DC * b + e + 1)
                        step(dve.reciprocal(rsum[:, e:e + 1], ssum[p][:, e:e + 1]))
                        dve.tensor_scalar(cts[p][:, e, :], ct[p][:, e, :], rsum[:, e:e + 1], None, ALU.mult).then_inc(ctx_scaled, 1)
                    for s in range(ST):
                        dve.wait_ge(out_ready, ST * b + s + 1)
                        xs = row(t.x, ST * b + s)
                        dve.scalar_tensor_tensor(out=xs, in0=out[s][:, :], scalar=t.gates[:, 0:1], in1=xs,
                                                 op0=ALU.mult, op1=ALU.add).then_inc(x_added, 1)
                    dve.sem_inc(batch_done, 1)
                    step.close()

        @block.scalar
        def _(act):
            act.wait_ge(zero_ready, 1)
            with act.Fori(0, nz) as n:
                act.dma_start(slots_z[ds(n, 1), :, :].rearrange("o p f -> (o p) f"), zero[:, :]).then_inc(zeroed, 16)
            with act.Fori(0, B // 2) as j:
                for p in range(2):
                    b = 2 * j + p
                    act.wait_ge(batch_done, b + 1)
                    for e in range(DC):
                        act.wait_ge(bias_ready, DC * b + e + 1)
                        act.activation(prob[p][:, e, :], score[e][:, :], ACT.Exp, bias=nb[p][:, e:e + 1], scale=scale,
                                       accum_out=ssum[p][:, e:e + 1]).then_inc(prob_ready, 1)
            act.wait_ge(zeroed, 16 * nz)

        @block.tensor
        def _(pe):
            pe.sem_inc(x_added, ST)
            with pe.Fori(0, B // 2) as j:
                for p in range(2):
                    b = 2 * j + p
                    pe.wait_ge(ctx_in[p], 32 * (j + 1))
                    pe.wait_ge(q_ready, ST * b + ST)
                    for e in range(DC):
                        for s in range(ST):
                            mm = pe.matmul(score[e][:, :], cn[p][:, s, e * P:(e + 1) * P], q[p][:, s, :], start=(s == 0), stop=(s == ST - 1))
                        mm.then_inc(score_ready, 1)
                    for s in range(ST):
                        pe.wait_ge(x_added, ST * b + s + 1)
                        for e in range(DC):
                            if s == 0:
                                pe.wait_ge(ctx_scaled, DC * b + e + 1)
                            mm = pe.matmul(out[s][:, :], cts[p][:, e, s * P:(s + 1) * P], prob[p][:, e, :], start=(e == 0), stop=(e == DC - 1))
                        mm.then_inc(out_ready, 1)


def transposed_tile(pe, psum, src, t):
    for c in range(DC):
        mm = pe.transpose(psum[:, c * P:(c + 1) * P], src[:, c * P:(c + 1) * P], t.ident[:, :])
    return mm


def route(nc, t, d):
    W = E0 + 2
    with ExitStack() as ctx:
        ph = Phase(nc, ctx, "r_")
        stats6 = ph.sb("stats6", [P, TT, 6])
        gate_wt = ph.sb("gate_wt", [P, DC, E0])
        slot_base = ph.sb("slot_base", [P, E0])
        xns = [ph.sb(f"xns{p}", [P, D]) for p in range(2)]
        xts = [ph.sb(f"xts{p}", [P, D]) for p in range(2)]
        logit = ph.sb("logit", [P, TT, E0])
        score = ph.sb("score", [P, TT, W])
        taken = ph.sb("taken", [P, TT, W])
        chosen = ph.sb("chosen", [P, TT, E0])
        chosen_before = ph.sb("chosen_before", [P, TT + 1, E0])
        wsel = ph.sb("wsel", [P, TT, E0])
        place = ph.sb("place", [P, TT, E0])
        top = ph.sb("top", [P, TT, 8])
        small = ph.sb("small", [P, TT])
        tp = [ph.ps(f"tp{p}", [P, D]) for p in range(2)]
        lg = ph.ps("lg", [P, D])
        count = ph.ps("count", [P, TT, E0])
        weights_in, stats_ready, rstd_ready, xn_ready, xn_copied, tp_ready, xts_ready, xt_ready, logit_ready, logit_out = ph.sems(
            "weights_in stats_ready rstd_ready xn_ready xn_copied tp_ready xts_ready xt_ready logit_ready logit_out")
        exp_asked, exp_ready, chosen_ready, counted, dve_step, pool_step = ph.sems(
            "exp_asked exp_ready chosen_ready counted dve_step pool_step")
        block = ctx.enter_context(nc.Block())

        def over(x):
            return x[:, :].unsqueeze(2).to_broadcast([P, TT, E0])

        @block.sync
        def _(sp):
            sp.dma_start(gate_wt[:, :, :], d["gate_wt"].rearrange("(c p) e -> p c e", p=P)).then_inc(weights_in, 16)
            sp.dma_start(slot_base[:, :], d["slot_base"]).then_inc(weights_in, 16)

        @block.gpsimd
        def _(pool):
            pool.sem_inc(xn_copied, 2)
            pool.sem_inc(xt_ready, 2)
            pool.wait_ge(stats_ready, 1)
            row_rstd(pool, Serial(pool, pool_step, 0, 2), t)
            pool.sem_inc(rstd_ready, 1)
            with pool.Fori(0, TT // 2) as j:
                for p in range(2):
                    i = 2 * j + p
                    pool.wait_ge(xn_ready, i + 1)
                    pool.tensor_copy(row(t.xn, i), xns[p][:, :]).then_inc(xn_copied, 1)
                    pool.wait_ge(xts_ready, i + 1)
                    pool.tensor_copy(t.xt[:, :, ds(i * P, P)], xts[p][:, :].rearrange("p (c s) -> p c s", c=DC)).then_inc(xt_ready, 1)

        @block.scalar
        def _(act):
            with act.Fori(0, TT // 2) as j:
                for p in range(2):
                    i = 2 * j + p
                    act.wait_ge(tp_ready, 2 + i + 1)
                    act.wait_ge(xt_ready, i + 1)
                    act.wait_ge(logit_ready, i + 1)
                    act.activation(xts[p][:, :], tp[p][:, :], ACT.Copy).then_inc(xts_ready, 1)
                    act.wait_ge(logit_ready, 2 + i + 1)
                    act.activation(row(logit, i), lg[:, 0:E0], ACT.Copy).then_inc(logit_out, 1)
            act.wait_ge(exp_asked, 1)
            act.activation(logit[:, :, :], logit[:, :, :], ACT.Exp).then_inc(exp_ready, 1)

        @block.vector
        def _(dve):
            row_stats(dve, Serial(dve, dve_step, 0, ROW_STATS), t, stats6)
            dve.sem_inc(stats_ready, 1)
            dve.wait_ge(rstd_ready, 1)
            with dve.Fori(0, TT // 2) as j:
                for p in range(2):
                    i = 2 * j + p
                    dve.wait_ge(tp_ready, i + 1)
                    dve.wait_ge(xn_copied, i + 1)
                    dve.tensor_scalar(xns[p][:, :], row(t.x, i), t.mv_at(i, 0), t.rstd_at(i), ALU.subtract, ALU.mult).then_inc(xn_ready, 1)
            dve.wait_ge(logit_out, 1 + TT)
            step = Serial(dve, dve_step, ROW_STATS, 1 + 4 + TT + 1 + TT + 2 + (TT - 1) + 4 + 5 + TT + 1 + 3 * K0 + 1)
            step(dve.reduce_max(small[:, :], logit[:, :, :], axis=AX.X))
            dve.tensor_tensor(logit[:, :, :], logit[:, :, :], over(small), ALU.subtract).then_inc(exp_asked, 1)
            step(dve.memset(score[:, :, E0:W], -1.0))
            dve.wait_ge(exp_ready, 1)
            step(dve.reduce_sum(small[:, :], logit[:, :, :], axis=AX.X))
            step(dve.reciprocal(small[:, :], small[:, :]))
            step(dve.tensor_tensor(score[:, :, 0:E0], logit[:, :, :], over(small), ALU.mult))
            for i in range(TT):
                step(dve.max(top[:, i, :], score[:, i, :]))
            step(dve.memset(top[:, :, K0:8], -1.0))
            for i in range(TT):
                step(dve.match_replace(taken[:, i, :], top[:, i, :], score[:, i, :], MARK))
            step(dve.tensor_scalar(chosen[:, :, :], taken[:, :, 0:E0], MARK, None, ALU.is_equal))
            step(dve.memset(chosen_before[:, 0, :], 0.0))
            for i in range(1, TT + 1):
                ins = dve.tensor_tensor(chosen_before[:, i, :], chosen_before[:, i - 1, :], chosen[:, i - 1, :], ALU.add)
                if i == TT:
                    ins.then_inc(chosen_ready, 1)
                else:
                    step(ins)
            step(dve.reduce_sum(small[:, :], top[:, :, 0:K0], axis=AX.X))
            step(dve.tensor_scalar(small[:, :], small[:, :], 1e-20, None, ALU.add))
            step(dve.reciprocal(small[:, :], small[:, :]))
            step(dve.tensor_tensor(wsel[:, :, :], score[:, :, 0:E0], over(small), ALU.mult))
            dve.wait_ge(counted, TT + 1)
            step(dve.tensor_copy(t.load[:, :], lg[:, 0:E0]))
            step(dve.tensor_scalar(taken[:, :, 0:E0], count[:, :, :], float(CAP), None, ALU.is_lt))
            step(dve.tensor_tensor(chosen[:, :, :], chosen[:, :, :], taken[:, :, 0:E0], ALU.mult))
            step(dve.tensor_tensor(place[:, :, :], count[:, :, :], slot_base[:, :].unsqueeze(1).to_broadcast([P, TT, E0]), ALU.add))
            step(dve.tensor_tensor(place[:, :, :], place[:, :, :], chosen[:, :, :], ALU.mult))
            step(dve.tensor_tensor(wsel[:, :, :], wsel[:, :, :], chosen[:, :, :], ALU.mult))
            for i in range(TT):
                step(dve.max(t.addr[:, i, :], place[:, i, :]))
            step(dve.tensor_scalar(wsel[:, :, :], wsel[:, :, :], t.gates[:, 1:2], None, ALU.mult))
            for k in range(K0):
                slot = t.addr[:, :, k].unsqueeze(2).to_broadcast([P, TT, E0])
                step(dve.tensor_tensor(taken[:, :, 0:E0], place[:, :, :], slot, ALU.is_equal))
                step(dve.tensor_tensor(taken[:, :, 0:E0], taken[:, :, 0:E0], wsel[:, :, :], ALU.mult))
                step(dve.reduce_sum(t.weight[:, :, k], taken[:, :, 0:E0], axis=AX.X))
            step.close()

        @block.tensor
        def _(pe):
            pe.sem_inc(tp_ready, 2)
            pe.sem_inc(logit_ready, 2)
            pe.sem_inc(logit_out, 1)
            pe.wait_ge(weights_in, 32)
            with pe.Fori(0, TT // 2) as j:
                for p in range(2):
                    i = 2 * j + p
                    pe.wait_ge(xn_ready, i + 1)
                    transposed_tile(pe, tp[p], xns[p], t).then_inc(tp_ready, 1)
                    pe.wait_ge(xts_ready, i + 1)
                    pe.wait_ge(logit_out, i + 1)
                    for c in range(DC):
                        mm = pe.matmul(lg[:, 0:E0], xts[p][:, c * P:(c + 1) * P], gate_wt[:, c, :], start=(c == 0), stop=(c == DC - 1))
                    mm.then_inc(logit_ready, 1)
            pe.wait_ge(chosen_ready, 1)
            for i in range(TT):
                pe.matmul(count[:, i, :], t.before[:, :], chosen[:, i, :], start=True, stop=False)
                mm = pe.matmul(count[:, i, :], t.ones[:, :], chosen_before[:, i, :], start=False, stop=True)
                mm.then_inc(counted, 1)
            pe.matmul(lg[:, 0:E0], t.ones[:, :], chosen_before[:, TT, :], start=True, stop=True).then_inc(counted, 1)


def dispatch(nc, t, d):
    with ExitStack() as ctx:
        ph = Phase(nc, ctx, "s_")
        big = ph.sb("big", [P, TT, 8])
        addr_f = ph.sb("addr_f", [P, TT, 8])
        rows = [ph.sb(f"rows{p}", [P, D]) for p in range(2)]
        to = [ph.sb(f"to{p}", [P, 8], U32) for p in range(2)]
        wg = ph.sb("wg", [P, DC, FS])
        wu = ph.sb("wu", [P, DC, FS])
        wd = ph.sb("wd", [P, len(FTS), D])
        sg = [ph.sb(f"sg{p}", [P, NTOK]) for p in range(2)]
        h = ph.sb("h", [P, len(FTS), NTOK])
        pg = [ph.ps(f"pg{p}", [P, NTOK]) for p in range(2)]
        pu = [ph.ps(f"pu{p}", [P, NTOK]) for p in range(2)]
        po = [ph.ps(f"po{p}", [P, D]) for p in range(2)]
        weights_in, addr_ready, staged, tiles_staged, gate_done, up_done, silu_ready, h_ready, out_done, x_added = ph.sems(
            "weights_in addr_ready staged tiles_staged gate_done up_done silu_ready h_ready out_done x_added")
        scattered = [ph.sem(f"scattered{p}") for p in range(2)]
        block = ctx.enter_context(nc.Block())
        NF = len(FTS)

        @block.sync
        def _(sp):
            sp.dma_start(wg[:, :, :], d["sh_gate"].rearrange("(c p) f -> p c f", p=P)).then_inc(weights_in, 16)
            sp.dma_start(wu[:, :, :], d["sh_up"].rearrange("(c p) f -> p c f", p=P)).then_inc(weights_in, 16)
            for k, (f, n) in enumerate(FTS):
                sp.dma_start(wd[0:n, k, :], d["sh_down"][f:f + n, :]).then_inc(weights_in, 16)

        @block.gpsimd
        def _(pool):
            pool.tensor_scalar(big[:, :, :], t.addr[:, :, :], 0.0, float(2 * SLOTS), ALU.is_equal, ALU.mult).then_inc(addr_ready, 1)
            pool.wait_ge(addr_ready, 1)
            pool.tensor_tensor(big[:, :, :], big[:, :, :], t.addr[:, :, :], ALU.add).then_inc(addr_ready, 1)
            pool.wait_ge(addr_ready, 2)
            pool.tensor_scalar(addr_f[:, :, :], big[:, :, :], -1.0, None, ALU.add).then_inc(addr_ready, 1)

            def scatter(j, p):
                i = 2 * j + p
                pool.tensor_copy(rows[p][:, :], row(t.xn, i)).then_inc(staged, 1)
                pool.tensor_copy(to[p][:, :], row(addr_f, i)).then_inc(staged, 1)
                pool.wait_ge(staged, 2 * i + 2)
                pool.sem_inc(tiles_staged, 1)
                for k in range(K0):
                    pool.indirect_dma_start(out=d["slots"], out_offset=bass.IndirectOffsetOnAxis(ap=to[p][:, k:k + 1], axis=0),
                                            in_=rows[p][:, :], in_offset=None, bounds_check=SLOTS - 1, oob_is_err=False).then_inc(scattered[p], 16)

            pool.wait_ge(addr_ready, 3)
            for p in range(2):
                scatter(0, p)
            with pool.Fori(1, TT // 2) as j:
                for p in range(2):
                    pool.wait_ge(scattered[p], 16 * K0 * j)
                    scatter(j, p)
            for p in range(2):
                pool.wait_ge(scattered[p], 16 * K0 * (TT // 2))

        @block.scalar
        def _(act):
            with act.Fori(0, T // NTOK) as n:
                for k, (f, m) in enumerate(FTS):
                    u = n * NF + k
                    act.wait_ge(gate_done, u + 1)
                    act.wait_ge(h_ready, u + 1)
                    act.activation(sg[k % 2][0:m, :], pg[k % 2][0:m, :], ACT.Silu).then_inc(silu_ready, 1)

        @block.vector
        def _(dve):
            dve.sem_inc(h_ready, 2)
            dve.sem_inc(x_added, 2)
            with dve.Fori(0, T // NTOK) as n:
                for k, (f, m) in enumerate(FTS):
                    u = n * NF + k
                    dve.wait_ge(up_done, u + 1)
                    dve.wait_ge(silu_ready, u + 1)
                    dve.tensor_tensor(h[0:m, k, :], sg[k % 2][0:m, :], pu[k % 2][0:m, :], ALU.mult).then_inc(h_ready, 1)
                for s in range(NTOK // P):
                    dve.wait_ge(out_done, n * (NTOK // P) + s + 1)
                    xs = row(t.x, n * (NTOK // P) + s)
                    dve.scalar_tensor_tensor(out=xs, in0=po[s % 2][:, :], scalar=t.gates[:, 1:2], in1=xs,
                                             op0=ALU.mult, op1=ALU.add).then_inc(x_added, 1)

        @block.tensor
        def _(pe):
            pe.wait_ge(weights_in, 16 * (2 + NF))
            with pe.Fori(0, T // NTOK) as n:
                for k, (f, m) in enumerate(FTS):
                    u = n * NF + k
                    pe.wait_ge(h_ready, u + 1)
                    for c in range(DC):
                        mm = pe.matmul(pg[k % 2][0:m, :], wg[:, c, f:f + m], t.xt[:, c, ds(n * NTOK, NTOK)], start=(c == 0), stop=(c == DC - 1))
                    mm.then_inc(gate_done, 1)
                    for c in range(DC):
                        mm = pe.matmul(pu[k % 2][0:m, :], wu[:, c, f:f + m], t.xt[:, c, ds(n * NTOK, NTOK)], start=(c == 0), stop=(c == DC - 1))
                    mm.then_inc(up_done, 1)
                pe.wait_ge(h_ready, n * NF + NF + 2)
                for s in range(NTOK // P):
                    pe.wait_ge(x_added, n * (NTOK // P) + s + 1)
                    for k, (f, m) in enumerate(FTS):
                        mm = pe.matmul(po[s % 2][:, :], h[0:m, k, s * P:(s + 1) * P], wd[0:m, k, :], start=(k == 0), stop=(k == NF - 1))
                    mm.then_inc(out_done, 1)


def experts(nc, t, d):
    with ExitStack() as ctx:
        ph = Phase(nc, ctx, "e_")
        NF = len(FT0)
        wg = [ph.sb(f"wg{p}", [P, DC, F0]) for p in range(2)]
        wu = [ph.sb(f"wu{p}", [P, DC, F0]) for p in range(2)]
        wd = [ph.sb(f"wd{p}", [P, NF, D]) for p in range(2)]
        xs = [ph.sb(f"xs{p}", [P, CT, D]) for p in range(2)]
        xt = [ph.sb(f"xt{p}", [P, DC, CAP]) for p in range(2)]
        sg = [ph.sb(f"sg{p}", [P, CAP]) for p in range(2)]
        h = [ph.sb(f"h{p}", [P, NF, CAP]) for p in range(2)]
        eo = [ph.sb(f"eo{p}", [P, CT, D]) for p in range(2)]
        tp = [ph.ps(f"tp{p}", [P, D]) for p in range(2)]
        pg = [ph.ps(f"pg{p}", [P, D]) for p in range(2)]
        pu = [ph.ps(f"pu{p}", [P, D]) for p in range(2)]
        po = [ph.ps(f"po{p}", [P, D]) for p in range(2)]
        weights_in = [ph.sem(f"weights_in{p}") for p in range(2)]
        xs_in = [ph.sem(f"xs_in{p}") for p in range(2)]
        stored = [ph.sem(f"stored{p}") for p in range(2)]
        tp_ready, xt_ready, gate_done, up_done, silu_ready, h_ready, out_done, eo_ready = ph.sems(
            "tp_ready xt_ready gate_done up_done silu_ready h_ready out_done eo_ready")
        block = ctx.enter_context(nc.Block())

        def by_load(eng, e, body):
            load = eng.value_load(t.load[0:1, ds(e, 1)], min_val=0, max_val=T)
            with eng.If(load > (CT - 1) * P):
                body(CT)
            with eng.Else():
                body(CT - 1)

        def rest(n, s):
            return 1 + CT - n if s == n - 1 else 1

        @block.sync
        def _(sp):
            with sp.Fori(0, E0 // 2) as j:
                for p in range(2):
                    e = 2 * j + p
                    sp.wait_ge(out_done, CT * (e + 1))
                    sp.dma_start(wg[p][:, :, :], d["w_gate"][ds(e, 1), :, :, :].rearrange("o p c f -> (o p) c f")).then_inc(weights_in[p], 16)
                    sp.dma_start(wu[p][:, :, :], d["w_up"][ds(e, 1), :, :, :].rearrange("o p c f -> (o p) c f")).then_inc(weights_in[p], 16)
                    for k, (f, m) in enumerate(FT0):
                        sp.dma_start(wd[p][0:m, k, :], d["w_down"][ds(e, 1), f:f + m, :].rearrange("o f d -> (o f) d")).then_inc(weights_in[p], 16)

        @block.gpsimd
        def _(pool):
            pool.sem_inc(tp_ready, 2 * CT)
            with pool.Fori(0, E0 // 2) as j:
                for p in range(2):
                    e = 2 * j + p

                    def body(n):
                        pool.wait_ge(tp_ready, CT * (e + 1))
                        pool.dma_start(xs[p][:, 0:n, :], d["slots"][ds(e * CAP, n * P), :].rearrange("(s p) d -> p s d", p=P)).then_inc(xs_in[p], 16)
                    by_load(pool, e, body)

        @block.scalar
        def _(act):
            def copy_rows(e, p):
                def body(n):
                    for s in range(n):
                        u = CT * e + s
                        act.wait_ge(tp_ready, 2 * CT + u + 1)
                        act.activation(xt[p][:, :, s * P:(s + 1) * P], tp[(CT * p + s) % 2][:, :].rearrange("p (c s) -> p c s", c=DC),
                                       ACT.Copy).then_inc(xt_ready, rest(n, s))
                by_load(act, e, body)

            def silus(e, p):
                def body(n):
                    for k, (f, m) in enumerate(FT0):
                        u = NF * e + k
                        act.wait_ge(gate_done, u + 1)
                        act.wait_ge(h_ready, u + 1)
                        q = (NF * p + k) % 2
                        act.activation(sg[q][0:m, 0:n * P], pg[q][0:m, 0:n * P], ACT.Silu).then_inc(silu_ready, 1)
                by_load(act, e, body)

            def store(e, p):
                def body(n):
                    act.wait_ge(eo_ready, 2 + CT * (e + 1))
                    act.dma_start(d["slots"][ds(e * CAP, n * P), :].rearrange("(s p) d -> p s d", p=P), eo[p][:, 0:n, :]).then_inc(stored[p], 16)
                by_load(act, e, body)

            copy_rows(0, 0)
            with act.Fori(0, E0 // 2 - 1) as j:
                for p in range(2):
                    silus(2 * j + p, p)
                    copy_rows(2 * j + p + 1, 1 - p)
                    store(2 * j + p, p)
            silus(E0 - 2, 0)
            copy_rows(E0 - 1, 1)
            store(E0 - 2, 0)
            silus(E0 - 1, 1)
            store(E0 - 1, 1)
            for p in range(2):
                act.wait_ge(stored[p], 16 * (E0 // 2))

        @block.vector
        def _(dve):
            dve.sem_inc(h_ready, 2)
            dve.sem_inc(eo_ready, 2)

            def hidden_and_out(j, p, first=False):
                e = 2 * j + p

                def body(n):
                    for k, (f, m) in enumerate(FT0):
                        u = NF * e + k
                        q = (NF * p + k) % 2
                        dve.wait_ge(up_done, u + 1)
                        dve.wait_ge(silu_ready, u + 1)
                        dve.tensor_tensor(h[p][0:m, k, 0:n * P], sg[q][0:m, 0:n * P], pu[q][0:m, 0:n * P], ALU.mult).then_inc(h_ready, 1)
                    if not first:
                        dve.wait_ge(stored[p], 16 * j)
                    for s in range(n):
                        dve.wait_ge(out_done, 2 * CT + CT * e + s + 1)
                        dve.tensor_copy(eo[p][:, s, :], po[(CT * p + s) % 2][:, :]).then_inc(eo_ready, rest(n, s))
                by_load(dve, e, body)

            for p in range(2):
                hidden_and_out(0, p, first=True)
            with dve.Fori(1, E0 // 2) as j:
                for p in range(2):
                    hidden_and_out(j, p)

        @block.tensor
        def _(pe):
            pe.sem_inc(out_done, 2 * CT)
            pe.sem_inc(xt_ready, 2)

            def transposes(j, e, p):
                def body(n):
                    pe.wait_ge(xs_in[p], 16 * (j + 1))
                    for s in range(n):
                        pe.wait_ge(xt_ready, CT * e + s + 1)
                        transposed_tile(pe, tp[(CT * p + s) % 2], xs[p][:, s, :], t).then_inc(tp_ready, rest(n, s))
                by_load(pe, e, body)

            def up(j, e, p):
                def body(n):
                    pe.wait_ge(weights_in[p], 16 * (2 + NF) * (j + 1))
                    pe.wait_ge(xt_ready, 2 + CT * (e + 1))
                    for k, (f, m) in enumerate(FT0):
                        u = NF * e + k
                        q = (NF * p + k) % 2
                        pe.wait_ge(h_ready, u + 1)
                        for c in range(DC):
                            mm = pe.matmul(pg[q][0:m, 0:n * P], wg[p][:, c, f:f + m], xt[p][:, c, 0:n * P], start=(c == 0), stop=(c == DC - 1))
                        mm.then_inc(gate_done, 1)
                        for c in range(DC):
                            mm = pe.matmul(pu[q][0:m, 0:n * P], wu[p][:, c, f:f + m], xt[p][:, c, 0:n * P], start=(c == 0), stop=(c == DC - 1))
                        mm.then_inc(up_done, 1)
                by_load(pe, e, body)

            def down(e, p):
                def body(n):
                    pe.wait_ge(h_ready, 2 + NF * (e + 1))
                    for s in range(n):
                        pe.wait_ge(eo_ready, CT * e + s + 1)
                        for k, (f, m) in enumerate(FT0):
                            mm = pe.matmul(po[(CT * p + s) % 2][:, :], h[p][0:m, k, s * P:(s + 1) * P], wd[p][0:m, k, :], start=(k == 0), stop=(k == NF - 1))
                        mm.then_inc(out_done, rest(n, s))
                by_load(pe, e, body)

            transposes(0, 0, 0)
            with pe.Fori(0, E0 // 2 - 1) as j:
                for p in range(2):
                    e = 2 * j + p
                    up(j, e, p)
                    transposes(j + p, e + 1, 1 - p)
                    down(e, p)
            j = E0 // 2 - 1
            up(j, E0 - 2, 0)
            transposes(j, E0 - 1, 1)
            down(E0 - 2, 0)
            up(j, E0 - 1, 1)
            down(E0 - 1, 1)


def combine(nc, t, d):
    with ExitStack() as ctx:
        ph = Phase(nc, ctx, "c_")
        addr_f = ph.sb("addr_f", [P, TT, 8])
        low = ph.sb("low", [P, TT, 8])
        frm = [ph.sb(f"frm{p}", [P, 8], U32) for p in range(2)]
        y = [ph.sb(f"y{p}", [P, K0, D]) for p in range(2)]
        addr_ready, staged, tiles_staged, y_used = ph.sems("addr_ready staged tiles_staged y_used")
        gathered = [ph.sem(f"gathered{p}") for p in range(2)]
        block = ctx.enter_context(nc.Block())

        @block.gpsimd
        def _(pool):
            pool.tensor_scalar(low[:, :, :], t.addr[:, :, :], 1.0, None, ALU.max).then_inc(addr_ready, 1)
            pool.wait_ge(addr_ready, 1)
            pool.tensor_scalar(addr_f[:, :, :], low[:, :, :], -1.0, None, ALU.add).then_inc(addr_ready, 1)
            pool.wait_ge(addr_ready, 2)
            with pool.Fori(0, TT // 2) as j:
                for p in range(2):
                    i = 2 * j + p
                    pool.wait_ge(y_used, K0 * (i + 1))
                    pool.tensor_copy(frm[p][:, :], row(addr_f, i)).then_inc(staged, 1)
                    pool.wait_ge(staged, i + 1)
                    pool.sem_inc(tiles_staged, 1)
                    for k in range(K0):
                        pool.indirect_dma_start(out=y[p][:, k, :], out_offset=None, in_=d["slots"],
                                                in_offset=bass.IndirectOffsetOnAxis(ap=frm[p][:, k:k + 1], axis=0),
                                                bounds_check=SLOTS - 1, oob_is_err=False).then_inc(gathered[p], 16)

        @block.vector
        def _(dve):
            dve.sem_inc(y_used, 2 * K0)
            with dve.Fori(0, TT // 2) as j:
                for p in range(2):
                    i = 2 * j + p
                    dve.wait_ge(gathered[p], 16 * K0 * (j + 1))
                    for k in range(K0):
                        xs = row(t.x, i)
                        w = t.weight[:, ds(i, 1), k:k + 1].rearrange("p o k -> p (o k)")
                        dve.scalar_tensor_tensor(out=xs, in0=y[p][:, k, :], scalar=w, in1=xs, op0=ALU.mult, op1=ALU.add).then_inc(y_used, 1)
                        dve.wait_ge(y_used, 2 * K0 + K0 * i + k + 1)


def moe0(nc, t, d):
    with ExitStack() as ctx:
        ph = Phase(nc, ctx, "m_")
        t.addr = ph.sb("addr", [P, TT, 8])
        t.weight = ph.sb("weight", [P, TT, K0])
        t.load = ph.sb("load", [P, E0], U32)
        with ExitStack() as inner:
            ph = Phase(nc, inner, "n_")
            t.xn = ph.sb("xn", [P, TT, D])
            t.xt = ph.sb("xt", [P, DC, T])
            route(nc, t, d)
            dispatch(nc, t, d)
        experts(nc, t, d)
        combine(nc, t, d)


def layer1_attention(nc, t, d):
    NU = ST * NH // 2
    NM = NH // 8
    NG = NH // 4
    NP = 3
    NR = 3 * NM * 4 // 2
    KT = 2 * ST
    SWAP = [i ^ (HD // 2) for i in range(32)]
    with ExitStack() as ctx:
        ph = Phase(nc, ctx, "q_")
        stats6 = ph.sb("stats6", [P, TT, 6])
        wq = ph.sb("wq", [P, DC, D])
        wk = ph.sb("wk", [P, DC, D])
        wv = ph.sb("wv", [P, DC, D])
        wo = ph.sb("wo", [P, NG, D])
        rope = ph.sb("rope", [P, 4, S])
        rep = ph.sb("rep", [P, 2, 2, 4, P], F32R)
        head_gate = ph.sb("head_gate", [P, NH // 2, 4])
        mask = ph.sb("mask", [P, ST, S])
        cxt = ph.sb("cxt", [P, DC, S])
        qs = ph.sb("qs", [P, NH // 2, S], F32R)
        ks = ph.sb("ks", [P, NH // 2, 2 * S], F32R)
        vv = ph.sb("vv", [P, KT, NH, HD])
        masked = ph.sb("masked", [P, 2, 2, S])
        xns = masked[:, :, :, :].rearrange("p a k s -> p a (k s)")
        top = ph.sb("top", [P, 4])
        ntop = [ph.sb(f"ntop{p}", [P, 4]) for p in range(2)]
        total = [ph.sb(f"total{p}", [P, 4]) for p in range(2)]
        share = [ph.sb(f"share{p}", [P, 4]) for p in range(2)]
        norm = [ph.sb(f"norm{p}", [P, 4]) for p in range(2)]
        prob = [ph.sb(f"prob{p}", [P, 2, 2 * S]) for p in range(NP)]
        probt, probt_at = [], []
        for p in range(2):
            probt_at.append(nc.sbuf_base)
            probt.append(ph.sb(f"probt{p}", [P, 4, KT, S]))
        turned, straight = ([x[:, k, :, :] for x in probt] for k in range(2))
        part_bytes = NM * S * 4
        high, low = ([nc.alloc_sbuf_tensor_at(f"q_{name}{p}", [P, NM, S], F32R, offset=probt_at[p] + k * part_bytes) for p in range(2)]
                     for name, k in (("high", 2), ("low", 3)))
        ots = ph.sb("ots", [P, NG, S])
        xt = ots[:, 0:DC, :]
        score = [ph.ps(f"score{p}", [P, 2, D]) for p in range(2)]
        tps = ph.ps("tps", [P, 2, D])
        ot = [ph.ps(f"ot{p}", [P, D]) for p in range(2)]
        ring = [tps[:, 0, :], tps[:, 1, :], ot[0][:, :], ot[1][:, :]]
        weights_in, ctx_in, mask_in, gates_ready, stats_ready, rstd_ready, xn_ready, xtp_ready, xt_ready = ph.sems(
            "weights_in ctx_in mask_in gates_ready stats_ready rstd_ready xn_ready xtp_ready xt_ready")
        q_done, k_done, ak_done, v_done, av_done, q_turned, k_turned, q_split, k_split, ak_high, ak_split, v_ready = ph.sems(
            "q_done k_done ak_done v_done av_done q_turned k_turned q_split k_split ak_high ak_split v_ready")
        rep_in, rep_ready, stack_done, stacked_act, stacked_dve = ph.sems("rep_in rep_ready stack_done stacked_act stacked_dve")
        score_ready, mask_used, top_ready, exp_ready, norm_ready, prob_ready, tps_ready, probt0_ready, probt1_ready, value_done = ph.sems(
            "score_ready mask_used top_ready exp_ready norm_ready prob_ready tps_ready probt0_ready probt1_ready value_done")
        ot_copied, out_ready, dve_step, pool_step, norm_seen, dve_seen = ph.sems("ot_copied out_ready dve_step pool_step norm_seen dve_seen")
        block = ctx.enter_context(nc.Block())

        def stack_tiles(c):
            kind, m, a = c // 8, c // 4 % 2 * 2, c % 4
            dst = (qs[:, :, :], ks[:, :, 0:S], ks[:, :, S:2 * S])[kind]
            return kind, m, a, dst[:, 4 * m + a:4 * m + a + 5:4, :]

        def unit(u):
            g, s, pr = u // 4, u // 2 % 2, u % 2
            return g, s, pr, 2 * g + pr

        @block.sync
        def _(sp):
            for w, n in ((wq, "wq"), (wk, "wk"), (wv, "wv")):
                sp.dma_start(w[:, :, :], d[n].rearrange("(c p) n -> p c n", p=P)).then_inc(weights_in, 16)
            sp.dma_start(wo[:, :, :], d["wo"]).then_inc(weights_in, 16)
            sp.dma_start(rope[:, :, :], d["rope"]).then_inc(weights_in, 16)
            sp.dma_start(probt[0][:, 0:2, :, :].rearrange("p a k s -> p (a k s)"), d["rep"]).then_inc(rep_in, 16)
            sp.dma_start(head_gate[:, :, :], d["head_gate"]).then_inc(weights_in, 16)

            def load(b):
                sp.dma_start(cxt[:, :, :], d["ctx_t"][ds(b, 1), :, :].rearrange("o (c p) s -> p (o c) s", p=P)).then_inc(ctx_in, 16)

            def load_mask(b):
                sp.dma_start(mask[:, :, :], d["mask"][ds(b, 1), :, :].rearrange("o (t p) k -> p (o t) k", p=P)).then_inc(mask_in, 16)

            load(0)
            load_mask(0)
            with sp.Fori(1, B) as b:
                sp.wait_ge(av_done, b)
                load(b)
                sp.wait_ge(mask_used, b)
                load_mask(b)

        @block.gpsimd
        def _(pool):
            pool.wait_ge(stats_ready, 1)
            row_rstd(pool, Serial(pool, pool_step, 0, 2), t)
            pool.sem_inc(rstd_ready, 1)
            with pool.Fori(0, B) as b:
                for u in range(NU):
                    pool.wait_ge(norm_ready, b * NU + u + 1)
                    pool.sem_inc(norm_seen, 1)
                    for k in range(4):
                        half = prob[u % NP][:, k % 2, (k // 2) * S:(k // 2 + 1) * S]
                        pool.tensor_scalar(half, half, norm[u % 2][:, k:k + 1], 1.0, ALU.mult, ALU.mult).then_inc(prob_ready, 1)

        @block.scalar
        def _(act):
            act.wait_ge(weights_in, 6 * 16)
            act.activation(head_gate[:, :, 2:4], head_gate[:, :, 2:4], ACT.Tanh).then_inc(gates_ready, 1)
            with act.Fori(0, B) as b:
                for s in range(ST):
                    act.wait_ge(xtp_ready, ST * b + s + 1)
                    act.activation(xt[:, :, s * P:(s + 1) * P], tps[:, s, :].rearrange("p (c s) -> p c s", c=DC), ACT.Copy).then_inc(xt_ready, 1)
                def stack(c):
                    act.wait_ge(stack_done, NR * b + c + 1)
                    act.activation(stack_tiles(c)[3], ring[c % 4].rearrange("p (t s) -> p t s", s=S), ACT.Copy).then_inc(stacked_act, 1)

                def values(k):
                    act.activation(vv[:, k, :, :], score[1 - k // ST][:, k % ST, :].rearrange("p (h d) -> p h d", d=HD), ACT.Copy).then_inc(v_ready, 1)

                for c in range(0, 8, 2):
                    stack(c)
                act.wait_ge(ak_done, b + 1)
                act.wait_ge(stack_done, NR * b + 8)
                act.activation(high[0][:, :, :], score[0][:, :, :].rearrange("p a (m s) -> p (a m) s", s=S), ACT.Copy).then_inc(ak_high, 1)
                act.wait_ge(v_done, b + 1)
                for k in range(ST):
                    values(k)
                for c in range(8, 16, 2):
                    stack(c)
                act.wait_ge(av_done, b + 1)
                for k in range(ST, KT):
                    values(k)
                for c in range(16, NR, 2):
                    stack(c)
                for i in range(NU + 4):
                    if i < NU:
                        act.wait_ge(top_ready, b * NU + i + 1)
                        if i >= NP:
                            act.wait_ge(tps_ready, b * NU + i - NP + 1)
                        for k in range(4):
                            src = masked[:, i % 2, k, :] if k < 2 else score[i % 2][:, k - 2, S:2 * S]
                            act.activation(prob[i % NP][:, k % 2, (k // 2) * S:(k // 2 + 1) * S], src, ACT.Exp,
                                           bias=ntop[i % 2][:, k:k + 1], accum_out=total[i % 2][:, k:k + 1]).then_inc(exp_ready, 1)
                    v = i - 2
                    if 0 <= v < NU:
                        act.wait_ge(tps_ready, b * NU + v + 1)
                        g, s, pr, pair = unit(v)
                        if g >= 2 and v % 4 == 0:
                            act.wait_ge(value_done, b * NG + g - 1)
                        act.activation(probt[g % 2][:, 2 * pr + 1, :, s * P:(s + 1) * P], tps[:, 1, :].rearrange("p (n q) -> p n q", q=P), ACT.Copy).then_inc(probt1_ready, 1)
                    v = i - 4
                    if v >= 0 and v % 4 == 3:
                        act.wait_ge(value_done, b * NG + v // 4 + 1)
                        act.activation(ots[:, v // 4, :], ot[v // 4 % 2][:, 0:S], ACT.Copy).then_inc(ot_copied, 1)

        @block.vector
        def _(dve):
            row_stats(dve, Serial(dve, dve_step, 0, ROW_STATS), t, stats6)
            dve.sem_inc(stats_ready, 1)
            dve.wait_ge(gates_ready, 1)
            step = Serial(dve, dve_step, ROW_STATS, 1)
            step(dve.memset(head_gate[:, :, 0:2], 1.0))
            dve.wait_ge(rep_in, 16)
            dve.tensor_copy(rep[:, :, :, :, :].rearrange("p a b c q -> p (a b c q)"), probt[0][:, 0:2, :, :].rearrange("p a k s -> p (a k s)")).then_inc(rep_ready, 1)
            dve.wait_ge(rep_ready, 1)
            dve.wait_ge(rstd_ready, 1)
            steps = 2 * 4 + 4 * NU
            with dve.Fori(0, B) as b:
                step = Serial(dve, dve_step, ROW_STATS + 1 + b * steps, steps)
                for s in range(ST):
                    dve.tensor_scalar(xns[:, s, :], row(t.x, ST * b + s), t.mv_at(ST * b + s, 0), t.rstd_at(ST * b + s),
                                      ALU.subtract, ALU.mult).then_inc(xn_ready, 1)
                for n, done, raw_read, split in ((0, q_done, q_turned, q_split), (1, k_done, k_turned, k_split)):
                    dve.wait_ge(done, b + 1)
                    raw = score[n][:, :, :].rearrange("p a (m s) -> p (a m) s", s=S)
                    cos = rope[:, 2 * n, :].unsqueeze(1).to_broadcast([P, NM, S])
                    sin = rope[:, 2 * n + 1, :].unsqueeze(1).to_broadcast([P, NM, S])
                    dve.sem_inc(dve_seen, 1)
                    step(dve.stream_shuffle(turned[n].rearrange("p m s -> p (m s)"), score[n][:, :, :].rearrange("p a f -> p (a f)"), SWAP))
                    dve.tensor_tensor(straight[n], raw, cos, ALU.mult).then_inc(raw_read, 1)
                    step(dve.tensor_tensor(turned[n], turned[n], sin, ALU.mult))
                    step(dve.tensor_tensor(straight[n], straight[n], turned[n], ALU.add))
                    step(dve.tensor_copy(high[n][:, :, :], straight[n]))
                    dve.tensor_tensor(low[n][:, :, :], straight[n], high[n][:, :, :].bitcast(F32), ALU.subtract).then_inc(split, 1)

                def stack(c):
                    dve.wait_ge(stack_done, NR * b + c + 1)
                    dve.tensor_copy(stack_tiles(c)[3], ring[c % 4].rearrange("p (t s) -> p t s", s=S)).then_inc(stacked_dve, 1)

                for c in range(1, 8, 2):
                    stack(c)
                dve.wait_ge(ak_high, b + 1)
                dve.tensor_tensor(low[0][:, :, :], score[0][:, :, :].rearrange("p a (m s) -> p (a m) s", s=S), high[0][:, :, :].bitcast(F32), ALU.subtract).then_inc(ak_split, 1)
                for c in range(9, NR, 2):
                    stack(c)
                dve.wait_ge(mask_in, 16 * (b + 1))
                step(dve.tensor_scalar(mask[:, :, :], mask[:, :, :], FMIN, None, ALU.max))
                for i in range(NU + 2):
                    if i < NU:
                        g, s, pr, pair = unit(i)
                        dve.wait_ge(score_ready, b * NU + i + 1)
                        if i >= 2:
                            dve.wait_ge(exp_ready, 4 * (b * NU + i - 1))
                        dve.sem_inc(dve_seen, 1)
                        for k in range(2):
                            ins = dve.tensor_tensor_reduce(out=masked[:, i % 2, k, :], in0=score[i % 2][:, k, 0:S], in1=mask[:, s, :], scale=1.0,
                                                           scalar=FMIN, op0=ALU.add, op1=ALU.max, accum_out=top[:, k:k + 1])
                            if i == NU - 1 and k == 1:
                                ins.then_inc(mask_used, 1)
                            else:
                                step.later(ins)
                        step.later(dve.reduce_max(top[:, 2:4], score[i % 2][:, :, S:2 * S], axis=AX.X))
                        step.all()
                        if i == NU - 1:
                            dve.wait_ge(mask_used, b + 1)
                        dve.tensor_scalar(ntop[i % 2][:, :], top[:, :], -1.0, None, ALU.mult).then_inc(top_ready, 1)
                        dve.wait_ge(top_ready, b * NU + i + 1)
                    v = i - 1
                    if 0 <= v < NU:
                        g, s, pr, pair = unit(v)
                        dve.wait_ge(exp_ready, 4 * (b * NU + v + 1))
                        step(dve.reciprocal(share[v % 2][:, :], total[v % 2][:, :]))
                        dve.tensor_tensor(norm[v % 2][:, :], share[v % 2][:, :], head_gate[:, pair, :], ALU.mult).then_inc(norm_ready, 1)
                    v = i - 2
                    if 0 <= v < NU:
                        dve.wait_ge(tps_ready, b * NU + v + 1)
                        g, s, pr, pair = unit(v)
                        if g >= 2 and v % 4 == 0:
                            dve.wait_ge(value_done, b * NG + g - 1)
                        dve.tensor_copy(probt[g % 2][:, 2 * pr, :, s * P:(s + 1) * P], tps[:, 0, :].rearrange("p (n q) -> p n q", q=P)).then_inc(probt0_ready, 1)
                for s in range(ST):
                    dve.wait_ge(out_ready, ST * b + s + 1)
                    xs = row(t.x, ST * b + s)
                    dve.scalar_tensor_tensor(out=xs, in0=tps[:, s, :], scalar=t.gates[:, 2:3], in1=xs, op0=ALU.mult, op1=ALU.add)
                step.close()

        @block.tensor
        def _(pe):
            pe.wait_ge(weights_in, 6 * 16)

            def heads_by_position(psum, w, x):
                for m in range(NM):
                    for c in range(DC):
                        mm = pe.matmul(psum[:, m // 2, (m % 2) * S:(m % 2 + 1) * S], w[:, c, m * P:(m + 1) * P], x[:, c, :], start=(c == 0), stop=(c == DC - 1))
                return mm

            def positions_by_head(psum, w, x):
                for s in range(ST):
                    for c in range(DC):
                        mm = pe.matmul(psum[:, s, :], x[:, c, s * P:(s + 1) * P], w[:, c, :], start=(c == 0), stop=(c == DC - 1))
                return mm

            with pe.Fori(0, B) as b:
                for s in range(ST):
                    pe.wait_ge(xn_ready, ST * b + s + 1)
                    transposed_tile(pe, tps[:, s, :], xns[:, s, :], t).then_inc(xtp_ready, 1)
                pe.wait_ge(xt_ready, ST * b + ST)
                heads_by_position(score[0], wq, xt).then_inc(q_done, 1)
                heads_by_position(score[1], wk, xt).then_inc(k_done, 1)
                def stack(kind):
                    for c in range(8 * kind, 8 * kind + 8):
                        if c >= 4:
                            pe.wait_ge((stacked_act, stacked_dve)[c % 2], NR // 2 * b + c // 2 - 1)
                        _, m, a, _ = stack_tiles(c)
                        n = kind % 2
                        pe.matmul(ring[c % 4], rep[:, min(kind, 1), 0, a, :], high[n][:, m:m + 2, :].rearrange("p m s -> p (m s)"), start=True, stop=False)
                        pe.matmul(ring[c % 4], rep[:, min(kind, 1), 1, a, :], low[n][:, m:m + 2, :].rearrange("p m s -> p (m s)"), start=False, stop=True).then_inc(stack_done, 1)

                pe.wait_ge(q_turned, b + 1)
                pe.wait_ge(ctx_in, 16 * (b + 1))
                heads_by_position(score[0], wk, cxt).then_inc(ak_done, 1)
                pe.wait_ge(q_split, b + 1)
                stack(0)
                pe.wait_ge(k_turned, b + 1)
                positions_by_head(score[1], wv, xt).then_inc(v_done, 1)
                pe.wait_ge(k_split, b + 1)
                stack(1)
                pe.wait_ge(ak_split, b + 1)
                positions_by_head(score[0], wv, cxt).then_inc(av_done, 1)
                stack(2)
                pe.wait_ge(stacked_act, NR // 2 * (b + 1))
                pe.wait_ge(stacked_dve, NR // 2 * (b + 1))
                pe.wait_ge(v_ready, KT * (b + 1))
                for i in range(NU + 3):
                    if i < NU:
                        g, s, pr, pair = unit(i)
                        if i >= 2:
                            pe.wait_ge(exp_ready, 4 * (b * NU + i - 1))
                        for k in range(2):
                            mm = pe.matmul(score[i % 2][:, k, :], qs[64 * k:64 * k + 64, pair, s * P:(s + 1) * P], ks[64 * k:64 * k + 64, pair, :], start=True, stop=True)
                        mm.then_inc(score_ready, 1)
                    v = i - 2
                    if 0 <= v < NU:
                        pe.wait_ge(prob_ready, 4 * (b * NU + v + 1))
                        if v >= 1:
                            pe.wait_ge(probt0_ready, b * NU + v)
                            pe.wait_ge(probt1_ready, b * NU + v)
                        for k in range(2):
                            mm = transposed_tile(pe, tps[:, k, :], prob[v % NP][:, k, :], t)
                        mm.then_inc(tps_ready, 1)
                    v = i - 3
                    if v >= 0 and v % 4 == 3:
                        g = v // 4
                        pe.wait_ge(probt0_ready, b * NU + v + 1)
                        pe.wait_ge(probt1_ready, b * NU + v + 1)
                        if g >= 2:
                            pe.wait_ge(ot_copied, b * NG + g - 1)
                        for n in range(KT):
                            for c in range(4):
                                mm = pe.matmul(ot[g % 2][32 * c:32 * c + HD, 0:S], vv[:, n, 4 * g + c, :], probt[g % 2][:, c, n, :], start=(n == 0), stop=(n == KT - 1))
                        mm.then_inc(value_done, 1)
                pe.wait_ge(ot_copied, NG * (b + 1))
                for s in range(ST):
                    for g in range(NG):
                        mm = pe.matmul(tps[:, s, :], ots[:, g, s * P:(s + 1) * P], wo[:, g, :], start=(g == 0), stop=(g == NG - 1))
                    mm.then_inc(out_ready, 1)


def moe1(nc, t, d):
    with ExitStack() as ctx:
        ph = Phase(nc, ctx, "v_")
        t.xt = ph.sb("xt", [P, DC, T])
        t.mix = ph.sb("mix", [P, TT, E1])
        route1(nc, t, d)
        experts1(nc, t, d)


def route1(nc, t, d):
    W = E1 + 8 - K1
    with ExitStack() as ctx:
        ph = Phase(nc, ctx, "w_")
        stats6 = ph.sb("stats6", [P, TT, 6])
        router_t = ph.sb("router_t", [P, DC, E1])
        router_b = ph.sb("router_b", [P, E1])
        down_b = ph.sb("down_b", [E1, D])
        xns = [ph.sb(f"xns{p}", [P, D]) for p in range(2)]
        xts = [ph.sb(f"xts{p}", [P, D]) for p in range(2)]
        logit = ph.sb("logit", [P, TT, W])
        taken = ph.sb("taken", [P, TT, W])
        top = ph.sb("top", [P, TT, 8])
        expd = ph.sb("expd", [P, TT, E1])
        total = ph.sb("total", [P, TT])
        mixt = ph.sb("mixt", [E1, T])
        tp = [ph.ps(f"tp{p}", [P, D]) for p in range(2)]
        lg = ph.ps("lg", [P, D])
        mt = ph.ps("mt", [E1, T])
        out = ph.ps("out", [P, D])
        weights_in, stats_ready, rstd_ready, xn_ready, tp_ready, xts_ready, xt_ready, logit_ready, logit_out = ph.sems(
            "weights_in stats_ready rstd_ready xn_ready tp_ready xts_ready xt_ready logit_ready logit_out")
        exp_asked, exp_ready, mix_ready, mt_ready, mixt_ready, bias_ready, x_added, dve_step, pool_step = ph.sems(
            "exp_asked exp_ready mix_ready mt_ready mixt_ready bias_ready x_added dve_step pool_step")
        block = ctx.enter_context(nc.Block())

        def over(x, n=E1):
            return x.unsqueeze(2).to_broadcast([P, TT, n])

        @block.sync
        def _(sp):
            sp.dma_start(router_t[:, :, :], d["router_t"].rearrange("(c p) e -> p c e", p=P)).then_inc(weights_in, 16)
            sp.dma_start(router_b[:, :], d["router_b"]).then_inc(weights_in, 16)
            sp.dma_start(down_b[:, :], d["down_b"]).then_inc(weights_in, 16)

        @block.gpsimd
        def _(pool):
            pool.sem_inc(xt_ready, 2)
            pool.wait_ge(stats_ready, 1)
            row_rstd(pool, Serial(pool, pool_step, 0, 2), t)
            pool.sem_inc(rstd_ready, 1)
            with pool.Fori(0, TT // 2) as j:
                for p in range(2):
                    i = 2 * j + p
                    pool.wait_ge(xts_ready, i + 1)
                    pool.tensor_copy(t.xt[:, :, ds(i * P, P)], xts[p][:, :].rearrange("p (c s) -> p c s", c=DC)).then_inc(xt_ready, 1)

        @block.scalar
        def _(act):
            with act.Fori(0, TT // 2) as j:
                for p in range(2):
                    i = 2 * j + p
                    act.wait_ge(tp_ready, 2 + i + 1)
                    act.wait_ge(xt_ready, i + 1)
                    act.wait_ge(logit_ready, i + 1)
                    act.activation(xts[p][:, :], tp[p][:, :], ACT.Copy).then_inc(xts_ready, 1)
                    act.wait_ge(logit_ready, 2 + i + 1)
                    act.activation(logit[:, ds(i, 1), 0:E1].rearrange("p o e -> p (o e)"), lg[:, 0:E1], ACT.Copy).then_inc(logit_out, 1)
            act.wait_ge(exp_asked, 1)
            act.activation(expd[:, :, :], expd[:, :, :], ACT.Exp).then_inc(exp_ready, 1)
            act.wait_ge(mt_ready, 1)
            act.activation(mixt[:, :], mt[:, :], ACT.Copy).then_inc(mixt_ready, 1)

        @block.vector
        def _(dve):
            row_stats(dve, Serial(dve, dve_step, 0, ROW_STATS), t, stats6)
            dve.sem_inc(stats_ready, 1)
            dve.wait_ge(rstd_ready, 1)
            with dve.Fori(0, TT // 2) as j:
                for p in range(2):
                    i = 2 * j + p
                    dve.wait_ge(tp_ready, i + 1)
                    dve.tensor_scalar(xns[p][:, :], row(t.x, i), t.mv_at(i, 0), t.rstd_at(i), ALU.subtract, ALU.mult).then_inc(xn_ready, 1)
            dve.wait_ge(logit_out, 1 + TT)
            dve.wait_ge(weights_in, 48)
            step = Serial(dve, dve_step, ROW_STATS, 2 * TT + 7)
            step(dve.tensor_tensor(logit[:, :, 0:E1], logit[:, :, 0:E1], router_b[:, :].unsqueeze(1).to_broadcast([P, TT, E1]), ALU.add))
            step(dve.memset(logit[:, :, E1:W], FMIN))
            for i in range(TT):
                step(dve.max(top[:, i, :], logit[:, i, :]))
            dve.tensor_tensor(expd[:, :, :], logit[:, :, 0:E1], over(top[:, :, 0]), ALU.subtract).then_inc(exp_asked, 1)
            step(dve.memset(top[:, :, K1:8], FMIN))
            for i in range(TT):
                step(dve.match_replace(taken[:, i, :], top[:, i, :], logit[:, i, :], MARK))
            step(dve.tensor_scalar(taken[:, :, :], taken[:, :, :], MARK, None, ALU.is_equal))
            dve.wait_ge(exp_ready, 1)
            step(dve.tensor_tensor(expd[:, :, :], expd[:, :, :], taken[:, :, 0:E1], ALU.mult))
            step(dve.reduce_sum(total[:, :], expd[:, :, :], axis=AX.X))
            step(dve.reciprocal(total[:, :], total[:, :]))
            dve.tensor_tensor(t.mix[:, :, :], expd[:, :, :], over(total[:, :]), ALU.mult).then_inc(mix_ready, 1)
            step.close()
            for i in range(TT):
                dve.wait_ge(bias_ready, i + 1)
                dve.scalar_tensor_tensor(out=t.x[:, i, :], in0=out[:, :], scalar=t.gates[:, 3:4], in1=t.x[:, i, :],
                                         op0=ALU.mult, op1=ALU.add).then_inc(x_added, 1)
            dve.tensor_scalar(t.mix[:, :, :], t.mix[:, :, :], t.gates[:, 3:4], None, ALU.mult)

        @block.tensor
        def _(pe):
            pe.sem_inc(tp_ready, 2)
            pe.sem_inc(logit_ready, 2)
            pe.sem_inc(logit_out, 1)
            pe.wait_ge(weights_in, 48)
            with pe.Fori(0, TT // 2) as j:
                for p in range(2):
                    i = 2 * j + p
                    pe.wait_ge(xn_ready, i + 1)
                    transposed_tile(pe, tp[p], xns[p], t).then_inc(tp_ready, 1)
                    pe.wait_ge(xts_ready, i + 1)
                    pe.wait_ge(logit_out, i + 1)
                    for c in range(DC):
                        mm = pe.matmul(lg[:, 0:E1], xts[p][:, c * P:(c + 1) * P], router_t[:, c, :], start=(c == 0), stop=(c == DC - 1))
                    mm.then_inc(logit_ready, 1)
            pe.wait_ge(mix_ready, 1)
            for i in range(TT):
                mm = pe.transpose(mt[:, i * P:(i + 1) * P], t.mix[:, i, :], t.ident[:, :])
            mm.then_inc(mt_ready, 1)
            pe.wait_ge(mixt_ready, 1)
            for i in range(TT):
                if i:
                    pe.wait_ge(x_added, i)
                pe.matmul(out[:, :], mixt[:, i * P:(i + 1) * P], down_b[:, :], start=True, stop=True).then_inc(bias_ready, 1)


def experts1(nc, t, d):
    NN = T // NTOK
    NS = NTOK // P
    NF = I1 // P
    NB = 2 * NN
    with ExitStack() as ctx:
        ph = Phase(nc, ctx, "x_")
        wgu = [ph.sb(f"wgu{p}", [P, DC, 2, I1]) for p in range(2)]
        wd = [ph.sb(f"wd{p}", [P, NF, D]) for p in range(2)]
        bgu = ph.sb("bgu", [P, E1, 2 * NF])
        gate = [ph.sb(f"gate{p}", [P, NTOK]) for p in range(2)]
        sig = [ph.sb(f"sig{p}", [P, NTOK]) for p in range(2)]
        up0 = [ph.sb(f"up0{p}", [P, NTOK]) for p in range(2)]
        up1 = [ph.sb(f"up1{p}", [P, NTOK]) for p in range(2)]
        h = [ph.sb(f"h{p}", [P, NF, NTOK]) for p in range(2)]
        pg = [ph.ps(f"pg{p}", [P, NTOK]) for p in range(2)]
        pu = [ph.ps(f"pu{p}", [P, NTOK]) for p in range(2)]
        po = [ph.ps(f"po{p}", [P, D]) for p in range(2)]
        weights_in = [ph.sem(f"weights_in{p}") for p in range(2)]
        bias_in, gate_done, up_done, gate_ready, up0_ready, sig_ready, up1_ready, glu_ready, h_ready, out_done, x_added, up_seen = ph.sems(
            "bias_in gate_done up_done gate_ready up0_ready sig_ready up1_ready glu_ready h_ready out_done x_added up_seen")
        block = ctx.enter_context(nc.Block())

        @block.sync
        def _(sp):
            sp.dma_start(bgu[:, :, :], d["gate_up_b"]).then_inc(bias_in, 16)

            def load(e, p):
                sp.dma_start(wgu[p][:, :, :, :], d["gate_up"][ds(e, 1), :, :, :, :].rearrange("o p c g f -> (o p) c g f")).then_inc(weights_in[p], 16)
                sp.dma_start(wd[p][:, :, :], d["down"][ds(e, 1), :, :].rearrange("o (k p) d -> p (o k) d", p=P)).then_inc(weights_in[p], 16)

            for p in range(2):
                load(p, p)
            with sp.Fori(1, E1 // 2) as j:
                for p in range(2):
                    sp.wait_ge(out_done, NS * (NB * (j - 1) + NN * (p + 1)))
                    load(2 * j + p, p)

        @block.scalar
        def _(act):
            act.sem_inc(glu_ready, 2)
            with act.Fori(0, E1 // 2) as j:
                for v in range(NB):
                    for k in range(NF):
                        n = NF * v + k
                        act.wait_ge(gate_ready, NF * NB * j + n + 1)
                        act.wait_ge(glu_ready, NF * NB * j + n + 1)
                        act.activation(sig[k % 2][:, :], gate[k % 2][:, :], ACT.Sigmoid, scale=ALPHA).then_inc(sig_ready, 1)

        @block.gpsimd
        def _(pool):
            pool.sem_inc(h_ready, 2)
            with pool.Fori(0, E1 // 2) as j:
                for v in range(NB):
                    for k in range(NF):
                        n = NF * v + k
                        pool.wait_ge(up0_ready, NF * NB * j + n + 1)
                        pool.wait_ge(h_ready, NF * NB * j + n + 1)
                        pool.sem_inc(up_seen, 1)
                        pool.tensor_scalar(up1[k % 2][:, :], up0[k % 2][:, :], -LIMIT, 1.0, ALU.max, ALU.add).then_inc(up1_ready, 1)

        @block.vector
        def _(dve):
            dve.sem_inc(x_added, 2)
            dve.wait_ge(bias_in, 16)
            with dve.Fori(0, E1 // 2) as j:
                def clamp(v, k):
                    n = NF * NB * j + NF * v + k
                    e = 2 * j + v // NN
                    for psum, dst, half, done, ready in ((pg, gate, 0, gate_done, gate_ready), (pu, up0, 1, up_done, up0_ready)):
                        bias = bgu[:, ds(e, 1), half * NF + k:half * NF + k + 1].rearrange("p o k -> p (o k)")
                        dve.wait_ge(done, n + 1)
                        dve.tensor_scalar(dst[k % 2][:, :], psum[k % 2][:, :], bias, LIMIT, ALU.add, ALU.min).then_inc(ready, 1)

                def glu(v, k):
                    n = NF * NB * j + NF * v + k
                    dve.wait_ge(sig_ready, n + 1)
                    dve.tensor_tensor(gate[k % 2][:, :], gate[k % 2][:, :], sig[k % 2][:, :], ALU.mult).then_inc(glu_ready, 1)
                    dve.wait_ge(glu_ready, 2 + n + 1)
                    dve.wait_ge(up1_ready, n + 1)
                    dve.tensor_tensor(h[v % 2][:, k, :], gate[k % 2][:, :], up1[k % 2][:, :], ALU.mult).then_inc(h_ready, 1)
                    dve.wait_ge(h_ready, 2 + n + 1)

                def add(v):
                    e = 2 * j + v // NN
                    for s in range(NS):
                        i = NS * (v % NN) + s
                        dve.wait_ge(out_done, NS * NB * j + NS * v + s + 1)
                        mix = t.mix[:, i, ds(e, 1)]
                        dve.scalar_tensor_tensor(out=t.x[:, i, :], in0=po[s % 2][:, :], scalar=mix, in1=t.x[:, i, :],
                                                 op0=ALU.mult, op1=ALU.add).then_inc(x_added, 1)

                for v in range(NB):
                    for k in range(NF):
                        clamp(v, k)
                        if k:
                            glu(v, k - 1)
                    glu(v, NF - 1)
                    if v:
                        add(v - 1)
                add(NB - 1)

        @block.tensor
        def _(pe):
            with pe.Fori(0, E1 // 2) as j:
                def up(v):
                    p, x0 = v // NN, (v % NN) * NTOK
                    if v % NN == 0:
                        pe.wait_ge(weights_in[p], 32 * (j + 1))
                    for k in range(NF):
                        pe.wait_ge(h_ready, NF * NB * j + NF * v + k + 1)
                        for half, psum, done in ((0, pg, gate_done), (1, pu, up_done)):
                            for c in range(DC):
                                mm = pe.matmul(psum[k % 2][:, :], wgu[p][:, c, half, k * P:(k + 1) * P], t.xt[:, c, x0:x0 + NTOK], start=(c == 0), stop=(c == DC - 1))
                            mm.then_inc(done, 1)

                def down(v):
                    p = v // NN
                    pe.wait_ge(h_ready, 2 + NF * NB * j + NF * (v + 1))
                    for s in range(NS):
                        pe.wait_ge(x_added, NS * NB * j + NS * v + s + 1)
                        for k in range(NF):
                            mm = pe.matmul(po[s % 2][:, :], h[v % 2][:, k, s * P:(s + 1) * P], wd[p][:, k, :], start=(k == 0), stop=(k == NF - 1))
                        mm.then_inc(out_done, 1)

                up(0)
                for v in range(NB):
                    if v + 1 < NB:
                        up(v + 1)
                    down(v)


def store_x(nc, t, d):
    with ExitStack() as ctx:
        ph = Phase(nc, ctx, "o_")
        stored, = ph.sems("stored")
        block = ctx.enter_context(nc.Block())

        @block.sync
        def _(sp):
            sp.dma_start(d["out"].rearrange("b (t p) d -> p (b t) d", p=P), t.x[:, :, :]).then_inc(stored, 16)
            sp.wait_ge(stored, 16)


def build(nc, d, stop=9):
    d["slots"] = nc.dram_tensor("expert_slots", (SLOTS, D), F32, kind="Internal").ap()
    with ExitStack() as ctx:
        ph = Phase(nc, ctx, "g_")
        t = Shared()
        t.x = ph.sb("x", [P, TT, D])
        t.mv = ph.sb("mv", [P, TT, 2])
        t.vareps = ph.sb("vareps", [P, TT])
        t.rstd = ph.sb("rstd", [P, TT])
        t.minus_half = ph.sb("minus_half", [P, TT])
        t.gates = ph.sb("gates", [P, 4])
        t.ident = ph.sb("ident", [P, P])
        t.before = ph.sb("before", [P, P])
        t.ones = ph.sb("ones", [P, P])
        t.mv_at = lambda i, k: t.mv[:, ds(i, 1), k:k + 1].rearrange("p o d -> p (o d)")
        t.rstd_at = lambda i: t.rstd[:, ds(i, 1)]
        load_constants(nc, t, d)
        if stop >= 1:
            layer0_attention(nc, t, d)
        if stop >= 2:
            moe0(nc, t, d)
        if stop >= 3:
            layer1_attention(nc, t, d)
        if stop >= 4:
            moe1(nc, t, d)
        store_x(nc, t, d)


_STOP = 4


def kernel(**inputs):
    import numpy as np
    import concourse.bacc as _bacc
    from concourse.bass_utils import run_bass_kernel_spmd as _run

    a = {k: np.ascontiguousarray(v) for k, v in inputs.items()}

    def chunked(w):
        e, f, dm = w.shape
        return np.ascontiguousarray(w.reshape(e, f, dm // 128, 128).transpose(0, 3, 2, 1))

    wo = np.zeros((128, NH // 4, D), np.float32)
    for h in range(NH):
        wo[32 * (h % 4):32 * (h % 4) + HD, h // 4, :] = a["L1_xattn_Wo"][HD * h:HD * (h + 1), :]
    inv = 1.0 / 10000.0 ** (np.arange(0, HD, 2, dtype=np.float32) / HD)
    angle = np.outer(np.arange(S, dtype=np.float32), inv)
    angle = np.concatenate([angle, angle], -1)
    sign = np.where(np.arange(HD) < HD // 2, -1.0, 1.0).astype(np.float32)
    cos, sin = (np.tile(x.astype(np.float32).T, (128 // HD, 1)) for x in (np.cos(angle), np.sin(angle) * sign))
    rope = np.stack([cos * np.float32(HD ** -0.5), sin * np.float32(HD ** -0.5), cos, sin], 1)
    rep = np.zeros((128, 2, 2, 4, 128), np.float32)
    for a1 in range(4):
        for a0 in range(2):
            for j in range(4):
                for r in range(HD):
                    rep[HD * (2 * a1 + a0) + r, 0, j % 2, a1, 64 * a0 + HD * j + r] = 1
                    rep[HD * (2 * a1 + a0) + r, 1, j // 2, a1, 64 * a0 + HD * j + r] = 1
    head_gate = np.zeros((128, NH // 2, 4), np.float32)
    head_gate[:, :, 2:4] = a["L1_xattn_gate"].reshape(NH // 2, 2)

    arrays = {
        "x": a["x"],
        "ctx": a["ctx_2048"],
        "ctx_t": np.ascontiguousarray(a["ctx_2048"].transpose(0, 2, 1)),
        "gates": np.ascontiguousarray(np.broadcast_to(np.concatenate([a["g_xattn"][0:1], a["g_ffn"][0:1], a["g_xattn"][1:2], a["g_ffn"][1:2]]), (128, 4))),
        "ident": np.eye(128, dtype=np.float32),
        "gate_wt": np.ascontiguousarray(a["L0_ffn_gate_w"].T),
        "slot_base": np.broadcast_to(np.arange(64, dtype=np.float32) * CAP + 1, (128, 64)).copy(),
        "sh_gate": np.ascontiguousarray(a["L0_ffn_sh_gate"].T),
        "sh_up": np.ascontiguousarray(a["L0_ffn_sh_up"].T),
        "sh_down": np.ascontiguousarray(a["L0_ffn_sh_down"].T),
        "w_gate": chunked(a["L0_ffn_w_gate"]),
        "w_up": chunked(a["L0_ffn_w_up"]),
        "w_down": np.ascontiguousarray(a["L0_ffn_w_down"].transpose(0, 2, 1)),
        "mask": a["mask_Bx1xSxS_fk0"].reshape(B, S, S),
        "wq": a["L1_xattn_Wq"], "wk": a["L1_xattn_Wk"], "wv": a["L1_xattn_Wv"],
        "wo": wo, "rope": rope, "rep": rep.reshape(128, -1), "head_gate": head_gate,
        "router_t": np.ascontiguousarray(a["L1_ffn_router_weight"].T),
        "router_b": np.broadcast_to(a["L1_ffn_router_bias"], (128, E1)).copy(),
        "gate_up": np.ascontiguousarray(a["L1_ffn_gate_up_proj"].reshape(E1, DC, 128, I1, 2).transpose(0, 2, 1, 4, 3)),
        "gate_up_b": np.ascontiguousarray(a["L1_ffn_gate_up_proj_bias"].reshape(E1, I1 // 128, 128, 2).transpose(2, 0, 3, 1)).reshape(128, E1, 2 * I1 // 128),
        "down": a["L1_ffn_down_proj"],
        "down_b": a["L1_ffn_down_proj_bias"],
        "before": np.triu(np.ones((128, 128), np.float32), 1),
    }
    nc = _bacc.Bacc("TRN2", target_bir_lowering=False, num_devices=1)
    d = {n: nc.dram_tensor("in_" + n, v.shape, mybir.dt.from_np(v.dtype), kind="ExternalInput").ap() for n, v in arrays.items()}
    d["out"] = nc.dram_tensor("out_0", a["x"].shape, F32, kind="ExternalOutput").ap()
    build(nc, d, _STOP)
    r = _run(nc, [{"in_" + n: v for n, v in arrays.items()}], core_ids=[0])
    return r.results[0]["out_0"]
```

```python
import concourse.bass as bass
from concourse import mybir
from contextlib import ExitStack

F32 = mybir.dt.float32
U32 = mybir.dt.uint32
F32R = mybir.dt.float32r
ALU = mybir.AluOpType
ACT = mybir.ActivationFunctionType
AX = mybir.AxisListType
ds = bass.ds

P = 128
B, S, D = 8, 256, 512
T = B * S
TT = T // P
ST = S // P
DC = D // P
EPS = 1e-5

E0, K0, F0 = 64, 6, 352
CAP = 2 * ((T * K0 + E0 - 1) // E0)
CT = CAP // P
SLOTS = E0 * CAP
ZROWS = 4
ZN = SLOTS // (P * ZROWS)
ZA = 2 * B
FT0 = [(f, min(P, F0 - f)) for f in range(0, F0, P)]
FS = 704
FTS = [(0, P), (P, P), (2 * P, P), (3 * P, P), (4 * P, 96), (4 * P + 96, 96)]
NTOK = 512

NH, HD = 32, 16
E1, I1, K1 = 8, 512, 2
JT = 3
JC = JT * P
NJ = 2 * (((T * K1 - E1) // JC + E1 + 1) // 2)
FJ = (T * K1 // JC) - 1
MJ = (T + JC - 1) // JC
LIMIT, ALPHA = 7.0, 1.702
FMIN = -3.4028234663852886e38
MARK = 3.0e38


class Serial:

    def __init__(self, eng, sem, base, steps):
        self.eng, self.sem, self.base, self.steps, self.n = eng, sem, base, steps, 0

    def __call__(self, ins):
        self.n += 1
        ins.then_inc(self.sem, 1)
        self.eng.wait_ge(self.sem, self.base + self.n)

    def later(self, ins):
        self.n += 1
        ins.then_inc(self.sem, 1)

    def all(self):
        self.eng.wait_ge(self.sem, self.base + self.n)

    def close(self):
        assert self.n == self.steps, self.n


class Phase:

    def __init__(self, nc, ctx, prefix):
        self.nc, self.ctx, self.prefix, self.held = nc, ctx, prefix, []
        ctx.callback(self.clear)

    def sb(self, name, shape, dt=F32):
        return self.ctx.enter_context(self.nc.sbuf_tensor(self.prefix + name, shape, dt))

    def ps(self, name, shape):
        return self.ctx.enter_context(self.nc.psum_tensor(self.prefix + name, shape, F32))

    def sem(self, name):
        sem = self.nc.alloc_semaphore(name=self.prefix + name)
        self.held.append(sem)
        return sem

    def sems(self, names):
        return [self.sem(n) for n in names.split()]

    def clear(self):
        if not self.held:
            return
        self.nc.clear_and_free_semaphores(self.held)
        self.nc.all_engine_barrier()


def row(x, i):
    return x[:, ds(i, 1), :].rearrange("p o d -> p (o d)")


def row_stats(dve, step, t, stats6):
    for i in range(TT):
        step(dve.bn_stats(stats6[:, i, :], t.x[:, i, :]))
    for i in range(TT):
        step(dve.bn_aggr(t.mv[:, i, :], stats6[:, i, :]))


ROW_STATS = 2 * TT


def row_rstd(pool, step, t):
    step(pool.tensor_scalar(t.vareps[:, :], t.mv[:, :, 1], EPS, None, ALU.add))
    step(pool.tensor_tensor(t.rstd[:, :], t.vareps[:, :], t.minus_half[:, :], ALU.pow))


class Shared:
    pass


def load_constants(nc, t, d):
    with ExitStack() as ctx:
        ph = Phase(nc, ctx, "i_")
        raw = ph.sb("raw", [P, 4])
        const_in, = ph.sems("const_in")
        block = ctx.enter_context(nc.Block())

        @block.sync
        def _(sp):
            sp.dma_start(t.ident[:, :], d["ident"]).then_inc(const_in, 16)
            sp.dma_start(t.before[:, :], d["before"]).then_inc(const_in, 16)
            sp.dma_start(raw[:, :], d["gates"]).then_inc(const_in, 16)
            sp.dma_start(t.x[:, :, :], d["x"].rearrange("b (t p) d -> p (b t) d", p=P)).then_inc(const_in, 16)
            sp.wait_ge(const_in, 64)

        @block.vector
        def _(dve):
            dve.memset(t.ones[:, :], 1.0)
            dve.memset(t.minus_half[:, :], -0.5)

        @block.scalar
        def _(act):
            act.wait_ge(const_in, 64)
            act.activation(t.gates[:, :], raw[:, :], ACT.Tanh)


def zero_slots(eng, t, d, n):
    slots = d["slots"].rearrange("(n p r) d -> n p (r d)", p=P, r=ZROWS)
    eng.dma_start(slots[ds(n, 1), :, :].rearrange("o p f -> (o p) f"), t.zero[:, :]).then_inc(t.zeroed, 16)


def layer0_attention(nc, t, d):
    scale = D ** -0.5
    with ExitStack() as ctx:
        ph = Phase(nc, ctx, "a_")
        cn = [ph.sb(f"cn{p}", [P, ST, D]) for p in range(2)]
        ct = [ph.sb(f"ct{p}", [P, DC, S]) for p in range(2)]
        cts = [ph.sb(f"cts{p}", [P, DC, S]) for p in range(2)]
        q = [ph.sb(f"q{p}", [P, ST, D]) for p in range(2)]
        prob = [ph.sb(f"prob{p}", [P, DC, D]) for p in range(2)]
        stats6 = ph.sb("stats6", [P, TT, 6])
        nmax = ph.sb("nmax", [P, DC])
        nb = [ph.sb(f"nb{p}", [P, DC]) for p in range(2)]
        ssum = [ph.sb(f"ssum{p}", [P, DC]) for p in range(2)]
        rsum = ph.sb("rsum", [P, DC])
        score = [ph.ps(f"score{e}", [P, D]) for e in range(DC)]
        out = [ph.ps(f"out{s}", [P, D]) for s in range(ST)]
        ctx_in = [ph.sem(f"ctx_in{p}") for p in range(2)]
        stats_ready, rstd_ready, q_ready, score_ready, bias_ready, prob_ready = ph.sems(
            "stats_ready rstd_ready q_ready score_ready bias_ready prob_ready")
        ctx_scaled, out_ready, x_added, batch_done, dve_step, pool_step, zero_ready = ph.sems(
            "ctx_scaled out_ready x_added batch_done dve_step pool_step zero_ready")
        block = ctx.enter_context(nc.Block())

        @block.sync
        def _(sp):
            with sp.Fori(0, B // 2) as j:
                for p in range(2):
                    b = 2 * j + p
                    sp.wait_ge(batch_done, b + 1)
                    sp.dma_start(cn[p][:, :, :], d["ctx"][ds(b, 1), :, :].rearrange("o (t p) d -> p (o t) d", p=P)).then_inc(ctx_in[p], 16)
                    sp.dma_start(ct[p][:, :, :], d["ctx_t"][ds(b, 1), :, :].rearrange("o (c p) s -> p (o c) s", p=P)).then_inc(ctx_in[p], 16)

        @block.gpsimd
        def _(pool):
            pool.sem_inc(batch_done, 2)
            pool.memset(t.zero[:, :], 0.0).then_inc(zero_ready, 1)
            pool.wait_ge(stats_ready, 1)
            row_rstd(pool, Serial(pool, pool_step, 0, 2), t)
            pool.sem_inc(rstd_ready, 1)

        @block.vector
        def _(dve):
            row_stats(dve, Serial(dve, dve_step, 0, ROW_STATS), t, stats6)
            dve.sem_inc(stats_ready, 1)
            dve.wait_ge(rstd_ready, 1)
            steps = 2 * DC
            with dve.Fori(0, B // 2) as j:
                for p in range(2):
                    b = 2 * j + p
                    step = Serial(dve, dve_step, ROW_STATS + b * steps, steps)
                    dve.wait_ge(batch_done, b + 1)
                    for s in range(ST):
                        dve.tensor_scalar(q[p][:, s, :], row(t.x, ST * b + s), t.mv_at(ST * b + s, 0), t.rstd_at(ST * b + s),
                                          ALU.subtract, ALU.mult).then_inc(q_ready, 1)
                    dve.wait_ge(ctx_in[p], 32 * (j + 1))
                    for e in range(DC):
                        dve.wait_ge(score_ready, DC * b + e + 1)
                        step(dve.reduce_max(nmax[:, e:e + 1], score[e][:, :], axis=AX.X))
                        dve.tensor_scalar(nb[p][:, e:e + 1], nmax[:, e:e + 1], -scale, None, ALU.mult).then_inc(bias_ready, 1)
                    for e in range(DC):
                        dve.wait_ge(prob_ready, DC * b + e + 1)
                        step(dve.reciprocal(rsum[:, e:e + 1], ssum[p][:, e:e + 1]))
                        dve.tensor_scalar(cts[p][:, e, :], ct[p][:, e, :], rsum[:, e:e + 1], None, ALU.mult).then_inc(ctx_scaled, 1)
                    for s in range(ST):
                        dve.wait_ge(out_ready, ST * b + s + 1)
                        xs = row(t.x, ST * b + s)
                        dve.scalar_tensor_tensor(out=xs, in0=out[s][:, :], scalar=t.gates[:, 0:1], in1=xs,
                                                 op0=ALU.mult, op1=ALU.add).then_inc(x_added, 1)
                    dve.sem_inc(batch_done, 1)
                    step.close()

        @block.scalar
        def _(act):
            act.wait_ge(zero_ready, 1)
            with act.Fori(0, B // 2) as j:
                for p in range(2):
                    b = 2 * j + p
                    act.wait_ge(ctx_in[p], 32 * (j + 1))
                    for k in range(ZA // B):
                        zero_slots(act, t, d, ZA // B * b + k)
                    act.wait_ge(batch_done, b + 1)
                    for e in range(DC):
                        act.wait_ge(bias_ready, DC * b + e + 1)
                        act.activation(prob[p][:, e, :], score[e][:, :], ACT.Exp, bias=nb[p][:, e:e + 1], scale=scale,
                                       accum_out=ssum[p][:, e:e + 1]).then_inc(prob_ready, 1)

        @block.tensor
        def _(pe):
            pe.sem_inc(x_added, ST)
            with pe.Fori(0, B // 2) as j:
                for p in range(2):
                    b = 2 * j + p
                    pe.wait_ge(ctx_in[p], 32 * (j + 1))
                    pe.wait_ge(q_ready, ST * b + ST)
                    for e in range(DC):
                        for s in range(ST):
                            mm = pe.matmul(score[e][:, :], cn[p][:, s, e * P:(e + 1) * P], q[p][:, s, :], start=(s == 0), stop=(s == ST - 1))
                        mm.then_inc(score_ready, 1)
                    for s in range(ST):
                        pe.wait_ge(x_added, ST * b + s + 1)
                        for e in range(DC):
                            if s == 0:
                                pe.wait_ge(ctx_scaled, DC * b + e + 1)
                            mm = pe.matmul(out[s][:, :], cts[p][:, e, s * P:(s + 1) * P], prob[p][:, e, :], start=(e == 0), stop=(e == DC - 1))
                        mm.then_inc(out_ready, 1)


def transposed_tile(pe, psum, src, t):
    for c in range(DC):
        mm = pe.transpose(psum[:, c * P:(c + 1) * P], src[:, c * P:(c + 1) * P], t.ident[:, :])
    return mm


def scatter_rows(pool, t, d, choices, addr_f, rows, to, staged, tiles_staged, scattered):
    def scatter(j, p):
        i = 2 * j + p
        pool.tensor_copy(rows[p][:, :], row(t.xn, i)).then_inc(staged, 1)
        pool.tensor_copy(to[p][:, :], row(addr_f, i)).then_inc(staged, 1)
        pool.wait_ge(staged, 2 * i + 2)
        pool.sem_inc(tiles_staged, 1)
        for k in range(choices):
            pool.indirect_dma_start(out=d["slots"], out_offset=bass.IndirectOffsetOnAxis(ap=to[p][:, k:k + 1], axis=0),
                                    in_=rows[p][:, :], in_offset=None, bounds_check=SLOTS - 1, oob_is_err=False).then_inc(scattered[p], 16)

    for p in range(2):
        scatter(0, p)
    with pool.Fori(1, TT // 2) as j:
        for p in range(2):
            pool.wait_ge(scattered[p], 16 * choices * j)
            scatter(j, p)
    for p in range(2):
        pool.wait_ge(scattered[p], 16 * choices * (TT // 2))


def route_and_share(nc, t, d):
    W = E0 + 2
    NF = len(FTS)
    NS = NTOK // P
    with ExitStack() as ctx:
        ph = Phase(nc, ctx, "r_")
        t.xn = ph.sb("xn", [P, TT, D])
        t.xt = ph.sb("xt", [P, DC, T])
        stats6 = ph.sb("stats6", [P, TT, 6])
        gate_wt = ph.sb("gate_wt", [P, DC, E0])
        slot_base = ph.sb("slot_base", [P, E0])
        xns = [ph.sb(f"xns{p}", [P, D]) for p in range(2)]
        xts = [ph.sb(f"xts{p}", [P, D]) for p in range(2)]
        logit = ph.sb("logit", [P, TT, E0])
        score = ph.sb("score", [P, TT, W])
        taken = ph.sb("taken", [P, TT, W])
        chosen = ph.sb("chosen", [P, TT, E0])
        chosen_before = ph.sb("chosen_before", [P, TT + 1, E0])
        wsel = ph.sb("wsel", [P, TT, E0])
        place = ph.sb("place", [P, TT, E0])
        top = ph.sb("top", [P, TT, 8])
        small = ph.sb("small", [P, TT])
        big = ph.sb("big", [P, TT, 8])
        addr_f = ph.sb("addr_f", [P, TT, 8])
        rows = xns
        to = [ph.sb(f"to{p}", [P, 8], U32) for p in range(2)]
        wg = ph.sb("wg", [P, DC, FS])
        wu = ph.sb("wu", [P, DC, FS])
        wd = ph.sb("wd", [P, NF, D])
        sg = [ph.sb(f"sg{p}", [P, NTOK]) for p in range(2)]
        h = ph.sb("h", [P, NF, NTOK])
        pg = [ph.ps(f"pg{p}", [P, NTOK]) for p in range(2)]
        pu = [ph.ps(f"pu{p}", [P, NTOK]) for p in range(2)]
        po = [ph.ps(f"po{p}", [P, D]) for p in range(2)]
        count = ph.ps("count", [P, TT, E0])
        tp, lg = pg, pu
        load = count[:, 0, :]
        router_in, weights_in, stats_ready, rstd_ready, xn_ready, xn_copied, tp_ready, xts_ready, xt_ready, logit_ready, logit_out = ph.sems(
            "router_in weights_in stats_ready rstd_ready xn_ready xn_copied tp_ready xts_ready xt_ready logit_ready logit_out")
        exp_asked, exp_ready, chosen_ready, counted, placed, loads_ready, routed, dve_step, pool_step = ph.sems(
            "exp_asked exp_ready chosen_ready counted placed loads_ready routed dve_step pool_step")
        addr_ready, staged, tiles_staged, gate_done, up_done, silu_ready, h_ready, out_done, x_added = ph.sems(
            "addr_ready staged tiles_staged gate_done up_done silu_ready h_ready out_done x_added")
        scattered = [ph.sem(f"scattered{p}") for p in range(2)]
        block = ctx.enter_context(nc.Block())

        def over(x):
            return x[:, :].unsqueeze(2).to_broadcast([P, TT, E0])

        @block.sync
        def _(sp):
            sp.dma_start(gate_wt[:, :, :], d["gate_wt"].rearrange("(c p) e -> p c e", p=P)).then_inc(router_in, 16)
            sp.dma_start(slot_base[:, :], d["slot_base"]).then_inc(router_in, 16)
            sp.dma_start(wg[:, :, :], d["sh_gate"].rearrange("(c p) f -> p c f", p=P)).then_inc(weights_in, 16)
            sp.dma_start(wu[:, :, :], d["sh_up"].rearrange("(c p) f -> p c f", p=P)).then_inc(weights_in, 16)
            for k, (f, n) in enumerate(FTS):
                sp.dma_start(wd[0:n, k, :], d["sh_down"][f:f + n, :]).then_inc(weights_in, 16)
            with sp.Fori(ZA, ZN) as n:
                zero_slots(sp, t, d, n)

        @block.gpsimd
        def _(pool):
            pool.sem_inc(xn_copied, 2)
            pool.sem_inc(xt_ready, 2)
            pool.wait_ge(stats_ready, 1)
            row_rstd(pool, Serial(pool, pool_step, 0, 2), t)
            pool.sem_inc(rstd_ready, 1)
            with pool.Fori(0, TT // 2) as j:
                for p in range(2):
                    i = 2 * j + p
                    pool.wait_ge(xn_ready, i + 1)
                    pool.tensor_copy(row(t.xn, i), xns[p][:, :]).then_inc(xn_copied, 1)
                    pool.wait_ge(xts_ready, i + 1)
                    pool.tensor_copy(t.xt[:, :, ds(i * P, P)], xts[p][:, :].rearrange("p (c s) -> p c s", c=DC)).then_inc(xt_ready, 1)
            pool.wait_ge(routed, 1)
            pool.tensor_scalar(big[:, :, :], t.addr[:, :, :], 0.0, float(2 * SLOTS), ALU.is_equal, ALU.mult).then_inc(addr_ready, 1)
            pool.wait_ge(addr_ready, 1)
            pool.tensor_tensor(big[:, :, :], big[:, :, :], t.addr[:, :, :], ALU.add).then_inc(addr_ready, 1)
            pool.wait_ge(addr_ready, 2)
            pool.tensor_scalar(addr_f[:, :, :], big[:, :, :], -1.0, None, ALU.add).then_inc(addr_ready, 1)
            pool.wait_ge(addr_ready, 3)
            pool.wait_ge(t.zeroed, 16 * ZN)
            scatter_rows(pool, t, d, K0, addr_f, rows, to, staged, tiles_staged, scattered)

        @block.scalar
        def _(act):
            def copy_tile(i, p):
                act.wait_ge(tp_ready, 2 + i + 1)
                act.wait_ge(xt_ready, i + 1)
                act.wait_ge(logit_ready, i + 1)
                act.activation(xts[p][:, :], tp[p][:, :], ACT.Copy).then_inc(xts_ready, 1)

            def copy_logits(i, p):
                act.wait_ge(logit_ready, 2 + i + 1)
                act.activation(row(logit, i), lg[p][:, 0:E0], ACT.Copy).then_inc(logit_out, 1)

            copy_tile(0, 0)
            with act.Fori(0, TT // 2 - 1) as j:
                for p in range(2):
                    copy_tile(2 * j + p + 1, 1 - p)
                    copy_logits(2 * j + p, p)
            copy_tile(TT - 1, 1)
            copy_logits(TT - 2, 0)
            copy_logits(TT - 1, 1)
            act.wait_ge(exp_asked, 1)
            act.activation(logit[:, :, :], logit[:, :, :], ACT.Exp).then_inc(exp_ready, 1)
            with act.Fori(0, T // NTOK) as n:
                for k, (f, m) in enumerate(FTS):
                    u = n * NF + k
                    act.wait_ge(gate_done, u + 1)
                    act.wait_ge(h_ready, u + 1)
                    act.activation(sg[k % 2][0:m, :], pg[k % 2][0:m, :], ACT.Silu).then_inc(silu_ready, 1)

        @block.vector
        def _(dve):
            row_stats(dve, Serial(dve, dve_step, 0, ROW_STATS), t, stats6)
            dve.sem_inc(stats_ready, 1)
            dve.wait_ge(rstd_ready, 1)
            with dve.Fori(0, TT // 2) as j:
                for p in range(2):
                    i = 2 * j + p
                    dve.wait_ge(tp_ready, i + 1)
                    dve.wait_ge(xn_copied, i + 1)
                    dve.tensor_scalar(xns[p][:, :], row(t.x, i), t.mv_at(i, 0), t.rstd_at(i), ALU.subtract, ALU.mult).then_inc(xn_ready, 1)
            dve.sem_inc(h_ready, 2)
            dve.sem_inc(x_added, 2)

            def hidden(n, k):
                f, m = FTS[k]
                u = n * NF + k
                dve.wait_ge(up_done, u + 1)
                dve.wait_ge(silu_ready, u + 1)
                dve.tensor_tensor(h[0:m, k, :], sg[k % 2][0:m, :], pu[k % 2][0:m, :], ALU.mult).then_inc(h_ready, 1)

            def add(n, s):
                dve.wait_ge(out_done, n * NS + s + 1)
                xs = row(t.x, n * NS + s)
                dve.scalar_tensor_tensor(out=xs, in0=po[s % 2][:, :], scalar=t.gates[:, 1:2], in1=xs,
                                         op0=ALU.mult, op1=ALU.add).then_inc(x_added, 1)

            dve.wait_ge(logit_out, TT)
            dve.wait_ge(router_in, 32)
            step = Serial(dve, dve_step, ROW_STATS, 5 + TT + 1 + TT + 2 + (TT - 1) + 10 + (TT - 1) + 3 * K0)
            step(dve.reduce_max(small[:, :], logit[:, :, :], axis=AX.X))
            dve.tensor_tensor(logit[:, :, :], logit[:, :, :], over(small), ALU.subtract).then_inc(exp_asked, 1)
            step(dve.memset(score[:, :, E0:W], -1.0))
            dve.wait_ge(exp_ready, 1)
            step(dve.reduce_sum(small[:, :], logit[:, :, :], axis=AX.X))
            hidden(0, 0)
            step(dve.reciprocal(small[:, :], small[:, :]))
            step(dve.tensor_tensor(score[:, :, 0:E0], logit[:, :, :], over(small), ALU.mult))
            for i in range(TT):
                step(dve.max(top[:, i, :], score[:, i, :]))
            step(dve.memset(top[:, :, K0:8], -1.0))
            hidden(0, 1)
            for i in range(TT):
                step(dve.match_replace(taken[:, i, :], top[:, i, :], score[:, i, :], MARK))
            hidden(0, 2)
            step(dve.tensor_scalar(chosen[:, :, :], taken[:, :, 0:E0], MARK, None, ALU.is_equal))
            step(dve.memset(chosen_before[:, 0, :], 0.0))
            for i in range(1, TT + 1):
                ins = dve.tensor_tensor(chosen_before[:, i, :], chosen_before[:, i - 1, :], chosen[:, i - 1, :], ALU.add)
                if i == TT:
                    ins.then_inc(chosen_ready, 1)
                else:
                    step(ins)
            hidden(0, 3)
            step(dve.reduce_sum(small[:, :], top[:, :, 0:K0], axis=AX.X))
            step(dve.tensor_scalar(small[:, :], small[:, :], 1e-20, None, ALU.add))
            step(dve.reciprocal(small[:, :], small[:, :]))
            step(dve.tensor_tensor(wsel[:, :, :], score[:, :, 0:E0], over(small), ALU.mult))
            step(dve.tensor_scalar(wsel[:, :, :], wsel[:, :, :], t.gates[:, 1:2], None, ALU.mult))
            hidden(0, 4)
            dve.wait_ge(counted, 1)
            step(dve.tensor_scalar(taken[:, :, 0:E0], count[:, :, :], float(CAP), None, ALU.is_lt))
            step(dve.tensor_tensor(place[:, :, :], count[:, :, :], slot_base[:, :].unsqueeze(1).to_broadcast([P, TT, E0]), ALU.add))
            dve.sem_inc(placed, 1)
            hidden(0, 5)
            step(dve.tensor_tensor(chosen[:, :, :], chosen[:, :, :], taken[:, :, 0:E0], ALU.mult))
            step(dve.tensor_tensor(place[:, :, :], place[:, :, :], chosen[:, :, :], ALU.mult))
            step(dve.tensor_tensor(wsel[:, :, :], wsel[:, :, :], chosen[:, :, :], ALU.mult))
            add(0, 0)
            for i in range(TT):
                ins = dve.max(t.addr[:, i, :], place[:, i, :])
                if i == TT - 1:
                    ins.then_inc(routed, 1)
                else:
                    step(ins)
            add(0, 1)
            dve.wait_ge(counted, 2)
            dve.tensor_copy(t.load[:, :], load).then_inc(loads_ready, 1)
            dve.wait_ge(routed, 1)
            for k in range(K0):
                slot = t.addr[:, :, k].unsqueeze(2).to_broadcast([P, TT, E0])
                step(dve.tensor_tensor(taken[:, :, 0:E0], place[:, :, :], slot, ALU.is_equal))
                step(dve.tensor_tensor(taken[:, :, 0:E0], taken[:, :, 0:E0], wsel[:, :, :], ALU.mult))
                step(dve.reduce_sum(t.weight[:, :, k], taken[:, :, 0:E0], axis=AX.X))
                if k < 2:
                    add(0, 2 + k)
            step.close()
            with dve.Fori(1, T // NTOK) as n:
                for k in range(NF):
                    hidden(n, k)
                for s in range(NS):
                    add(n, s)

        @block.tensor
        def _(pe):
            pe.sem_inc(tp_ready, 2)
            pe.sem_inc(logit_ready, 2)

            def turn(i, p, first=False):
                pe.wait_ge(xn_ready, i + 1)
                if not first:
                    pe.wait_ge(xts_ready, i - 1)
                transposed_tile(pe, tp[p], xns[p], t).then_inc(tp_ready, 1)

            def logits(i, p, first=False):
                pe.wait_ge(xts_ready, i + 1)
                if not first:
                    pe.wait_ge(logit_out, i - 1)
                for c in range(DC):
                    mm = pe.matmul(lg[p][:, 0:E0], xts[p][:, c * P:(c + 1) * P], gate_wt[:, c, :], start=(c == 0), stop=(c == DC - 1))
                mm.then_inc(logit_ready, 1)

            pe.wait_ge(router_in, 32)
            turn(0, 0, first=True)
            for i in range(2):
                turn(i + 1, 1 - i, first=(i == 0))
                logits(i, i, first=True)
            with pe.Fori(1, TT // 2 - 1) as j:
                for p in range(2):
                    turn(2 * j + p + 1, 1 - p)
                    logits(2 * j + p, p)
            turn(TT - 1, 1)
            logits(TT - 2, 0)
            logits(TT - 1, 1)

            def up(n, k):
                f, m = FTS[k]
                pe.wait_ge(h_ready, n * NF + k + 1)
                for w, psum, done in ((wg, pg, gate_done), (wu, pu, up_done)):
                    for c in range(DC):
                        mm = pe.matmul(psum[k % 2][0:m, :], w[:, c, f:f + m], t.xt[:, c, ds(n * NTOK, NTOK)], start=(c == 0), stop=(c == DC - 1))
                    mm.then_inc(done, 1)

            def down(n):
                pe.wait_ge(h_ready, n * NF + NF + 2)
                for s in range(NS):
                    pe.wait_ge(x_added, n * NS + s + 1)
                    for k, (f, m) in enumerate(FTS):
                        mm = pe.matmul(po[s % 2][:, :], h[0:m, k, s * P:(s + 1) * P], wd[0:m, k, :], start=(k == 0), stop=(k == NF - 1))
                    mm.then_inc(out_done, 1)

            pe.wait_ge(xt_ready, 2 + TT)
            pe.wait_ge(logit_out, TT)
            pe.wait_ge(weights_in, 16 * (2 + NF))
            for k in range(NF - 1):
                up(0, k)
            pe.wait_ge(chosen_ready, 1)
            for i in range(0, TT, TT // 2):
                pe.matmul(count[:, i:i + TT // 2, :], t.before[:, :], chosen[:, i:i + TT // 2, :], start=True, stop=False)
                mm = pe.matmul(count[:, i:i + TT // 2, :], t.ones[:, :], chosen_before[:, i:i + TT // 2, :], start=False, stop=True)
            mm.then_inc(counted, 1)
            up(0, NF - 1)
            pe.wait_ge(placed, 1)
            pe.matmul(load, t.ones[:, :], chosen_before[:, TT, :], start=True, stop=True).then_inc(counted, 1)
            down(0)
            with pe.Fori(1, T // NTOK) as n:
                for k in range(NF):
                    up(n, k)
                down(n)


def experts(nc, t, d):
    with ExitStack() as ctx:
        ph = Phase(nc, ctx, "e_")
        NF = len(FT0)
        wg = [ph.sb(f"wg{p}", [P, DC, F0]) for p in range(2)]
        wu = [ph.sb(f"wu{p}", [P, DC, F0]) for p in range(2)]
        wd = [ph.sb(f"wd{p}", [P, NF, D]) for p in range(2)]
        xs = [ph.sb(f"xs{p}", [P, CT, D]) for p in range(2)]
        xt = [ph.sb(f"xt{p}", [P, DC, CAP]) for p in range(2)]
        sg = [ph.sb(f"sg{p}", [P, CAP]) for p in range(2)]
        h = [ph.sb(f"h{p}", [P, NF, CAP]) for p in range(2)]
        eo = [ph.sb(f"eo{p}", [P, CT, D]) for p in range(2)]
        tp = [ph.ps(f"tp{p}", [P, D]) for p in range(2)]
        pg = [ph.ps(f"pg{p}", [P, D]) for p in range(2)]
        pu = [ph.ps(f"pu{p}", [P, D]) for p in range(2)]
        po = [ph.ps(f"po{p}", [P, D]) for p in range(2)]
        weights_in = [ph.sem(f"weights_in{p}") for p in range(2)]
        xs_in = [ph.sem(f"xs_in{p}") for p in range(2)]
        stored = [ph.sem(f"stored{p}") for p in range(2)]
        tp_ready, xt_ready, gate_done, up_done, silu_ready, h_ready, out_done, eo_ready = ph.sems(
            "tp_ready xt_ready gate_done up_done silu_ready h_ready out_done eo_ready")
        block = ctx.enter_context(nc.Block())

        def by_load(eng, e, body):
            load = eng.value_load(t.load[0:1, ds(e, 1)], min_val=0, max_val=T)
            with eng.If(load > (CT - 1) * P):
                body(CT)
            with eng.Else():
                body(CT - 1)

        def rest(n, s):
            return 1 + CT - n if s == n - 1 else 1

        @block.sync
        def _(sp):
            with sp.Fori(0, E0 // 2) as j:
                for p in range(2):
                    e = 2 * j + p
                    sp.wait_ge(out_done, CT * (e + 1))
                    sp.dma_start(wg[p][:, :, :], d["w_gate"][ds(e, 1), :, :, :].rearrange("o p c f -> (o p) c f")).then_inc(weights_in[p], 16)
                    sp.dma_start(wu[p][:, :, :], d["w_up"][ds(e, 1), :, :, :].rearrange("o p c f -> (o p) c f")).then_inc(weights_in[p], 16)
                    for k, (f, m) in enumerate(FT0):
                        sp.dma_start(wd[p][0:m, k, :], d["w_down"][ds(e, 1), f:f + m, :].rearrange("o f d -> (o f) d")).then_inc(weights_in[p], 16)

        @block.gpsimd
        def _(pool):
            pool.sem_inc(tp_ready, 2 * CT)
            with pool.Fori(0, E0 // 2) as j:
                for p in range(2):
                    e = 2 * j + p

                    def body(n):
                        pool.wait_ge(tp_ready, CT * (e + 1))
                        pool.dma_start(xs[p][:, 0:n, :], d["slots"][ds(e * CAP, n * P), :].rearrange("(s p) d -> p s d", p=P)).then_inc(xs_in[p], 16)
                    by_load(pool, e, body)

        @block.scalar
        def _(act):
            def copy_rows(e, p):
                def body(n):
                    for s in range(n):
                        u = CT * e + s
                        act.wait_ge(tp_ready, 2 * CT + u + 1)
                        act.activation(xt[p][:, :, s * P:(s + 1) * P], tp[(CT * p + s) % 2][:, :].rearrange("p (c s) -> p c s", c=DC),
                                       ACT.Copy).then_inc(xt_ready, rest(n, s))
                by_load(act, e, body)

            def silus(e, p):
                def body(n):
                    for k, (f, m) in enumerate(FT0):
                        u = NF * e + k
                        act.wait_ge(gate_done, u + 1)
                        act.wait_ge(h_ready, u + 1)
                        q = (NF * p + k) % 2
                        act.activation(sg[q][0:m, 0:n * P], pg[q][0:m, 0:n * P], ACT.Silu).then_inc(silu_ready, 1)
                by_load(act, e, body)

            def store(e, p):
                def body(n):
                    act.wait_ge(eo_ready, 2 + CT * (e + 1))
                    act.dma_start(d["slots"][ds(e * CAP, n * P), :].rearrange("(s p) d -> p s d", p=P), eo[p][:, 0:n, :]).then_inc(stored[p], 16)
                by_load(act, e, body)

            copy_rows(0, 0)
            with act.Fori(0, E0 // 2 - 1) as j:
                for p in range(2):
                    silus(2 * j + p, p)
                    copy_rows(2 * j + p + 1, 1 - p)
                    store(2 * j + p, p)
            silus(E0 - 2, 0)
            copy_rows(E0 - 1, 1)
            store(E0 - 2, 0)
            silus(E0 - 1, 1)
            store(E0 - 1, 1)
            for p in range(2):
                act.wait_ge(stored[p], 16 * (E0 // 2))

        @block.vector
        def _(dve):
            dve.sem_inc(h_ready, 2)
            dve.sem_inc(eo_ready, 2)

            def hidden_and_out(j, p, first=False):
                e = 2 * j + p

                def body(n):
                    for k, (f, m) in enumerate(FT0):
                        u = NF * e + k
                        q = (NF * p + k) % 2
                        dve.wait_ge(up_done, u + 1)
                        dve.wait_ge(silu_ready, u + 1)
                        dve.tensor_tensor(h[p][0:m, k, 0:n * P], sg[q][0:m, 0:n * P], pu[q][0:m, 0:n * P], ALU.mult).then_inc(h_ready, 1)
                    if not first:
                        dve.wait_ge(stored[p], 16 * j)
                    for s in range(n):
                        dve.wait_ge(out_done, 2 * CT + CT * e + s + 1)
                        dve.tensor_copy(eo[p][:, s, :], po[(CT * p + s) % 2][:, :]).then_inc(eo_ready, rest(n, s))
                by_load(dve, e, body)

            for p in range(2):
                hidden_and_out(0, p, first=True)
            with dve.Fori(1, E0 // 2) as j:
                for p in range(2):
                    hidden_and_out(j, p)

        @block.tensor
        def _(pe):
            pe.sem_inc(out_done, 2 * CT)
            pe.sem_inc(xt_ready, 2)

            def transposes(j, e, p):
                def body(n):
                    pe.wait_ge(xs_in[p], 16 * (j + 1))
                    for s in range(n):
                        pe.wait_ge(xt_ready, CT * e + s + 1)
                        transposed_tile(pe, tp[(CT * p + s) % 2], xs[p][:, s, :], t).then_inc(tp_ready, rest(n, s))
                by_load(pe, e, body)

            def up(j, e, p):
                def body(n):
                    pe.wait_ge(weights_in[p], 16 * (2 + NF) * (j + 1))
                    pe.wait_ge(xt_ready, 2 + CT * (e + 1))
                    for k, (f, m) in enumerate(FT0):
                        u = NF * e + k
                        q = (NF * p + k) % 2
                        pe.wait_ge(h_ready, u + 1)
                        for c in range(DC):
                            mm = pe.matmul(pg[q][0:m, 0:n * P], wg[p][:, c, f:f + m], xt[p][:, c, 0:n * P], start=(c == 0), stop=(c == DC - 1))
                        mm.then_inc(gate_done, 1)
                        for c in range(DC):
                            mm = pe.matmul(pu[q][0:m, 0:n * P], wu[p][:, c, f:f + m], xt[p][:, c, 0:n * P], start=(c == 0), stop=(c == DC - 1))
                        mm.then_inc(up_done, 1)
                by_load(pe, e, body)

            def down(e, p):
                def body(n):
                    pe.wait_ge(h_ready, 2 + NF * (e + 1))
                    for s in range(n):
                        pe.wait_ge(eo_ready, CT * e + s + 1)
                        for k, (f, m) in enumerate(FT0):
                            mm = pe.matmul(po[(CT * p + s) % 2][:, :], h[p][0:m, k, s * P:(s + 1) * P], wd[p][0:m, k, :], start=(k == 0), stop=(k == NF - 1))
                        mm.then_inc(out_done, rest(n, s))
                by_load(pe, e, body)

            transposes(0, 0, 0)
            with pe.Fori(0, E0 // 2 - 1) as j:
                for p in range(2):
                    e = 2 * j + p
                    up(j, e, p)
                    transposes(j + p, e + 1, 1 - p)
                    down(e, p)
            j = E0 // 2 - 1
            up(j, E0 - 2, 0)
            transposes(j, E0 - 1, 1)
            down(E0 - 2, 0)
            up(j, E0 - 1, 1)
            down(E0 - 1, 1)


def combine(nc, t, d, prefix, choices):
    with ExitStack() as ctx:
        ph = Phase(nc, ctx, prefix)
        addr_f = ph.sb("addr_f", [P, TT, 8])
        low = ph.sb("low", [P, TT, 8])
        frm = [ph.sb(f"frm{p}", [P, 8], U32) for p in range(2)]
        y = [ph.sb(f"y{p}", [P, choices, D]) for p in range(2)]
        addr_ready, staged, tiles_staged, y_used = ph.sems("addr_ready staged tiles_staged y_used")
        gathered = [ph.sem(f"gathered{p}") for p in range(2)]
        block = ctx.enter_context(nc.Block())

        @block.gpsimd
        def _(pool):
            pool.tensor_scalar(low[:, :, :], t.addr[:, :, :], 1.0, None, ALU.max).then_inc(addr_ready, 1)
            pool.wait_ge(addr_ready, 1)
            pool.tensor_scalar(addr_f[:, :, :], low[:, :, :], -1.0, None, ALU.add).then_inc(addr_ready, 1)
            pool.wait_ge(addr_ready, 2)
            with pool.Fori(0, TT // 2) as j:
                for p in range(2):
                    i = 2 * j + p
                    pool.wait_ge(y_used, choices * (i + 1))
                    pool.tensor_copy(frm[p][:, :], row(addr_f, i)).then_inc(staged, 1)
                    pool.wait_ge(staged, i + 1)
                    pool.sem_inc(tiles_staged, 1)
                    for k in range(choices):
                        pool.indirect_dma_start(out=y[p][:, k, :], out_offset=None, in_=d["slots"],
                                                in_offset=bass.IndirectOffsetOnAxis(ap=frm[p][:, k:k + 1], axis=0),
                                                bounds_check=SLOTS - 1, oob_is_err=False).then_inc(gathered[p], 16)

        @block.vector
        def _(dve):
            dve.sem_inc(y_used, 2 * choices)
            with dve.Fori(0, TT // 2) as j:
                for p in range(2):
                    i = 2 * j + p
                    dve.wait_ge(gathered[p], 16 * choices * (j + 1))
                    for k in range(choices):
                        xs = row(t.x, i)
                        w = t.weight[:, ds(i, 1), k:k + 1].rearrange("p o k -> p (o k)")
                        dve.scalar_tensor_tensor(out=xs, in0=y[p][:, k, :], scalar=w, in1=xs, op0=ALU.mult, op1=ALU.add).then_inc(y_used, 1)
                        dve.wait_ge(y_used, 2 * choices + choices * i + k + 1)


def layer0(nc, t, d, stop):
    with ExitStack() as ctx:
        ph = Phase(nc, ctx, "m_")
        t.addr = ph.sb("addr", [P, TT, 8])
        t.weight = ph.sb("weight", [P, TT, K0])
        t.load = ph.sb("load", [P, E0], U32)
        with ExitStack() as inner:
            ph = Phase(nc, inner, "z_")
            t.zero = ph.sb("zero", [P, ZROWS * D])
            t.zeroed, = ph.sems("zeroed")
            layer0_attention(nc, t, d)
            route_and_share(nc, t, d)
        experts(nc, t, d)
        combine(nc, t, d, "c_", K0)


def layer1_attention(nc, t, d):
    NU = ST * NH // 2
    NM = NH // 8
    NG = NH // 4
    NP = 4
    LT = 3
    NR = 3 * NM * 4 // 2
    KT = 2 * ST
    SWAP = [i ^ (HD // 2) for i in range(32)]
    with ExitStack() as ctx:
        ph = Phase(nc, ctx, "q_")
        stats6 = ph.sb("stats6", [P, TT, 6])
        wq = ph.sb("wq", [P, DC, D])
        wk = ph.sb("wk", [P, DC, D])
        wv = ph.sb("wv", [P, DC, D])
        wo = ph.sb("wo", [P, NG, D])
        rope = ph.sb("rope", [P, 2, S])
        rep = ph.sb("rep", [P, 2, 2, 4, P], F32R)
        head_gate = ph.sb("head_gate", [P, NH // 2, 4])
        mask = ph.sb("mask", [P, ST, S])
        cxt = ph.sb("cxt", [P, DC, S])
        qs = ph.sb("qs", [P, NH // 2, S], F32R)
        ks = ph.sb("ks", [P, NH // 2, 2 * S], F32R)
        vv = ph.sb("vv", [P, KT, NH, HD])
        masked = ph.sb("masked", [P, 2, 2, S])
        xns = masked[:, :, :, :].rearrange("p a k s -> p a (k s)")
        top = ph.sb("top", [P, 4])
        ntop = [ph.sb(f"ntop{p}", [P, 4]) for p in range(2)]
        total = [ph.sb(f"total{p}", [P, 4]) for p in range(2)]
        share = [ph.sb(f"share{p}", [P, 4]) for p in range(2)]
        norm = [ph.sb(f"norm{p}", [P, 4]) for p in range(2)]
        prob = [ph.sb(f"prob{p}", [P, 2, 2 * S]) for p in range(NP)]
        probt, probt_at = [], []
        for p in range(2):
            probt_at.append(nc.sbuf_base)
            probt.append(ph.sb(f"probt{p}", [P, 4, KT, S]))
        turned, straight = ([x[:, k, :, :] for x in probt] for k in range(2))
        part_bytes = NM * S * 4
        high, low = ([nc.alloc_sbuf_tensor_at(f"q_{name}{p}", [P, NM, S], F32R, offset=probt_at[p] + k * part_bytes) for p in range(2)]
                     for name, k in (("high", 2), ("low", 3)))
        ots = ph.sb("ots", [P, NG, S])
        xt = ots[:, 0:DC, :]
        score = [ph.ps(f"score{p}", [P, 2, D]) for p in range(2)]
        tps = ph.ps("tps", [P, 2, D])
        ot = [ph.ps(f"ot{p}", [P, D]) for p in range(2)]
        ring = [tps[:, 0, :], tps[:, 1, :], ot[0][:, :], ot[1][:, :]]
        weights_in, ctx_in, mask_in, gates_ready, stats_ready, rstd_ready, xn_ready, xtp_ready, xt_ready = ph.sems(
            "weights_in ctx_in mask_in gates_ready stats_ready rstd_ready xn_ready xtp_ready xt_ready")
        q_done, k_done, ak_done, v_done, av_done, q_turned, k_turned, q_split, k_split, ak_high, ak_split, v_ready = ph.sems(
            "q_done k_done ak_done v_done av_done q_turned k_turned q_split k_split ak_high ak_split v_ready")
        rep_in, rep_ready, stack_done, stacked_act, stacked_dve = ph.sems("rep_in rep_ready stack_done stacked_act stacked_dve")
        score_ready, mask_used, top_ready, exp_ready, norm_ready, prob_ready, tps_ready, probt0_ready, probt1_ready, value_done = ph.sems(
            "score_ready mask_used top_ready exp_ready norm_ready prob_ready tps_ready probt0_ready probt1_ready value_done")
        ot_copied, out_ready, dve_step, pool_step, norm_seen, dve_seen = ph.sems("ot_copied out_ready dve_step pool_step norm_seen dve_seen")
        block = ctx.enter_context(nc.Block())

        def stack_tiles(c):
            kind, m, a = c // 8, c // 4 % 2 * 2, c % 4
            dst = (qs[:, :, :], ks[:, :, 0:S], ks[:, :, S:2 * S])[kind]
            return kind, m, a, dst[:, 4 * m + a:4 * m + a + 5:4, :]

        def unit(u):
            g, s, pr = u // 4, u // 2 % 2, u % 2
            return g, s, pr, 2 * g + pr

        @block.sync
        def _(sp):
            for w, n in ((wq, "wq"), (wk, "wk"), (wv, "wv")):
                sp.dma_start(w[:, :, :], d[n].rearrange("(c p) n -> p c n", p=P)).then_inc(weights_in, 16)
            sp.dma_start(wo[:, :, :], d["wo"]).then_inc(weights_in, 16)
            sp.dma_start(rope[:, :, :], d["rope"]).then_inc(weights_in, 16)
            sp.dma_start(probt[0][:, 0:2, :, :].rearrange("p a k s -> p (a k s)"), d["rep"]).then_inc(rep_in, 16)
            sp.dma_start(head_gate[:, :, :], d["head_gate"]).then_inc(weights_in, 16)

            def load(b):
                sp.dma_start(cxt[:, :, :], d["ctx_t"][ds(b, 1), :, :].rearrange("o (c p) s -> p (o c) s", p=P)).then_inc(ctx_in, 16)

            def load_mask(b):
                sp.dma_start(mask[:, :, :], d["mask"][ds(b, 1), :, :].rearrange("o (t p) k -> p (o t) k", p=P)).then_inc(mask_in, 16)

            load(0)
            load_mask(0)
            with sp.Fori(1, B) as b:
                sp.wait_ge(av_done, b)
                load(b)
                sp.wait_ge(mask_used, b)
                load_mask(b)

        @block.gpsimd
        def _(pool):
            pool.wait_ge(stats_ready, 1)
            row_rstd(pool, Serial(pool, pool_step, 0, 2), t)
            pool.sem_inc(rstd_ready, 1)
            with pool.Fori(0, B) as b:
                for u in range(NU):
                    pool.wait_ge(norm_ready, b * NU + u + 1)
                    pool.sem_inc(norm_seen, 1)
                    for k in range(4):
                        half = prob[u % NP][:, k % 2, (k // 2) * S:(k // 2 + 1) * S]
                        pool.tensor_scalar(half, half, norm[u % 2][:, k:k + 1], 1.0, ALU.mult, ALU.mult).then_inc(prob_ready, 1)

        @block.scalar
        def _(act):
            act.wait_ge(weights_in, 6 * 16)
            act.activation(head_gate[:, :, 2:4], head_gate[:, :, 2:4], ACT.Tanh).then_inc(gates_ready, 1)
            with act.Fori(0, B) as b:
                for s in range(ST):
                    act.wait_ge(xtp_ready, ST * b + s + 1)
                    act.activation(xt[:, :, s * P:(s + 1) * P], tps[:, s, :].rearrange("p (c s) -> p c s", c=DC), ACT.Copy).then_inc(xt_ready, 1)
                def stack(c):
                    act.wait_ge(stack_done, NR * b + c + 1)
                    act.activation(stack_tiles(c)[3], ring[c % 4].rearrange("p (t s) -> p t s", s=S), ACT.Copy).then_inc(stacked_act, 1)

                def values(k):
                    act.activation(vv[:, k, :, :], score[1 - k // ST][:, k % ST, :].rearrange("p (h d) -> p h d", d=HD), ACT.Copy).then_inc(v_ready, 1)

                for c in range(0, 8, 2):
                    stack(c)
                act.wait_ge(ak_done, b + 1)
                act.wait_ge(stack_done, NR * b + 8)
                act.activation(high[0][:, :, :], score[0][:, :, :].rearrange("p a (m s) -> p (a m) s", s=S), ACT.Copy).then_inc(ak_high, 1)
                act.wait_ge(v_done, b + 1)
                for k in range(ST):
                    values(k)
                for c in range(8, 16, 2):
                    stack(c)
                act.wait_ge(av_done, b + 1)
                for k in range(ST, KT):
                    values(k)
                for c in range(16, NR, 2):
                    stack(c)
                for i in range(NU + LT + 2):
                    v = i - LT
                    if 0 <= v < NU:
                        act.wait_ge(tps_ready, b * NU + v + 1)
                        g, s, pr, pair = unit(v)
                        if g >= 2 and v % 4 == 0:
                            act.wait_ge(value_done, b * NG + g - 1)
                        act.activation(probt[g % 2][:, 2 * pr + 1, :, s * P:(s + 1) * P], tps[:, 1, :].rearrange("p (n q) -> p n q", q=P), ACT.Copy).then_inc(probt1_ready, 1)
                    if i < NU:
                        act.wait_ge(top_ready, b * NU + i + 1)
                        if i >= NP:
                            act.wait_ge(tps_ready, b * NU + i - NP + 1)
                        for k in range(4):
                            src = masked[:, i % 2, k, :] if k < 2 else score[i % 2][:, k - 2, S:2 * S]
                            act.activation(prob[i % NP][:, k % 2, (k // 2) * S:(k // 2 + 1) * S], src, ACT.Exp,
                                           bias=ntop[i % 2][:, k:k + 1], accum_out=total[i % 2][:, k:k + 1]).then_inc(exp_ready, 1)
                    v = i - LT - 2
                    if v >= 0 and v % 4 == 3:
                        act.wait_ge(value_done, b * NG + v // 4 + 1)
                        act.activation(ots[:, v // 4, :], ot[v // 4 % 2][:, 0:S], ACT.Copy).then_inc(ot_copied, 1)

        @block.vector
        def _(dve):
            row_stats(dve, Serial(dve, dve_step, 0, ROW_STATS), t, stats6)
            dve.sem_inc(stats_ready, 1)
            dve.wait_ge(gates_ready, 1)
            step = Serial(dve, dve_step, ROW_STATS, 1)
            step(dve.memset(head_gate[:, :, 0:2], 1.0))
            dve.wait_ge(rep_in, 16)
            dve.tensor_copy(rep[:, :, :, :, :].rearrange("p a b c q -> p (a b c q)"), probt[0][:, 0:2, :, :].rearrange("p a k s -> p (a k s)")).then_inc(rep_ready, 1)
            dve.wait_ge(rep_ready, 1)
            dve.wait_ge(rstd_ready, 1)
            steps = 2 * 4 + 4 * NU
            with dve.Fori(0, B) as b:
                step = Serial(dve, dve_step, ROW_STATS + 1 + b * steps, steps)
                for s in range(ST):
                    dve.tensor_scalar(xns[:, s, :], row(t.x, ST * b + s), t.mv_at(ST * b + s, 0), t.rstd_at(ST * b + s),
                                      ALU.subtract, ALU.mult).then_inc(xn_ready, 1)
                for n, done, raw_read, split in ((0, q_done, q_turned, q_split), (1, k_done, k_turned, k_split)):
                    dve.wait_ge(done, b + 1)
                    raw = score[n][:, :, :].rearrange("p a (m s) -> p (a m) s", s=S)
                    cos = rope[:, 0, :].unsqueeze(1).to_broadcast([P, NM, S])
                    sin = rope[:, 1, :].unsqueeze(1).to_broadcast([P, NM, S])
                    dve.sem_inc(dve_seen, 1)
                    step(dve.stream_shuffle(turned[n].rearrange("p m s -> p (m s)"), score[n][:, :, :].rearrange("p a f -> p (a f)"), SWAP))
                    dve.tensor_tensor(straight[n], raw, cos, ALU.mult).then_inc(raw_read, 1)
                    step(dve.tensor_tensor(turned[n], turned[n], sin, ALU.mult))
                    step(dve.tensor_tensor(straight[n], straight[n], turned[n], ALU.add))
                    step(dve.tensor_copy(high[n][:, :, :], straight[n]))
                    dve.tensor_tensor(low[n][:, :, :], straight[n], high[n][:, :, :].bitcast(F32), ALU.subtract).then_inc(split, 1)

                def stack(c):
                    dve.wait_ge(stack_done, NR * b + c + 1)
                    dve.tensor_copy(stack_tiles(c)[3], ring[c % 4].rearrange("p (t s) -> p t s", s=S)).then_inc(stacked_dve, 1)

                for c in range(1, 8, 2):
                    stack(c)
                dve.wait_ge(ak_high, b + 1)
                dve.tensor_tensor(low[0][:, :, :], score[0][:, :, :].rearrange("p a (m s) -> p (a m) s", s=S), high[0][:, :, :].bitcast(F32), ALU.subtract).then_inc(ak_split, 1)
                for c in range(9, NR, 2):
                    stack(c)
                dve.wait_ge(mask_in, 16 * (b + 1))
                step(dve.tensor_scalar(mask[:, :, :], mask[:, :, :], FMIN, None, ALU.max))
                for i in range(NU + LT):
                    if i < NU:
                        g, s, pr, pair = unit(i)
                        dve.wait_ge(score_ready, b * NU + i + 1)
                        if i >= 2:
                            dve.wait_ge(exp_ready, 4 * (b * NU + i - 1))
                        dve.sem_inc(dve_seen, 1)
                        for k in range(2):
                            ins = dve.tensor_tensor_reduce(out=masked[:, i % 2, k, :], in0=score[i % 2][:, k, 0:S], in1=mask[:, s, :], scale=1.0,
                                                           scalar=FMIN, op0=ALU.add, op1=ALU.max, accum_out=top[:, k:k + 1])
                            if i == NU - 1 and k == 1:
                                ins.then_inc(mask_used, 1)
                            else:
                                step.later(ins)
                        step.later(dve.reduce_max(top[:, 2:4], score[i % 2][:, :, S:2 * S], axis=AX.X))
                        step.all()
                        if i == NU - 1:
                            dve.wait_ge(mask_used, b + 1)
                        dve.tensor_scalar(ntop[i % 2][:, :], top[:, :], -1.0, None, ALU.mult).then_inc(top_ready, 1)
                        dve.wait_ge(top_ready, b * NU + i + 1)
                    v = i - 1
                    if 0 <= v < NU:
                        g, s, pr, pair = unit(v)
                        if v >= 2:
                            dve.wait_ge(prob_ready, 4 * (b * NU + v - 1))
                        dve.wait_ge(exp_ready, 4 * (b * NU + v + 1))
                        step(dve.reciprocal(share[v % 2][:, :], total[v % 2][:, :]))
                        dve.tensor_tensor(norm[v % 2][:, :], share[v % 2][:, :], head_gate[:, pair, :], ALU.mult).then_inc(norm_ready, 1)
                    v = i - LT
                    if 0 <= v < NU:
                        dve.wait_ge(tps_ready, b * NU + v + 1)
                        g, s, pr, pair = unit(v)
                        if g >= 2 and v % 4 == 0:
                            dve.wait_ge(value_done, b * NG + g - 1)
                        dve.tensor_copy(probt[g % 2][:, 2 * pr, :, s * P:(s + 1) * P], tps[:, 0, :].rearrange("p (n q) -> p n q", q=P)).then_inc(probt0_ready, 1)
                for s in range(ST):
                    dve.wait_ge(out_ready, ST * b + s + 1)
                    xs = row(t.x, ST * b + s)
                    dve.scalar_tensor_tensor(out=xs, in0=tps[:, s, :], scalar=t.gates[:, 2:3], in1=xs, op0=ALU.mult, op1=ALU.add)
                step.close()

        @block.tensor
        def _(pe):
            pe.wait_ge(weights_in, 6 * 16)

            def heads_by_position(psum, w, x):
                for m in range(NM):
                    for c in range(DC):
                        mm = pe.matmul(psum[:, m // 2, (m % 2) * S:(m % 2 + 1) * S], w[:, c, m * P:(m + 1) * P], x[:, c, :], start=(c == 0), stop=(c == DC - 1))
                return mm

            def positions_by_head(psum, w, x):
                for s in range(ST):
                    for c in range(DC):
                        mm = pe.matmul(psum[:, s, :], x[:, c, s * P:(s + 1) * P], w[:, c, :], start=(c == 0), stop=(c == DC - 1))
                return mm

            with pe.Fori(0, B) as b:
                for s in range(ST):
                    pe.wait_ge(xn_ready, ST * b + s + 1)
                    transposed_tile(pe, tps[:, s, :], xns[:, s, :], t).then_inc(xtp_ready, 1)
                pe.wait_ge(xt_ready, ST * b + ST)
                heads_by_position(score[0], wq, xt).then_inc(q_done, 1)
                heads_by_position(score[1], wk, xt).then_inc(k_done, 1)
                def stack(kind):
                    for c in range(8 * kind, 8 * kind + 8):
                        if c >= 4:
                            pe.wait_ge((stacked_act, stacked_dve)[c % 2], NR // 2 * b + c // 2 - 1)
                        _, m, a, _ = stack_tiles(c)
                        n = kind % 2
                        pe.matmul(ring[c % 4], rep[:, min(kind, 1), 0, a, :], high[n][:, m:m + 2, :].rearrange("p m s -> p (m s)"), start=True, stop=False)
                        pe.matmul(ring[c % 4], rep[:, min(kind, 1), 1, a, :], low[n][:, m:m + 2, :].rearrange("p m s -> p (m s)"), start=False, stop=True).then_inc(stack_done, 1)

                pe.wait_ge(q_turned, b + 1)
                pe.wait_ge(ctx_in, 16 * (b + 1))
                heads_by_position(score[0], wk, cxt).then_inc(ak_done, 1)
                pe.wait_ge(q_split, b + 1)
                stack(0)
                pe.wait_ge(k_turned, b + 1)
                positions_by_head(score[1], wv, xt).then_inc(v_done, 1)
                pe.wait_ge(k_split, b + 1)
                stack(1)
                pe.wait_ge(ak_split, b + 1)
                positions_by_head(score[0], wv, cxt).then_inc(av_done, 1)
                stack(2)
                pe.wait_ge(stacked_act, NR // 2 * (b + 1))
                pe.wait_ge(stacked_dve, NR // 2 * (b + 1))
                pe.wait_ge(v_ready, KT * (b + 1))
                for i in range(NU + LT + 1):
                    if i < NU:
                        g, s, pr, pair = unit(i)
                        if i >= 2:
                            pe.wait_ge(exp_ready, 4 * (b * NU + i - 1))
                        for k in range(2):
                            mm = pe.matmul(score[i % 2][:, k, :], qs[64 * k:64 * k + 64, pair, s * P:(s + 1) * P], ks[64 * k:64 * k + 64, pair, :], start=True, stop=True)
                        mm.then_inc(score_ready, 1)
                    v = i - LT
                    if 0 <= v < NU:
                        pe.wait_ge(prob_ready, 4 * (b * NU + v + 1))
                        if v >= 1:
                            pe.wait_ge(probt0_ready, b * NU + v)
                            pe.wait_ge(probt1_ready, b * NU + v)
                        for k in range(2):
                            mm = transposed_tile(pe, tps[:, k, :], prob[v % NP][:, k, :], t)
                        mm.then_inc(tps_ready, 1)
                    v = i - LT - 1
                    if v >= 0 and v % 4 == 3:
                        g = v // 4
                        pe.wait_ge(probt0_ready, b * NU + v + 1)
                        pe.wait_ge(probt1_ready, b * NU + v + 1)
                        if g >= 2:
                            pe.wait_ge(ot_copied, b * NG + g - 1)
                        for n in range(KT):
                            for c in range(4):
                                mm = pe.matmul(ot[g % 2][32 * c:32 * c + HD, 0:S], vv[:, n, 4 * g + c, :], probt[g % 2][:, c, n, :], start=(n == 0), stop=(n == KT - 1))
                        mm.then_inc(value_done, 1)
                pe.wait_ge(ot_copied, NG * (b + 1))
                for s in range(ST):
                    for g in range(NG):
                        mm = pe.matmul(tps[:, s, :], ots[:, g, s * P:(s + 1) * P], wo[:, g, :], start=(g == 0), stop=(g == NG - 1))
                    mm.then_inc(out_ready, 1)


def moe1(nc, t, d):
    with ExitStack() as ctx:
        ph = Phase(nc, ctx, "v_")
        t.addr = ph.sb("addr", [P, TT, 8])
        t.weight = ph.sb("weight", [P, TT, K1])
        t.job_expert = ph.sb("job_expert", [P, NJ], U32)
        t.jobs = ph.sb("jobs", [P, 4], U32)
        with ExitStack() as inner:
            ph = Phase(nc, inner, "u_")
            t.xn = ph.sb("xn", [P, TT, D])
            route1(nc, t, d)
            experts1(nc, t, d)
        combine(nc, t, d, "y_", K1)


def route1(nc, t, d):
    W = E1 + 8 - K1
    with ExitStack() as ctx:
        ph = Phase(nc, ctx, "w_")
        stats6 = ph.sb("stats6", [P, TT, 6])
        router_t = ph.sb("router_t", [P, DC, E1])
        router_b = ph.sb("router_b", [P, E1])
        down_b = ph.sb("down_b", [E1, D])
        job_starts = ph.sb("job_starts", [P, E1, MJ])
        up_to = ph.sb("up_to", [P, E1, E1])
        job_number = ph.sb("job_number", [P, NJ])
        xns = [ph.sb(f"xns{p}", [P, D]) for p in range(2)]
        xts = [ph.sb(f"xts{p}", [P, D]) for p in range(2)]
        logit = ph.sb("logit", [P, TT, W])
        taken = ph.sb("taken", [P, TT, W])
        top = ph.sb("top", [P, TT, 8])
        expd = ph.sb("expd", [P, TT, E1])
        mix = ph.sb("mix", [P, TT, E1])
        chosen = ph.sb("chosen", [P, TT, E1])
        chosen_before = ph.sb("chosen_before", [P, TT + 1, E1])
        place = ph.sb("place", [P, TT, E1])
        total = ph.sb("total", [P, TT])
        started = ph.sb("started", [P, E1, MJ])
        jobs_of = ph.sb("jobs_of", [P, E1])
        jobs_up_to = ph.sb("jobs_up_to", [P, E1, E1])
        job_end = ph.sb("job_end", [P, E1])
        slot_base = ph.sb("slot_base", [P, E1])
        ended = ph.sb("ended", [P, NJ, E1])
        job_counts = ph.sb("job_counts", [P, NJ])
        mixt = ph.sb("mixt", [E1, T])
        tp = [ph.ps(f"tp{p}", [P, D]) for p in range(2)]
        lg = ph.ps("lg", [P, D])
        mt = ph.ps("mt", [E1, T])
        out = ph.ps("out", [P, D])
        count = lg[:, 0:TT * E1].rearrange("p (i e) -> p i e", e=E1)
        load = lg[:, TT * E1:(TT + 1) * E1]
        weights_in, stats_ready, rstd_ready, xn_ready, xn_copied, tp_ready, xts_ready, logit_ready, logit_out = ph.sems(
            "weights_in stats_ready rstd_ready xn_ready xn_copied tp_ready xts_ready logit_ready logit_out")
        exp_asked, exp_ready, mix_ready, mt_ready, mixt_ready, bias_ready, x_added, chosen_ready, counted, dve_step, pool_step = ph.sems(
            "exp_asked exp_ready mix_ready mt_ready mixt_ready bias_ready x_added chosen_ready counted dve_step pool_step")
        block = ctx.enter_context(nc.Block())

        def over(x, n=E1):
            return x.unsqueeze(2).to_broadcast([P, TT, n])

        @block.sync
        def _(sp):
            sp.dma_start(router_t[:, :, :], d["router_t"].rearrange("(c p) e -> p c e", p=P)).then_inc(weights_in, 16)
            sp.dma_start(router_b[:, :], d["router_b"]).then_inc(weights_in, 16)
            sp.dma_start(down_b[:, :], d["down_b"]).then_inc(weights_in, 16)
            sp.dma_start(job_starts[:, :, :], d["job_starts"]).then_inc(weights_in, 16)
            sp.dma_start(up_to[:, :, :], d["up_to"]).then_inc(weights_in, 16)
            sp.dma_start(job_number[:, :], d["job_number"]).then_inc(weights_in, 16)

        @block.gpsimd
        def _(pool):
            pool.sem_inc(xn_copied, 2)
            pool.wait_ge(stats_ready, 1)
            row_rstd(pool, Serial(pool, pool_step, 0, 2), t)
            pool.sem_inc(rstd_ready, 1)
            with pool.Fori(0, TT // 2) as j:
                for p in range(2):
                    i = 2 * j + p
                    pool.wait_ge(xn_ready, i + 1)
                    pool.tensor_copy(row(t.xn, i), xns[p][:, :]).then_inc(xn_copied, 1)

        @block.scalar
        def _(act):
            with act.Fori(0, TT // 2) as j:
                for p in range(2):
                    i = 2 * j + p
                    act.wait_ge(tp_ready, 2 + i + 1)
                    act.wait_ge(logit_ready, i + 1)
                    act.activation(xts[p][:, :], tp[p][:, :], ACT.Copy).then_inc(xts_ready, 1)
                    act.wait_ge(logit_ready, 2 + i + 1)
                    act.activation(logit[:, ds(i, 1), 0:E1].rearrange("p o e -> p (o e)"), lg[:, 0:E1], ACT.Copy).then_inc(logit_out, 1)
            act.wait_ge(exp_asked, 1)
            act.activation(expd[:, :, :], expd[:, :, :], ACT.Exp).then_inc(exp_ready, 1)
            act.wait_ge(mt_ready, 1)
            act.activation(mixt[:, :], mt[:, :], ACT.Copy).then_inc(mixt_ready, 1)

        @block.vector
        def _(dve):
            row_stats(dve, Serial(dve, dve_step, 0, ROW_STATS), t, stats6)
            dve.sem_inc(stats_ready, 1)
            dve.wait_ge(rstd_ready, 1)
            with dve.Fori(0, TT // 2) as j:
                for p in range(2):
                    i = 2 * j + p
                    dve.wait_ge(tp_ready, i + 1)
                    dve.wait_ge(xn_copied, i + 1)
                    dve.tensor_scalar(xns[p][:, :], row(t.x, i), t.mv_at(i, 0), t.rstd_at(i), ALU.subtract, ALU.mult).then_inc(xn_ready, 1)
            dve.wait_ge(logit_out, 1 + TT)
            dve.wait_ge(weights_in, 6 * 16)
            step = Serial(dve, dve_step, ROW_STATS, 4 + 2 * TT + TT + 3 + 16 + TT + 3 * K1)
            step(dve.tensor_tensor(logit[:, :, 0:E1], logit[:, :, 0:E1], router_b[:, :].unsqueeze(1).to_broadcast([P, TT, E1]), ALU.add))
            step(dve.memset(logit[:, :, E1:W], FMIN))
            for i in range(TT):
                step(dve.max(top[:, i, :], logit[:, i, :]))
            dve.tensor_tensor(expd[:, :, :], logit[:, :, 0:E1], over(top[:, :, 0]), ALU.subtract).then_inc(exp_asked, 1)
            step(dve.memset(top[:, :, K1:8], FMIN))
            for i in range(TT):
                step(dve.match_replace(taken[:, i, :], top[:, i, :], logit[:, i, :], MARK))
            step(dve.tensor_scalar(chosen[:, :, :], taken[:, :, 0:E1], MARK, None, ALU.is_equal))
            step(dve.memset(chosen_before[:, 0, :], 0.0))
            for i in range(1, TT + 1):
                ins = dve.tensor_tensor(chosen_before[:, i, :], chosen_before[:, i - 1, :], chosen[:, i - 1, :], ALU.add)
                if i == TT:
                    ins.then_inc(chosen_ready, 1)
                else:
                    step(ins)
            dve.wait_ge(exp_ready, 1)
            step(dve.tensor_tensor(expd[:, :, :], expd[:, :, :], chosen[:, :, :], ALU.mult))
            step(dve.reduce_sum(total[:, :], expd[:, :, :], axis=AX.X))
            step(dve.reciprocal(total[:, :], total[:, :]))
            dve.tensor_tensor(mix[:, :, :], expd[:, :, :], over(total[:, :]), ALU.mult).then_inc(mix_ready, 1)
            dve.wait_ge(counted, 1)
            step(dve.tensor_copy(slot_base[:, :], load))
            step(dve.tensor_tensor(started[:, :, :], slot_base[:, :].unsqueeze(2).to_broadcast([P, E1, MJ]), job_starts[:, :, :], ALU.is_gt))
            step(dve.reduce_sum(jobs_of[:, :], started[:, :, :], axis=AX.X))
            step(dve.tensor_tensor(jobs_up_to[:, :, :], jobs_of[:, :].unsqueeze(1).to_broadcast([P, E1, E1]), up_to[:, :, :], ALU.mult))
            step(dve.reduce_sum(job_end[:, :], jobs_up_to[:, :, :], axis=AX.X))
            step(dve.tensor_tensor(slot_base[:, :], job_end[:, :], jobs_of[:, :], ALU.subtract))
            step(dve.tensor_scalar(slot_base[:, :], slot_base[:, :], float(JC), 1.0, ALU.mult, ALU.add))
            step(dve.tensor_tensor(ended[:, :, :], job_end[:, :].unsqueeze(1).to_broadcast([P, NJ, E1]),
                                   job_number[:, :].unsqueeze(2).to_broadcast([P, NJ, E1]), ALU.is_le))
            step(dve.reduce_sum(job_counts[:, :], ended[:, :, :], axis=AX.X))
            step(dve.tensor_scalar(t.job_expert[:, :], job_counts[:, :], float(E1 - 1), None, ALU.min))
            step(dve.tensor_copy(t.jobs[:, 0:1], job_end[:, E1 - 1:E1]))
            step(dve.tensor_tensor(job_counts[:, :], job_end[:, E1 - 1:E1].to_broadcast([P, NJ]), job_number[:, :], ALU.is_gt))
            step(dve.reduce_sum(total[:, 0:2], job_counts[:, :].rearrange("p (j two) -> p two j", two=2), axis=AX.X))
            step(dve.tensor_copy(t.jobs[:, 1:3], total[:, 0:2]))
            step(dve.tensor_tensor(place[:, :, :], count, slot_base[:, :].unsqueeze(1).to_broadcast([P, TT, E1]), ALU.add))
            step(dve.tensor_tensor(place[:, :, :], place[:, :, :], chosen[:, :, :], ALU.mult))
            for i in range(TT):
                step(dve.max(t.addr[:, i, :], place[:, i, :]))
            dve.wait_ge(mix_ready, 1)
            dve.tensor_scalar(expd[:, :, :], mix[:, :, :], t.gates[:, 3:4], None, ALU.mult).then_inc(mix_ready, 1)
            dve.wait_ge(mix_ready, 2)
            for k in range(K1):
                slot = over(t.addr[:, :, k])
                step(dve.tensor_tensor(taken[:, :, 0:E1], place[:, :, :], slot, ALU.is_equal))
                step(dve.tensor_tensor(taken[:, :, 0:E1], taken[:, :, 0:E1], expd[:, :, :], ALU.mult))
                step(dve.reduce_sum(t.weight[:, :, k], taken[:, :, 0:E1], axis=AX.X))
            step.close()
            for i in range(TT):
                dve.wait_ge(bias_ready, i + 1)
                dve.scalar_tensor_tensor(out=t.x[:, i, :], in0=out[:, :], scalar=t.gates[:, 3:4], in1=t.x[:, i, :],
                                         op0=ALU.mult, op1=ALU.add).then_inc(x_added, 1)

        @block.tensor
        def _(pe):
            pe.sem_inc(tp_ready, 2)
            pe.sem_inc(logit_ready, 2)
            pe.sem_inc(logit_out, 1)
            pe.wait_ge(weights_in, 6 * 16)
            with pe.Fori(0, TT // 2) as j:
                for p in range(2):
                    i = 2 * j + p
                    pe.wait_ge(xn_ready, i + 1)
                    transposed_tile(pe, tp[p], xns[p], t).then_inc(tp_ready, 1)
                    pe.wait_ge(xts_ready, i + 1)
                    pe.wait_ge(logit_out, i + 1)
                    for c in range(DC):
                        mm = pe.matmul(lg[:, 0:E1], xts[p][:, c * P:(c + 1) * P], router_t[:, c, :], start=(c == 0), stop=(c == DC - 1))
                    mm.then_inc(logit_ready, 1)
            pe.wait_ge(logit_out, 1 + TT)
            pe.wait_ge(chosen_ready, 1)
            pe.matmul(count, t.before[:, :], chosen[:, :, :], start=True, stop=False)
            pe.matmul(count, t.ones[:, :], chosen_before[:, 0:TT, :], start=False, stop=True)
            pe.matmul(load, t.ones[:, :], chosen_before[:, TT, :], start=True, stop=True).then_inc(counted, 1)
            pe.wait_ge(mix_ready, 1)
            for i in range(TT):
                mm = pe.transpose(mt[:, i * P:(i + 1) * P], mix[:, i, :], t.ident[:, :])
            mm.then_inc(mt_ready, 1)
            pe.wait_ge(mixt_ready, 1)
            for i in range(TT):
                if i:
                    pe.wait_ge(x_added, i)
                pe.matmul(out[:, :], mixt[:, i * P:(i + 1) * P], down_b[:, :], start=True, stop=True).then_inc(bias_ready, 1)


def experts1(nc, t, d):
    NF = I1 // P
    with ExitStack() as ctx:
        ph = Phase(nc, ctx, "x_")
        addr_f = ph.sb("addr_f", [P, TT, 8])
        rows = [ph.sb(f"rows{p}", [P, D]) for p in range(2)]
        to = [ph.sb(f"to{p}", [P, 8], U32) for p in range(2)]
        wgu = [ph.sb(f"wgu{p}", [P, DC, 2, I1]) for p in range(2)]
        wd = [ph.sb(f"wd{p}", [P, NF, D]) for p in range(2)]
        bgu = ph.sb("bgu", [P, E1, 2 * NF])
        xs = [ph.sb(f"xs{p}", [P, JT, D]) for p in range(2)]
        xt = [ph.sb(f"xt{p}", [P, DC, JC]) for p in range(2)]
        gate = [ph.sb(f"gate{p}", [P, JC]) for p in range(2)]
        sig = [ph.sb(f"sig{p}", [P, JC]) for p in range(2)]
        up0 = [ph.sb(f"up0{p}", [P, JC]) for p in range(2)]
        up1 = [ph.sb(f"up1{p}", [P, JC]) for p in range(2)]
        h = [ph.sb(f"h{p}", [P, NF, JC]) for p in range(2)]
        eo = [ph.sb(f"eo{p}", [P, JT, D]) for p in range(2)]
        tp = [ph.ps(f"tp{p}", [P, D]) for p in range(2)]
        pg = [ph.ps(f"pg{p}", [P, D]) for p in range(2)]
        pu = [ph.ps(f"pu{p}", [P, D]) for p in range(2)]
        po = [ph.ps(f"po{p}", [P, D]) for p in range(2)]
        weights_in = [ph.sem(f"weights_in{p}") for p in range(2)]
        scattered = [ph.sem(f"scattered{p}") for p in range(2)]
        xs_in = [ph.sem(f"xs_in{p}") for p in range(2)]
        stored = [ph.sem(f"stored{p}") for p in range(2)]
        addr_ready, staged, tiles_staged, all_scattered, all_stored, bias_in, tp_ready, xt_ready, gate_done, up_done = ph.sems(
            "addr_ready staged tiles_staged all_scattered all_stored bias_in tp_ready xt_ready gate_done up_done")
        gate_ready, up0_ready, sig_ready, up1_ready, glu_ready, h_ready, out_done, eo_ready, up_seen = ph.sems(
            "gate_ready up0_ready sig_ready up1_ready glu_ready h_ready out_done eo_ready up_seen")
        block = ctx.enter_context(nc.Block())

        def job_count(eng):
            return eng.value_load(t.jobs[0:1, 0:1], min_val=FJ, max_val=NJ)

        def expert_of(eng, job):
            return eng.value_load(t.job_expert[0:1, ds(job, 1)], min_val=0, max_val=E1 - 1)

        def slots_of(job):
            return d["slots"][ds(job * JC, JC), :].rearrange("(s p) d -> p s d", p=P)

        @block.sync
        def _(sp):
            sp.dma_start(bgu[:, :, :], d["gate_up_b"]).then_inc(bias_in, 16)

            def load_weights(e, p):
                sp.dma_start(wgu[p][:, :, :, :], d["gate_up"][ds(e, 1), :, :, :, :].rearrange("o p c g f -> (o p) c g f")).then_inc(weights_in[p], 16)
                sp.dma_start(wd[p][:, :, :], d["down"][ds(e, 1), :, :].rearrange("o (k p) d -> p (o k) d", p=P)).then_inc(weights_in[p], 16)

            for p in range(2):
                load_weights(expert_of(sp, p), p)
            sp.wait_ge(all_scattered, 1)
            for p in range(2):
                sp.dma_start(xs[p][:, :, :], slots_of(p)).then_inc(xs_in[p], 16)
            n = job_count(sp)
            with sp.Fori(1, NJ // 2) as j:
                for p in range(2):
                    job = 2 * j + p
                    with sp.If(n > job):
                        e = expert_of(sp, job)
                        sp.wait_ge(tp_ready, JT * (job - 1))
                        sp.dma_start(xs[p][:, :, :], slots_of(job)).then_inc(xs_in[p], 16)
                        sp.wait_ge(out_done, JT * (job - 1))
                        load_weights(e, p)

        @block.gpsimd
        def _(pool):
            pool.tensor_scalar(addr_f[:, :, :], t.addr[:, :, :], -1.0, None, ALU.add).then_inc(addr_ready, 1)
            pool.wait_ge(addr_ready, 1)
            scatter_rows(pool, t, d, K1, addr_f, rows, to, staged, tiles_staged, scattered)
            pool.sem_inc(all_scattered, 1)
            n = job_count(pool)
            pool.sem_inc(h_ready, 2)
            with pool.Fori(0, NJ // 2) as j:
                for p in range(2):
                    job = 2 * j + p
                    with pool.If(n > job):
                        for k in range(NF):
                            u = NF * job + k
                            pool.wait_ge(up0_ready, u + 1)
                            pool.wait_ge(h_ready, u + 1)
                            pool.sem_inc(up_seen, 1)
                            pool.tensor_scalar(up1[k % 2][:, :], up0[k % 2][:, :], -LIMIT, 1.0, ALU.max, ALU.add).then_inc(up1_ready, 1)

        @block.scalar
        def _(act):
            n = job_count(act)

            def copy_rows(job, p):
                for s in range(JT):
                    act.wait_ge(tp_ready, JT * job + s + 1)
                    act.activation(xt[p][:, :, s * P:(s + 1) * P], tp[(JT * p + s) % 2][:, :].rearrange("p (c s) -> p c s", c=DC),
                                   ACT.Copy).then_inc(xt_ready, 1)

            act.sem_inc(glu_ready, 2)
            copy_rows(0, 0)
            with act.Fori(0, NJ // 2) as j:
                for p in range(2):
                    job = 2 * j + p
                    with act.If(n > job):
                        for k in range(NF):
                            u = NF * job + k
                            act.wait_ge(gate_ready, u + 1)
                            act.wait_ge(glu_ready, u + 1)
                            act.activation(sig[k % 2][:, :], gate[k % 2][:, :], ACT.Sigmoid, scale=ALPHA).then_inc(sig_ready, 1)
                    with act.If(n > job + 1):
                        copy_rows(job + 1, 1 - p)
                    with act.If(n > job):
                        act.wait_ge(eo_ready, 2 + JT * (job + 1))
                        act.dma_start(slots_of(job), eo[p][:, :, :]).then_inc(stored[p], 16)
            mine = [act.value_load(t.jobs[0:1, 1 + p:2 + p], min_val=FJ // 2, max_val=NJ // 2) for p in range(2)]
            for p in range(2):
                act.wait_ge(stored[p], 16 * mine[p])
                act.sem_inc(all_stored, 1)

        @block.vector
        def _(dve):
            dve.sem_inc(eo_ready, 2)
            dve.wait_ge(bias_in, 16)
            n = job_count(dve)

            def one_job(job, j, p):
                e = expert_of(dve, job)

                def clamp(k):
                    for psum, dst, half, done, ready in ((pg, gate, 0, gate_done, gate_ready), (pu, up0, 1, up_done, up0_ready)):
                        bias = bgu[:, ds(e, 1), half * NF + k:half * NF + k + 1].rearrange("p o k -> p (o k)")
                        dve.wait_ge(done, NF * job + k + 1)
                        dve.tensor_scalar(dst[k % 2][:, :], psum[k % 2][:, 0:JC], bias, LIMIT, ALU.add, ALU.min).then_inc(ready, 1)

                def glu(k):
                    u = NF * job + k
                    dve.wait_ge(sig_ready, u + 1)
                    dve.tensor_tensor(gate[k % 2][:, :], gate[k % 2][:, :], sig[k % 2][:, :], ALU.mult).then_inc(glu_ready, 1)
                    dve.wait_ge(glu_ready, 2 + u + 1)
                    dve.wait_ge(up1_ready, u + 1)
                    dve.tensor_tensor(h[p][:, k, :], gate[k % 2][:, :], up1[k % 2][:, :], ALU.mult).then_inc(h_ready, 1)
                    dve.wait_ge(h_ready, 2 + u + 1)

                for k in range(NF):
                    clamp(k)
                    if k:
                        glu(k - 1)
                glu(NF - 1)
                if j is not None:
                    dve.wait_ge(stored[p], 16 * j)
                for s in range(JT):
                    dve.wait_ge(out_done, JT * job + s + 1)
                    dve.tensor_copy(eo[p][:, s, :], po[(JT * p + s) % 2][:, :]).then_inc(eo_ready, 1)

            for p in range(2):
                one_job(p, None, p)
            with dve.Fori(1, NJ // 2) as j:
                for p in range(2):
                    with dve.If(n > 2 * j + p):
                        one_job(2 * j + p, j, p)

        @block.tensor
        def _(pe):
            pe.sem_inc(xt_ready, 2)
            n = job_count(pe)

            def transposes(j, job, p):
                pe.wait_ge(xs_in[p], 16 * (j + 1))
                for s in range(JT):
                    pe.wait_ge(xt_ready, JT * job + s + 1)
                    transposed_tile(pe, tp[(JT * p + s) % 2], xs[p][:, s, :], t).then_inc(tp_ready, 1)

            def up(j, job, p):
                pe.wait_ge(weights_in[p], 32 * (j + 1))
                pe.wait_ge(xt_ready, 2 + JT * (job + 1))
                for k in range(NF):
                    pe.wait_ge(h_ready, NF * job + k + 1)
                    for half, psum, done in ((0, pg, gate_done), (1, pu, up_done)):
                        for c in range(DC):
                            mm = pe.matmul(psum[k % 2][:, 0:JC], wgu[p][:, c, half, k * P:(k + 1) * P], xt[p][:, c, :], start=(c == 0), stop=(c == DC - 1))
                        mm.then_inc(done, 1)

            def down(job, p):
                pe.wait_ge(h_ready, 2 + NF * (job + 1))
                for s in range(JT):
                    pe.wait_ge(eo_ready, JT * job + s + 1)
                    for k in range(NF):
                        mm = pe.matmul(po[(JT * p + s) % 2][:, :], h[p][:, k, s * P:(s + 1) * P], wd[p][:, k, :], start=(k == 0), stop=(k == NF - 1))
                    mm.then_inc(out_done, 1)

            transposes(0, 0, 0)
            with pe.Fori(0, NJ // 2) as j:
                for p in range(2):
                    job = 2 * j + p
                    with pe.If(n > job):
                        up(j, job, p)
                    with pe.If(n > job + 1):
                        transposes(j + p, job + 1, 1 - p)
                    with pe.If(n > job):
                        down(job, p)


def store_x(nc, t, d):
    with ExitStack() as ctx:
        ph = Phase(nc, ctx, "o_")
        stored, = ph.sems("stored")
        block = ctx.enter_context(nc.Block())

        @block.sync
        def _(sp):
            sp.dma_start(d["out"].rearrange("b (t p) d -> p (b t) d", p=P), t.x[:, :, :]).then_inc(stored, 16)
            sp.wait_ge(stored, 16)


def build(nc, d, stop=9):
    d["slots"] = nc.dram_tensor("expert_slots", (SLOTS, D), F32, kind="Internal").ap()
    with ExitStack() as ctx:
        ph = Phase(nc, ctx, "g_")
        t = Shared()
        t.x = ph.sb("x", [P, TT, D])
        t.mv = ph.sb("mv", [P, TT, 2])
        t.vareps = ph.sb("vareps", [P, TT])
        t.rstd = ph.sb("rstd", [P, TT])
        t.minus_half = ph.sb("minus_half", [P, TT])
        t.gates = ph.sb("gates", [P, 4])
        t.ident = ph.sb("ident", [P, P])
        t.before = ph.sb("before", [P, P])
        t.ones = ph.sb("ones", [P, P])
        t.mv_at = lambda i, k: t.mv[:, ds(i, 1), k:k + 1].rearrange("p o d -> p (o d)")
        t.rstd_at = lambda i: t.rstd[:, ds(i, 1)]
        load_constants(nc, t, d)
        layer0(nc, t, d, stop)
        if stop >= 3:
            layer1_attention(nc, t, d)
        if stop >= 4:
            moe1(nc, t, d)
        store_x(nc, t, d)


_STOP = 4


def kernel(**inputs):
    import numpy as np
    import concourse.bacc as _bacc
    from concourse.bass_utils import run_bass_kernel_spmd as _run

    a = {k: np.ascontiguousarray(v) for k, v in inputs.items()}

    def chunked(w):
        e, f, dm = w.shape
        return np.ascontiguousarray(w.reshape(e, f, dm // 128, 128).transpose(0, 3, 2, 1))

    wo = np.zeros((128, NH // 4, D), np.float32)
    for h in range(NH):
        wo[32 * (h % 4):32 * (h % 4) + HD, h // 4, :] = a["L1_xattn_Wo"][HD * h:HD * (h + 1), :]
    inv = 1.0 / 10000.0 ** (np.arange(0, HD, 2, dtype=np.float32) / HD)
    angle = np.outer(np.arange(S, dtype=np.float32), inv)
    angle = np.concatenate([angle, angle], -1)
    sign = np.where(np.arange(HD) < HD // 2, -1.0, 1.0).astype(np.float32)
    cos, sin = (np.tile(x.astype(np.float32).T, (128 // HD, 1)) for x in (np.cos(angle), np.sin(angle) * sign))
    rope = np.stack([cos, sin], 1)
    rep = np.zeros((128, 2, 2, 4, 128), np.float32)
    for a1 in range(4):
        for a0 in range(2):
            for j in range(4):
                for r in range(HD):
                    rep[HD * (2 * a1 + a0) + r, 0, j % 2, a1, 64 * a0 + HD * j + r] = HD ** -0.5
                    rep[HD * (2 * a1 + a0) + r, 1, j // 2, a1, 64 * a0 + HD * j + r] = 1
    head_gate = np.zeros((128, NH // 2, 4), np.float32)
    head_gate[:, :, 2:4] = a["L1_xattn_gate"].reshape(NH // 2, 2)

    arrays = {
        "x": a["x"],
        "ctx": a["ctx_2048"],
        "ctx_t": np.ascontiguousarray(a["ctx_2048"].transpose(0, 2, 1)),
        "gates": np.ascontiguousarray(np.broadcast_to(np.concatenate([a["g_xattn"][0:1], a["g_ffn"][0:1], a["g_xattn"][1:2], a["g_ffn"][1:2]]), (128, 4))),
        "ident": np.eye(128, dtype=np.float32),
        "gate_wt": np.ascontiguousarray(a["L0_ffn_gate_w"].T),
        "slot_base": np.broadcast_to(np.arange(64, dtype=np.float32) * CAP + 1, (128, 64)).copy(),
        "sh_gate": np.ascontiguousarray(a["L0_ffn_sh_gate"].T),
        "sh_up": np.ascontiguousarray(a["L0_ffn_sh_up"].T),
        "sh_down": np.ascontiguousarray(a["L0_ffn_sh_down"].T),
        "w_gate": chunked(a["L0_ffn_w_gate"]),
        "w_up": chunked(a["L0_ffn_w_up"]),
        "w_down": np.ascontiguousarray(a["L0_ffn_w_down"].transpose(0, 2, 1)),
        "mask": a["mask_Bx1xSxS_fk0"].reshape(B, S, S),
        "wq": a["L1_xattn_Wq"], "wk": a["L1_xattn_Wk"], "wv": a["L1_xattn_Wv"],
        "wo": wo, "rope": rope, "rep": rep.reshape(128, -1), "head_gate": head_gate,
        "router_t": np.ascontiguousarray(a["L1_ffn_router_weight"].T),
        "router_b": np.broadcast_to(a["L1_ffn_router_bias"], (128, E1)).copy(),
        "gate_up": np.ascontiguousarray(a["L1_ffn_gate_up_proj"].reshape(E1, DC, 128, I1, 2).transpose(0, 2, 1, 4, 3)),
        "gate_up_b": np.ascontiguousarray(a["L1_ffn_gate_up_proj_bias"].reshape(E1, I1 // 128, 128, 2).transpose(2, 0, 3, 1)).reshape(128, E1, 2 * I1 // 128),
        "down": a["L1_ffn_down_proj"],
        "down_b": a["L1_ffn_down_proj_bias"],
        "job_starts": np.broadcast_to(np.arange(MJ, dtype=np.float32) * JC, (128, E1, MJ)).copy(),
        "up_to": np.broadcast_to(np.tril(np.ones((E1, E1), np.float32)), (128, E1, E1)).copy(),
        "job_number": np.broadcast_to(np.arange(NJ, dtype=np.float32), (128, NJ)).copy(),
        "before": np.triu(np.ones((128, 128), np.float32), 1),
    }
    nc = _bacc.Bacc("TRN2", target_bir_lowering=False, num_devices=1)
    d = {n: nc.dram_tensor("in_" + n, v.shape, mybir.dt.from_np(v.dtype), kind="ExternalInput").ap() for n, v in arrays.items()}
    d["out"] = nc.dram_tensor("out_0", a["x"].shape, F32, kind="ExternalOutput").ap()
    build(nc, d, _STOP)
    r = _run(nc, [{"in_" + n: v for n, v in arrays.items()}], core_ids=[0])
    return r.results[0]["out_0"]
```

```python
import concourse.bass as bass
from concourse import mybir
from contextlib import ExitStack

F32 = mybir.dt.float32
U32 = mybir.dt.uint32
F32R = mybir.dt.float32r
ALU = mybir.AluOpType
ACT = mybir.ActivationFunctionType
AX = mybir.AxisListType
ds = bass.ds

P = 128
B, S, D = 8, 256, 512
T = B * S
TT = T // P
ST = S // P
DC = D // P
EPS = 1e-5

E0, K0, F0 = 64, 6, 352
CAP = 2 * ((T * K0 + E0 - 1) // E0)
CT = CAP // P
SLOTS = E0 * CAP
WIDTHS = (CAP, 2 * P, 2 * P - 32, 2 * P - 64)
ZROWS = 4
ZN = SLOTS // (P * ZROWS)
ZA = 2 * B
FT0 = [(f, min(P, F0 - f)) for f in range(0, F0, P)]
FS = 704
FTS = [(0, P), (P, P), (2 * P, P), (3 * P, P), (4 * P, 96), (4 * P + 96, 96)]
NTOK = 512

NH, HD = 32, 16
E1, I1, K1 = 8, 512, 2
JT = 3
JC = JT * P
NJ = 2 * (((T * K1 - E1) // JC + E1 + 1) // 2)
FJ = (T * K1 // JC) - 1
MJ = (T + JC - 1) // JC
LIMIT, ALPHA = 7.0, 1.702
FMIN = -3.4028234663852886e38
MARK = 3.0e38


class Serial:

    def __init__(self, eng, sem, base, steps):
        self.eng, self.sem, self.base, self.steps, self.n = eng, sem, base, steps, 0

    def __call__(self, ins):
        self.n += 1
        ins.then_inc(self.sem, 1)
        self.eng.wait_ge(self.sem, self.base + self.n)

    def later(self, ins):
        self.n += 1
        ins.then_inc(self.sem, 1)

    def all(self):
        self.eng.wait_ge(self.sem, self.base + self.n)

    def close(self):
        assert self.n == self.steps, self.n


class Phase:

    def __init__(self, nc, ctx, prefix):
        self.nc, self.ctx, self.prefix, self.held = nc, ctx, prefix, []
        ctx.callback(self.clear)

    def sb(self, name, shape, dt=F32):
        return self.ctx.enter_context(self.nc.sbuf_tensor(self.prefix + name, shape, dt))

    def ps(self, name, shape):
        return self.ctx.enter_context(self.nc.psum_tensor(self.prefix + name, shape, F32))

    def sem(self, name):
        sem = self.nc.alloc_semaphore(name=self.prefix + name)
        self.held.append(sem)
        return sem

    def sems(self, names):
        return [self.sem(n) for n in names.split()]

    def clear(self):
        if not self.held:
            return
        self.nc.clear_and_free_semaphores(self.held)
        self.nc.all_engine_barrier()


def row(x, i):
    return x[:, ds(i, 1), :].rearrange("p o d -> p (o d)")


def row_stats(dve, step, t, stats6):
    for i in range(TT):
        step.later(dve.bn_stats(stats6[:, i, :], t.x[:, i, :]))
    step.all()
    for i in range(TT):
        step.later(dve.bn_aggr(t.mv[:, i, :], stats6[:, i, :]))
    step.all()


ROW_STATS = 2 * TT


def row_rstd(pool, step, t):
    step(pool.tensor_scalar(t.vareps[:, :], t.mv[:, :, 1], EPS, None, ALU.add))
    step(pool.tensor_tensor(t.rstd[:, :], t.vareps[:, :], t.minus_half[:, :], ALU.pow))


class Shared:
    pass


def load_constants(nc, t, d):
    with ExitStack() as ctx:
        ph = Phase(nc, ctx, "i_")
        raw = ph.sb("raw", [P, 4])
        const_in, = ph.sems("const_in")
        block = ctx.enter_context(nc.Block())

        @block.sync
        def _(sp):
            sp.dma_start(t.ident[:, :], d["ident"]).then_inc(const_in, 16)
            sp.dma_start(t.before[:, :], d["before"]).then_inc(const_in, 16)
            sp.dma_start(raw[:, :], d["gates"]).then_inc(const_in, 16)
            sp.dma_start(t.x[:, :, :], d["x"].rearrange("b (t p) d -> p (b t) d", p=P)).then_inc(const_in, 16)
            sp.wait_ge(const_in, 64)

        @block.vector
        def _(dve):
            dve.memset(t.ones[:, :], 1.0)
            dve.memset(t.minus_half[:, :], -0.5)

        @block.scalar
        def _(act):
            act.wait_ge(const_in, 64)
            act.activation(t.gates[:, :], raw[:, :], ACT.Tanh)


def zero_slots(eng, t, d, n):
    slots = d["slots"].rearrange("(n p r) d -> n p (r d)", p=P, r=ZROWS)
    eng.dma_start(slots[ds(n, 1), :, :].rearrange("o p f -> (o p) f"), t.zero[:, :]).then_inc(t.zeroed, 16)


def layer0_attention(nc, t, d):
    scale = D ** -0.5
    with ExitStack() as ctx:
        ph = Phase(nc, ctx, "a_")
        cn = [ph.sb(f"cn{p}", [P, ST, D]) for p in range(2)]
        ct = [ph.sb(f"ct{p}", [P, DC, S]) for p in range(2)]
        cts = [ph.sb(f"cts{p}", [P, DC, S]) for p in range(2)]
        q = [ph.sb(f"q{p}", [P, ST, D]) for p in range(2)]
        prob = [ph.sb(f"prob{p}", [P, DC, D]) for p in range(2)]
        stats6 = ph.sb("stats6", [P, TT, 6])
        nmax = ph.sb("nmax", [P, DC])
        nb = [ph.sb(f"nb{p}", [P, DC]) for p in range(2)]
        ssum = [ph.sb(f"ssum{p}", [P, DC]) for p in range(2)]
        rsum = ph.sb("rsum", [P, DC])
        score = [ph.ps(f"score{e}", [P, D]) for e in range(DC)]
        out = [ph.ps(f"out{s}", [P, D]) for s in range(ST)]
        ctx_in = [ph.sem(f"ctx_in{p}") for p in range(2)]
        stats_ready, rstd_ready, q_ready, score_ready, bias_ready, prob_ready = ph.sems(
            "stats_ready rstd_ready q_ready score_ready bias_ready prob_ready")
        ctx_scaled, out_ready, x_added, batch_done, dve_step, pool_step, zero_ready = ph.sems(
            "ctx_scaled out_ready x_added batch_done dve_step pool_step zero_ready")
        block = ctx.enter_context(nc.Block())

        @block.sync
        def _(sp):
            with sp.Fori(0, B // 2) as j:
                for p in range(2):
                    b = 2 * j + p
                    sp.wait_ge(batch_done, b + 1)
                    sp.dma_start(cn[p][:, :, :], d["ctx"][ds(b, 1), :, :].rearrange("o (t p) d -> p (o t) d", p=P)).then_inc(ctx_in[p], 16)
                    sp.dma_start(ct[p][:, :, :], d["ctx_t"][ds(b, 1), :, :].rearrange("o (c p) s -> p (o c) s", p=P)).then_inc(ctx_in[p], 16)

        @block.gpsimd
        def _(pool):
            pool.sem_inc(batch_done, 2)
            pool.memset(t.zero[:, :], 0.0).then_inc(zero_ready, 1)
            pool.wait_ge(stats_ready, 1)
            row_rstd(pool, Serial(pool, pool_step, 0, 2), t)
            pool.sem_inc(rstd_ready, 1)

        @block.vector
        def _(dve):
            row_stats(dve, Serial(dve, dve_step, 0, ROW_STATS), t, stats6)
            dve.sem_inc(stats_ready, 1)
            dve.wait_ge(rstd_ready, 1)
            steps = 2 * DC

            def normalise(b, p):
                for s in range(ST):
                    dve.tensor_scalar(q[p][:, s, :], row(t.x, ST * b + s), t.mv_at(ST * b + s, 0), t.rstd_at(ST * b + s),
                                      ALU.subtract, ALU.mult).then_inc(q_ready, 1)

            def batch(j, p, last=False):
                b = 2 * j + p
                step = Serial(dve, dve_step, ROW_STATS + b * steps, steps)
                dve.wait_ge(batch_done, b + 1)
                dve.wait_ge(ctx_in[p], 32 * (j + 1))
                for e in range(DC):
                    dve.wait_ge(score_ready, DC * b + e + 1)
                    step(dve.reduce_max(nmax[:, e:e + 1], score[e][:, :], axis=AX.X))
                    dve.tensor_scalar(nb[p][:, e:e + 1], nmax[:, e:e + 1], -scale, None, ALU.mult).then_inc(bias_ready, 1)
                for e in range(DC):
                    dve.wait_ge(prob_ready, DC * b + e + 1)
                    step(dve.reciprocal(rsum[:, e:e + 1], ssum[p][:, e:e + 1]))
                    dve.tensor_scalar(cts[p][:, e, :], ct[p][:, e, :], rsum[:, e:e + 1], None, ALU.mult).then_inc(ctx_scaled, 1)
                if not last:
                    normalise(b + 1, 1 - p)
                for s in range(ST):
                    dve.wait_ge(out_ready, ST * b + s + 1)
                    xs = row(t.x, ST * b + s)
                    dve.scalar_tensor_tensor(out=xs, in0=out[s][:, :], scalar=t.gates[:, 0:1], in1=xs,
                                             op0=ALU.mult, op1=ALU.add).then_inc(x_added, 1)
                dve.sem_inc(batch_done, 1)
                step.close()

            normalise(0, 0)
            with dve.Fori(0, B // 2 - 1) as j:
                for p in range(2):
                    batch(j, p)
            batch(B // 2 - 1, 0)
            batch(B // 2 - 1, 1, last=True)

        @block.scalar
        def _(act):
            act.wait_ge(zero_ready, 1)
            with act.Fori(0, B // 2) as j:
                for p in range(2):
                    b = 2 * j + p
                    act.wait_ge(ctx_in[p], 32 * (j + 1))
                    for k in range(ZA // B):
                        zero_slots(act, t, d, ZA // B * b + k)
                    act.wait_ge(batch_done, b + 1)
                    for e in range(DC):
                        act.wait_ge(bias_ready, DC * b + e + 1)
                        act.activation(prob[p][:, e, :], score[e][:, :], ACT.Exp, bias=nb[p][:, e:e + 1], scale=scale,
                                       accum_out=ssum[p][:, e:e + 1]).then_inc(prob_ready, 1)

        @block.tensor
        def _(pe):
            pe.sem_inc(x_added, ST)
            with pe.Fori(0, B // 2) as j:
                for p in range(2):
                    b = 2 * j + p
                    pe.wait_ge(ctx_in[p], 32 * (j + 1))
                    pe.wait_ge(q_ready, ST * b + ST)
                    for e in range(DC):
                        for s in range(ST):
                            mm = pe.matmul(score[e][:, :], cn[p][:, s, e * P:(e + 1) * P], q[p][:, s, :], start=(s == 0), stop=(s == ST - 1))
                        mm.then_inc(score_ready, 1)
                    for s in range(ST):
                        pe.wait_ge(x_added, ST * b + s + 1)
                        for e in range(DC):
                            if s == 0:
                                pe.wait_ge(ctx_scaled, DC * b + e + 1)
                            mm = pe.matmul(out[s][:, :], cts[p][:, e, s * P:(s + 1) * P], prob[p][:, e, :], start=(e == 0), stop=(e == DC - 1))
                        mm.then_inc(out_ready, 1)


def transposed_tile(pe, psum, src, t):
    for c in range(DC):
        mm = pe.transpose(psum[:, c * P:(c + 1) * P], src[:, c * P:(c + 1) * P], t.ident[:, :])
    return mm


def scatter_rows(pool, t, d, choices, addr_f, rows, to, staged, tiles_staged, scattered):
    def scatter(j, p):
        i = 2 * j + p
        pool.tensor_copy(rows[p][:, :], row(t.xn, i)).then_inc(staged, 1)
        pool.tensor_copy(to[p][:, :], row(addr_f, i)).then_inc(staged, 1)
        pool.wait_ge(staged, 2 * i + 2)
        pool.sem_inc(tiles_staged, 1)
        for k in range(choices):
            pool.indirect_dma_start(out=d["slots"], out_offset=bass.IndirectOffsetOnAxis(ap=to[p][:, k:k + 1], axis=0),
                                    in_=rows[p][:, :], in_offset=None, bounds_check=SLOTS - 1, oob_is_err=False).then_inc(scattered[p], 16)

    for p in range(2):
        scatter(0, p)
    with pool.Fori(1, TT // 2) as j:
        for p in range(2):
            pool.wait_ge(scattered[p], 16 * choices * j)
            scatter(j, p)
    for p in range(2):
        pool.wait_ge(scattered[p], 16 * choices * (TT // 2))


def route_and_share(nc, t, d):
    W = E0 + 2
    NF = len(FTS)
    NS = NTOK // P
    with ExitStack() as ctx:
        ph = Phase(nc, ctx, "r_")
        t.xn = ph.sb("xn", [P, TT, D])
        t.xt = ph.sb("xt", [P, DC, T])
        stats6 = ph.sb("stats6", [P, TT, 6])
        gate_wt = ph.sb("gate_wt", [P, DC, E0])
        slot_base = ph.sb("slot_base", [P, E0])
        xns = [ph.sb(f"xns{p}", [P, D]) for p in range(2)]
        xts = [ph.sb(f"xts{p}", [P, D]) for p in range(2)]
        logit = ph.sb("logit", [P, TT, E0])
        score = ph.sb("score", [P, TT, W])
        taken = ph.sb("taken", [P, TT, W])
        chosen = ph.sb("chosen", [P, TT, E0])
        chosen_before = ph.sb("chosen_before", [P, TT + 1, E0])
        wsel = ph.sb("wsel", [P, TT, E0])
        place = ph.sb("place", [P, TT, E0])
        top = ph.sb("top", [P, TT, 8])
        small = ph.sb("small", [P, TT])
        big = ph.sb("big", [P, TT, 8])
        addr_f = ph.sb("addr_f", [P, TT, 8])
        rows = xns
        to = [ph.sb(f"to{p}", [P, 8], U32) for p in range(2)]
        wg = ph.sb("wg", [P, DC, FS])
        wu = ph.sb("wu", [P, DC, FS])
        wd = ph.sb("wd", [P, NF, D])
        sg = [ph.sb(f"sg{p}", [P, NTOK]) for p in range(2)]
        h = ph.sb("h", [P, NF, NTOK])
        pg = [ph.ps(f"pg{p}", [P, NTOK]) for p in range(2)]
        pu = [ph.ps(f"pu{p}", [P, NTOK]) for p in range(2)]
        po = [ph.ps(f"po{p}", [P, D]) for p in range(2)]
        count = ph.ps("count", [P, TT, E0])
        tp, lg = pg, pu
        load = count[:, 0, :]
        router_in, weights_in, stats_ready, rstd_ready, xn_ready, xn_copied, tp_ready, xts_ready, xt_ready, logit_ready, logit_out = ph.sems(
            "router_in weights_in stats_ready rstd_ready xn_ready xn_copied tp_ready xts_ready xt_ready logit_ready logit_out")
        exp_asked, exp_ready, chosen_ready, counted, placed, loads_ready, routed, dve_step, pool_step = ph.sems(
            "exp_asked exp_ready chosen_ready counted placed loads_ready routed dve_step pool_step")
        addr_ready, staged, tiles_staged, gate_done, up_done, silu_ready, h_ready, out_done, x_added = ph.sems(
            "addr_ready staged tiles_staged gate_done up_done silu_ready h_ready out_done x_added")
        scattered = [ph.sem(f"scattered{p}") for p in range(2)]
        block = ctx.enter_context(nc.Block())

        def over(x):
            return x[:, :].unsqueeze(2).to_broadcast([P, TT, E0])

        @block.sync
        def _(sp):
            sp.dma_start(gate_wt[:, :, :], d["gate_wt"].rearrange("(c p) e -> p c e", p=P)).then_inc(router_in, 16)
            sp.dma_start(slot_base[:, :], d["slot_base"]).then_inc(router_in, 16)
            sp.dma_start(wg[:, :, :], d["sh_gate"].rearrange("(c p) f -> p c f", p=P)).then_inc(weights_in, 16)
            sp.dma_start(wu[:, :, :], d["sh_up"].rearrange("(c p) f -> p c f", p=P)).then_inc(weights_in, 16)
            for k, (f, n) in enumerate(FTS):
                sp.dma_start(wd[0:n, k, :], d["sh_down"][f:f + n, :]).then_inc(weights_in, 16)
            with sp.Fori(ZA, ZN) as n:
                zero_slots(sp, t, d, n)

        @block.gpsimd
        def _(pool):
            pool.sem_inc(xn_copied, 2)
            pool.sem_inc(xt_ready, 2)
            pool.wait_ge(stats_ready, 1)
            row_rstd(pool, Serial(pool, pool_step, 0, 2), t)
            pool.sem_inc(rstd_ready, 1)
            with pool.Fori(0, TT // 2) as j:
                for p in range(2):
                    i = 2 * j + p
                    pool.wait_ge(xn_ready, i + 1)
                    pool.tensor_copy(row(t.xn, i), xns[p][:, :]).then_inc(xn_copied, 1)
                    pool.wait_ge(xts_ready, i + 1)
                    pool.tensor_copy(t.xt[:, :, ds(i * P, P)], xts[p][:, :].rearrange("p (c s) -> p c s", c=DC)).then_inc(xt_ready, 1)
            pool.wait_ge(routed, 1)
            pool.tensor_scalar(big[:, :, :], t.addr[:, :, :], 0.0, float(2 * SLOTS), ALU.is_equal, ALU.mult).then_inc(addr_ready, 1)
            pool.wait_ge(addr_ready, 1)
            pool.tensor_tensor(big[:, :, :], big[:, :, :], t.addr[:, :, :], ALU.add).then_inc(addr_ready, 1)
            pool.wait_ge(addr_ready, 2)
            pool.tensor_scalar(addr_f[:, :, :], big[:, :, :], -1.0, None, ALU.add).then_inc(addr_ready, 1)
            pool.wait_ge(addr_ready, 3)
            pool.wait_ge(t.zeroed, 16 * ZN)
            scatter_rows(pool, t, d, K0, addr_f, rows, to, staged, tiles_staged, scattered)

        @block.scalar
        def _(act):
            def copy_tile(i, p):
                act.wait_ge(tp_ready, 2 + i + 1)
                act.wait_ge(xt_ready, i + 1)
                act.wait_ge(logit_ready, i + 1)
                act.activation(xts[p][:, :], tp[p][:, :], ACT.Copy).then_inc(xts_ready, 1)

            def copy_logits(i, p):
                act.wait_ge(logit_ready, 2 + i + 1)
                act.activation(row(logit, i), lg[p][:, 0:E0], ACT.Copy).then_inc(logit_out, 1)

            copy_tile(0, 0)
            with act.Fori(0, TT // 2 - 1) as j:
                for p in range(2):
                    copy_tile(2 * j + p + 1, 1 - p)
                    copy_logits(2 * j + p, p)
            copy_tile(TT - 1, 1)
            copy_logits(TT - 2, 0)
            copy_logits(TT - 1, 1)
            act.wait_ge(exp_asked, 1)
            act.activation(logit[:, :, :], logit[:, :, :], ACT.Exp).then_inc(exp_ready, 1)
            with act.Fori(0, T // NTOK) as n:
                for k, (f, m) in enumerate(FTS):
                    u = n * NF + k
                    act.wait_ge(gate_done, u + 1)
                    act.wait_ge(h_ready, u + 1)
                    act.activation(sg[k % 2][0:m, :], pg[k % 2][0:m, :], ACT.Silu).then_inc(silu_ready, 1)

        @block.vector
        def _(dve):
            row_stats(dve, Serial(dve, dve_step, 0, ROW_STATS), t, stats6)
            dve.sem_inc(stats_ready, 1)
            dve.wait_ge(rstd_ready, 1)
            with dve.Fori(0, TT // 2) as j:
                for p in range(2):
                    i = 2 * j + p
                    dve.wait_ge(tp_ready, i + 1)
                    dve.wait_ge(xn_copied, i + 1)
                    dve.tensor_scalar(xns[p][:, :], row(t.x, i), t.mv_at(i, 0), t.rstd_at(i), ALU.subtract, ALU.mult).then_inc(xn_ready, 1)
            dve.sem_inc(h_ready, 2)
            dve.sem_inc(x_added, 2)

            def hidden(n, k):
                f, m = FTS[k]
                u = n * NF + k
                dve.wait_ge(up_done, u + 1)
                dve.wait_ge(silu_ready, u + 1)
                dve.tensor_tensor(h[0:m, k, :], sg[k % 2][0:m, :], pu[k % 2][0:m, :], ALU.mult).then_inc(h_ready, 1)

            def add(n, s):
                dve.wait_ge(out_done, n * NS + s + 1)
                xs = row(t.x, n * NS + s)
                dve.scalar_tensor_tensor(out=xs, in0=po[s % 2][:, :], scalar=t.gates[:, 1:2], in1=xs,
                                         op0=ALU.mult, op1=ALU.add).then_inc(x_added, 1)

            dve.wait_ge(logit_out, TT)
            dve.wait_ge(router_in, 32)
            step = Serial(dve, dve_step, ROW_STATS, 5 + TT + 1 + TT + 2 + (TT - 1) + 10 + TT + 3 * K0)
            step(dve.reduce_max(small[:, :], logit[:, :, :], axis=AX.X))
            dve.tensor_tensor(logit[:, :, :], logit[:, :, :], over(small), ALU.subtract).then_inc(exp_asked, 1)
            step(dve.memset(score[:, :, E0:W], -1.0))
            dve.wait_ge(exp_ready, 1)
            step(dve.reduce_sum(small[:, :], logit[:, :, :], axis=AX.X))
            hidden(0, 0)
            step(dve.reciprocal(small[:, :], small[:, :]))
            step(dve.tensor_tensor(score[:, :, 0:E0], logit[:, :, :], over(small), ALU.mult))
            for i in range(TT):
                step.later(dve.max(top[:, i, :], score[:, i, :]))
            step.all()
            step(dve.memset(top[:, :, K0:8], -1.0))
            hidden(0, 1)
            for i in range(TT):
                step.later(dve.match_replace(taken[:, i, :], top[:, i, :], score[:, i, :], MARK))
            step.all()
            hidden(0, 2)
            step(dve.tensor_scalar(chosen[:, :, :], taken[:, :, 0:E0], MARK, None, ALU.is_equal))
            step(dve.memset(chosen_before[:, 0, :], 0.0))
            for i in range(1, TT + 1):
                ins = dve.tensor_tensor(chosen_before[:, i, :], chosen_before[:, i - 1, :], chosen[:, i - 1, :], ALU.add)
                if i == TT:
                    ins.then_inc(chosen_ready, 1)
                else:
                    step(ins)
            hidden(0, 3)
            step(dve.reduce_sum(small[:, :], top[:, :, 0:K0], axis=AX.X))
            step(dve.tensor_scalar(small[:, :], small[:, :], 1e-20, None, ALU.add))
            step(dve.reciprocal(small[:, :], small[:, :]))
            step(dve.tensor_tensor(wsel[:, :, :], score[:, :, 0:E0], over(small), ALU.mult))
            step(dve.tensor_scalar(wsel[:, :, :], wsel[:, :, :], t.gates[:, 1:2], None, ALU.mult))
            hidden(0, 4)
            dve.wait_ge(counted, 1)
            step(dve.tensor_scalar(taken[:, :, 0:E0], count[:, :, :], float(CAP), None, ALU.is_lt))
            step(dve.tensor_tensor(place[:, :, :], count[:, :, :], slot_base[:, :].unsqueeze(1).to_broadcast([P, TT, E0]), ALU.add))
            dve.sem_inc(placed, 1)
            hidden(0, 5)
            step(dve.tensor_tensor(chosen[:, :, :], chosen[:, :, :], taken[:, :, 0:E0], ALU.mult))
            step(dve.tensor_tensor(place[:, :, :], place[:, :, :], chosen[:, :, :], ALU.mult))
            step(dve.tensor_tensor(wsel[:, :, :], wsel[:, :, :], chosen[:, :, :], ALU.mult))
            add(0, 0)
            for i in range(TT):
                step.later(dve.max(t.addr[:, i, :], place[:, i, :]))
            step.all()
            dve.sem_inc(routed, 1)
            add(0, 1)
            dve.wait_ge(counted, 2)
            dve.tensor_copy(t.load[:, :], load).then_inc(loads_ready, 1)
            for k in range(K0):
                slot = t.addr[:, :, k].unsqueeze(2).to_broadcast([P, TT, E0])
                step(dve.tensor_tensor(taken[:, :, 0:E0], place[:, :, :], slot, ALU.is_equal))
                step(dve.tensor_tensor(taken[:, :, 0:E0], taken[:, :, 0:E0], wsel[:, :, :], ALU.mult))
                step(dve.reduce_sum(t.weight[:, :, k], taken[:, :, 0:E0], axis=AX.X))
                if k < 2:
                    add(0, 2 + k)
            step.close()
            with dve.Fori(1, T // NTOK) as n:
                for k in range(NF):
                    hidden(n, k)
                for s in range(NS):
                    add(n, s)

        @block.tensor
        def _(pe):
            pe.sem_inc(tp_ready, 2)
            pe.sem_inc(logit_ready, 2)

            def turn(i, p, first=False):
                pe.wait_ge(xn_ready, i + 1)
                if not first:
                    pe.wait_ge(xts_ready, i - 1)
                transposed_tile(pe, tp[p], xns[p], t).then_inc(tp_ready, 1)

            def logits(i, p, first=False):
                pe.wait_ge(xts_ready, i + 1)
                if not first:
                    pe.wait_ge(logit_out, i - 1)
                for c in range(DC):
                    mm = pe.matmul(lg[p][:, 0:E0], xts[p][:, c * P:(c + 1) * P], gate_wt[:, c, :], start=(c == 0), stop=(c == DC - 1))
                mm.then_inc(logit_ready, 1)

            pe.wait_ge(router_in, 32)
            turn(0, 0, first=True)
            for i in range(2):
                turn(i + 1, 1 - i, first=(i == 0))
                logits(i, i, first=True)
            with pe.Fori(1, TT // 2 - 1) as j:
                for p in range(2):
                    turn(2 * j + p + 1, 1 - p)
                    logits(2 * j + p, p)
            turn(TT - 1, 1)
            logits(TT - 2, 0)
            logits(TT - 1, 1)

            def up(n, k):
                f, m = FTS[k]
                pe.wait_ge(h_ready, n * NF + k + 1)
                for w, psum, done in ((wg, pg, gate_done), (wu, pu, up_done)):
                    for c in range(DC):
                        mm = pe.matmul(psum[k % 2][0:m, :], w[:, c, f:f + m], t.xt[:, c, ds(n * NTOK, NTOK)], start=(c == 0), stop=(c == DC - 1))
                    mm.then_inc(done, 1)

            def down(n):
                pe.wait_ge(h_ready, n * NF + NF + 2)
                for s in range(NS):
                    pe.wait_ge(x_added, n * NS + s + 1)
                    for k, (f, m) in enumerate(FTS):
                        mm = pe.matmul(po[s % 2][:, :], h[0:m, k, s * P:(s + 1) * P], wd[0:m, k, :], start=(k == 0), stop=(k == NF - 1))
                    mm.then_inc(out_done, 1)

            pe.wait_ge(xt_ready, 2 + TT)
            pe.wait_ge(logit_out, TT)
            pe.wait_ge(weights_in, 16 * (2 + NF))
            for k in range(NF - 1):
                up(0, k)
            pe.wait_ge(chosen_ready, 1)
            for i in range(0, TT, TT // 2):
                pe.matmul(count[:, i:i + TT // 2, :], t.before[:, :], chosen[:, i:i + TT // 2, :], start=True, stop=False)
                mm = pe.matmul(count[:, i:i + TT // 2, :], t.ones[:, :], chosen_before[:, i:i + TT // 2, :], start=False, stop=True)
            mm.then_inc(counted, 1)
            up(0, NF - 1)
            pe.wait_ge(placed, 1)
            pe.matmul(load, t.ones[:, :], chosen_before[:, TT, :], start=True, stop=True).then_inc(counted, 1)
            down(0)
            with pe.Fori(1, T // NTOK) as n:
                for k in range(NF):
                    up(n, k)
                down(n)


def experts(nc, t, d):
    with ExitStack() as ctx:
        ph = Phase(nc, ctx, "e_")
        NF = len(FT0)
        wg = [ph.sb(f"wg{p}", [P, DC, F0]) for p in range(2)]
        wu = [ph.sb(f"wu{p}", [P, DC, F0]) for p in range(2)]
        wd = [ph.sb(f"wd{p}", [P, NF, D]) for p in range(2)]
        xs = [ph.sb(f"xs{p}", [P, CT, D]) for p in range(2)]
        xt = [ph.sb(f"xt{p}", [P, DC, CAP]) for p in range(2)]
        sg = [ph.sb(f"sg{p}", [P, CAP]) for p in range(2)]
        h = [ph.sb(f"h{p}", [P, NF, CAP]) for p in range(2)]
        eo = [ph.sb(f"eo{p}", [P, CT, D]) for p in range(2)]
        tp = [ph.ps(f"tp{p}", [P, D]) for p in range(2)]
        pg = [ph.ps(f"pg{p}", [P, D]) for p in range(2)]
        pu = [ph.ps(f"pu{p}", [P, D]) for p in range(2)]
        po = [ph.ps(f"po{p}", [P, D]) for p in range(2)]
        weights_in = [ph.sem(f"weights_in{p}") for p in range(2)]
        xs_in = [ph.sem(f"xs_in{p}") for p in range(2)]
        stored = [ph.sem(f"stored{p}") for p in range(2)]
        tp_ready, xt_ready, gate_done, up_done, silu_ready, h_cleared, h_ready, out_done, eo_ready = ph.sems(
            "tp_ready xt_ready gate_done up_done silu_ready h_cleared h_ready out_done eo_ready")
        block = ctx.enter_context(nc.Block())

        def by_load(eng, e, body):
            load = eng.value_load(t.load[0:1, ds(e, 1)], min_val=0, max_val=T)
            with eng.If(load > (CT - 1) * P):
                body(CT)
            with eng.Else():
                body(CT - 1)

        def by_width(eng, e, body):
            load = eng.value_load(t.load[0:1, ds(e, 1)], min_val=0, max_val=T)

            def choose(k):
                if k == len(WIDTHS) - 1:
                    body(WIDTHS[k])
                    return
                with eng.If(load > WIDTHS[k + 1]):
                    body(WIDTHS[k])
                with eng.Else():
                    choose(k + 1)
            choose(0)

        def rest(n, s):
            return 1 + CT - n if s == n - 1 else 1

        @block.sync
        def _(sp):
            with sp.Fori(0, E0 // 2) as j:
                for p in range(2):
                    e = 2 * j + p
                    sp.wait_ge(out_done, CT * (e + 1))
                    sp.dma_start(wg[p][:, :, :], d["w_gate"][ds(e, 1), :, :, :].rearrange("o p c f -> (o p) c f")).then_inc(weights_in[p], 16)
                    sp.dma_start(wu[p][:, :, :], d["w_up"][ds(e, 1), :, :, :].rearrange("o p c f -> (o p) c f")).then_inc(weights_in[p], 16)
                    for k, (f, m) in enumerate(FT0):
                        sp.dma_start(wd[p][0:m, k, :], d["w_down"][ds(e, 1), f:f + m, :].rearrange("o f d -> (o f) d")).then_inc(weights_in[p], 16)

        @block.gpsimd
        def _(pool):
            pool.sem_inc(tp_ready, 2 * CT)
            with pool.Fori(0, E0 // 2) as j:
                for p in range(2):
                    e = 2 * j + p

                    def body(n):
                        pool.wait_ge(tp_ready, CT * (e + 1))
                        pool.dma_start(xs[p][:, 0:n, :], d["slots"][ds(e * CAP, n * P), :].rearrange("(s p) d -> p s d", p=P)).then_inc(xs_in[p], 16)
                    by_load(pool, e, body)

        @block.scalar
        def _(act):
            def copy_rows(e, p):
                def body(n):
                    for s in range(n):
                        u = CT * e + s
                        act.wait_ge(tp_ready, 2 * CT + u + 1)
                        act.activation(xt[p][:, :, s * P:(s + 1) * P], tp[(CT * p + s) % 2][:, :].rearrange("p (c s) -> p c s", c=DC),
                                       ACT.Copy).then_inc(xt_ready, rest(n, s))
                by_load(act, e, body)

            def silus(e, p):
                def body(w):
                    for k, (f, m) in enumerate(FT0):
                        u = NF * e + k
                        act.wait_ge(gate_done, u + 1)
                        act.wait_ge(h_ready, u + 1)
                        q = (NF * p + k) % 2
                        act.activation(sg[q][0:m, 0:w], pg[q][0:m, 0:w], ACT.Silu).then_inc(silu_ready, 1)
                by_width(act, e, body)

            def store(e, p):
                def body(n):
                    act.wait_ge(eo_ready, 2 + CT * (e + 1))
                    act.dma_start(d["slots"][ds(e * CAP, n * P), :].rearrange("(s p) d -> p s d", p=P), eo[p][:, 0:n, :]).then_inc(stored[p], 16)
                by_load(act, e, body)

            copy_rows(0, 0)
            with act.Fori(0, E0 // 2 - 1) as j:
                for p in range(2):
                    silus(2 * j + p, p)
                    copy_rows(2 * j + p + 1, 1 - p)
                    store(2 * j + p, p)
            silus(E0 - 2, 0)
            copy_rows(E0 - 1, 1)
            store(E0 - 2, 0)
            silus(E0 - 1, 1)
            store(E0 - 1, 1)
            for p in range(2):
                act.wait_ge(stored[p], 16 * (E0 // 2))

        @block.vector
        def _(dve):
            dve.sem_inc(h_ready, 2)
            dve.sem_inc(eo_ready, 2)
            for p in range(2):
                dve.memset(h[p][:, :, :], 0.0).then_inc(h_cleared, 1)
            dve.wait_ge(h_cleared, 2)

            def hidden_and_out(j, p, first=False):
                e = 2 * j + p

                def hidden(w):
                    for k, (f, m) in enumerate(FT0):
                        u = NF * e + k
                        q = (NF * p + k) % 2
                        dve.wait_ge(up_done, u + 1)
                        dve.wait_ge(silu_ready, u + 1)
                        dve.tensor_tensor(h[p][0:m, k, 0:w], sg[q][0:m, 0:w], pu[q][0:m, 0:w], ALU.mult).then_inc(h_ready, 1)

                def body(n):
                    if not first:
                        dve.wait_ge(stored[p], 16 * j)
                    for s in range(n):
                        dve.wait_ge(out_done, 2 * CT + CT * e + s + 1)
                        dve.tensor_copy(eo[p][:, s, :], po[(CT * p + s) % 2][:, :]).then_inc(eo_ready, rest(n, s))
                by_width(dve, e, hidden)
                by_load(dve, e, body)

            for p in range(2):
                hidden_and_out(0, p, first=True)
            with dve.Fori(1, E0 // 2) as j:
                for p in range(2):
                    hidden_and_out(j, p)

        @block.tensor
        def _(pe):
            pe.sem_inc(out_done, 2 * CT)
            pe.sem_inc(xt_ready, 2)

            def transposes(j, e, p):
                def body(n):
                    pe.wait_ge(xs_in[p], 16 * (j + 1))
                    for s in range(n):
                        pe.wait_ge(xt_ready, CT * e + s + 1)
                        transposed_tile(pe, tp[(CT * p + s) % 2], xs[p][:, s, :], t).then_inc(tp_ready, rest(n, s))
                by_load(pe, e, body)

            def up(j, e, p):
                def body(w):
                    pe.wait_ge(weights_in[p], 16 * (2 + NF) * (j + 1))
                    pe.wait_ge(xt_ready, 2 + CT * (e + 1))
                    for k, (f, m) in enumerate(FT0):
                        u = NF * e + k
                        q = (NF * p + k) % 2
                        pe.wait_ge(h_ready, u + 1)
                        for c in range(DC):
                            mm = pe.matmul(pg[q][0:m, 0:w], wg[p][:, c, f:f + m], xt[p][:, c, 0:w], start=(c == 0), stop=(c == DC - 1))
                        mm.then_inc(gate_done, 1)
                        for c in range(DC):
                            mm = pe.matmul(pu[q][0:m, 0:w], wu[p][:, c, f:f + m], xt[p][:, c, 0:w], start=(c == 0), stop=(c == DC - 1))
                        mm.then_inc(up_done, 1)
                by_width(pe, e, body)

            def down(e, p):
                def body(n):
                    pe.wait_ge(h_ready, 2 + NF * (e + 1))
                    for s in range(n):
                        pe.wait_ge(eo_ready, CT * e + s + 1)
                        for k, (f, m) in enumerate(FT0):
                            mm = pe.matmul(po[(CT * p + s) % 2][:, :], h[p][0:m, k, s * P:(s + 1) * P], wd[p][0:m, k, :], start=(k == 0), stop=(k == NF - 1))
                        mm.then_inc(out_done, rest(n, s))
                by_load(pe, e, body)

            transposes(0, 0, 0)
            with pe.Fori(0, E0 // 2 - 1) as j:
                for p in range(2):
                    e = 2 * j + p
                    up(j, e, p)
                    transposes(j + p, e + 1, 1 - p)
                    down(e, p)
            j = E0 // 2 - 1
            up(j, E0 - 2, 0)
            transposes(j, E0 - 1, 1)
            down(E0 - 2, 0)
            up(j, E0 - 1, 1)
            down(E0 - 1, 1)


def combine(nc, t, d):
    with ExitStack() as ctx:
        ph = Phase(nc, ctx, "c_")
        addr_f = ph.sb("addr_f", [P, TT, 8])
        low = ph.sb("low", [P, TT, 8])
        frm = [ph.sb(f"frm{p}", [P, 8], U32) for p in range(2)]
        y = [ph.sb(f"y{p}", [P, K0, D]) for p in range(2)]
        addr_ready, staged, tiles_staged, y_used = ph.sems("addr_ready staged tiles_staged y_used")
        gathered = [ph.sem(f"gathered{p}") for p in range(2)]
        block = ctx.enter_context(nc.Block())

        @block.gpsimd
        def _(pool):
            pool.tensor_scalar(low[:, :, :], t.addr[:, :, :], 1.0, None, ALU.max).then_inc(addr_ready, 1)
            pool.wait_ge(addr_ready, 1)
            pool.tensor_scalar(addr_f[:, :, :], low[:, :, :], -1.0, None, ALU.add).then_inc(addr_ready, 1)
            pool.wait_ge(addr_ready, 2)
            with pool.Fori(0, TT // 2) as j:
                for p in range(2):
                    i = 2 * j + p
                    pool.wait_ge(y_used, K0 * (i + 1))
                    pool.tensor_copy(frm[p][:, :], row(addr_f, i)).then_inc(staged, 1)
                    pool.wait_ge(staged, i + 1)
                    pool.sem_inc(tiles_staged, 1)
                    for k in range(K0):
                        pool.indirect_dma_start(out=y[p][:, k, :], out_offset=None, in_=d["slots"],
                                                in_offset=bass.IndirectOffsetOnAxis(ap=frm[p][:, k:k + 1], axis=0),
                                                bounds_check=SLOTS - 1, oob_is_err=False).then_inc(gathered[p], 16)

        @block.vector
        def _(dve):
            dve.sem_inc(y_used, 2 * K0)
            with dve.Fori(0, TT // 2) as j:
                for p in range(2):
                    i = 2 * j + p
                    dve.wait_ge(gathered[p], 16 * K0 * (j + 1))
                    for k in range(K0):
                        xs = row(t.x, i)
                        w = t.weight[:, ds(i, 1), k:k + 1].rearrange("p o k -> p (o k)")
                        dve.scalar_tensor_tensor(out=xs, in0=y[p][:, k, :], scalar=w, in1=xs, op0=ALU.mult, op1=ALU.add).then_inc(y_used, 1)
                        dve.wait_ge(y_used, 2 * K0 + K0 * i + k + 1)


def layer0(nc, t, d):
    with ExitStack() as ctx:
        ph = Phase(nc, ctx, "m_")
        t.addr = ph.sb("addr", [P, TT, 8])
        t.weight = ph.sb("weight", [P, TT, K0])
        t.load = ph.sb("load", [P, E0], U32)
        with ExitStack() as inner:
            ph = Phase(nc, inner, "z_")
            t.zero = ph.sb("zero", [P, ZROWS * D])
            t.zeroed, = ph.sems("zeroed")
            layer0_attention(nc, t, d)
            route_and_share(nc, t, d)
        experts(nc, t, d)
        combine(nc, t, d)


def layer1_attention(nc, t, d):
    NU = ST * NH // 2
    NM = NH // 8
    NG = NH // 4
    NP = 4
    LT = 3
    OS = NG // 2
    NR = 3 * NM * 4 // 2
    KT = 2 * ST
    SWAP = [i ^ (HD // 2) for i in range(32)]
    with ExitStack() as ctx:
        ph = Phase(nc, ctx, "q_")
        stats6 = ph.sb("stats6", [P, TT, 6])
        wq = ph.sb("wq", [P, DC, D])
        wk = ph.sb("wk", [P, DC, D])
        wv = ph.sb("wv", [P, DC, D])
        wo = ph.sb("wo", [P, NG, D])
        rope = ph.sb("rope", [P, 2, S])
        rep = ph.sb("rep", [P, 2, 2, 4, P], F32R)
        head_gate = ph.sb("head_gate", [P, NH // 2, 4])
        mask = ph.sb("mask", [P, ST, S])
        cxt = ph.sb("cxt", [P, DC, S])
        qs = ph.sb("qs", [P, NH // 2, S], F32R)
        ks = ph.sb("ks", [P, NH // 2, 2 * S], F32R)
        vv = ph.sb("vv", [P, KT, NH, HD])
        masked = ph.sb("masked", [P, 2, 2, S])
        xns = masked[:, :, :, :].rearrange("p a k s -> p a (k s)")
        top = ph.sb("top", [P, 4])
        ntop = [ph.sb(f"ntop{p}", [P, 4]) for p in range(2)]
        total = [ph.sb(f"total{p}", [P, 4]) for p in range(2)]
        share = [ph.sb(f"share{p}", [P, 4]) for p in range(2)]
        norm = [ph.sb(f"norm{p}", [P, 4]) for p in range(2)]
        prob = [ph.sb(f"prob{p}", [P, 2, 2 * S]) for p in range(NP)]
        probt, probt_at = [], []
        for p in range(2):
            probt_at.append(nc.sbuf_base)
            probt.append(ph.sb(f"probt{p}", [P, 4, KT, S]))
        turned, straight = ([x[:, k, :, :] for x in probt] for k in range(2))
        part_bytes = NM * S * 4
        high, low = ([nc.alloc_sbuf_tensor_at(f"q_{name}{p}", [P, NM, S], F32R, offset=probt_at[p] + k * part_bytes) for p in range(2)]
                     for name, k in (("high", 2), ("low", 3)))
        ots = ph.sb("ots", [P, NG, S])
        xt = prob[0][:, :, :].rearrange("p a (c s) -> p (a c) s", s=S)
        score = [ph.ps(f"score{p}", [P, 2, D]) for p in range(2)]
        tps = ph.ps("tps", [P, 2, D])
        ot = ph.ps("ot", [P, D])
        out = ph.ps("out", [P, D])
        ring = [tps[:, 0, :], tps[:, 1, :], ot[:, :], out[:, :]]
        weights_in, ctx_in, mask_in, gates_ready, stats_ready, rstd_ready, xn_ready, xtp_ready, xt_ready = ph.sems(
            "weights_in ctx_in mask_in gates_ready stats_ready rstd_ready xn_ready xtp_ready xt_ready")
        q_done, k_done, ak_done, v_done, av_done, q_turned, k_turned, q_split, k_split, ak_high, ak_split, v_ready = ph.sems(
            "q_done k_done ak_done v_done av_done q_turned k_turned q_split k_split ak_high ak_split v_ready")
        rep_in, rep_ready, stack_done, stacked_act, stacked_dve = ph.sems("rep_in rep_ready stack_done stacked_act stacked_dve")
        score_ready, mask_used, top_ready, exp_ready, norm_ready, prob_ready, tps_ready, probt0_ready, probt1_ready, value_done = ph.sems(
            "score_ready mask_used top_ready exp_ready norm_ready prob_ready tps_ready probt0_ready probt1_ready value_done")
        ot_copied, out_ready, x_added, dve_step, pool_step, norm_seen, dve_seen = ph.sems("ot_copied out_ready x_added dve_step pool_step norm_seen dve_seen")
        block = ctx.enter_context(nc.Block())

        def stack_tiles(c):
            kind, m, a = c // 8, c // 4 % 2 * 2, c % 4
            dst = (qs[:, :, :], ks[:, :, 0:S], ks[:, :, S:2 * S])[kind]
            return kind, m, a, dst[:, 4 * m + a:4 * m + a + 5:4, :]

        def unit(u):
            g, s, pr = u // 4, u // 2 % 2, u % 2
            return g, s, pr, 2 * g + pr

        def value_parts(i):
            v = i - LT - 4
            if v == NU - 4:
                return [(NG - 1, n) for n in range(KT)]
            return [(v // 4, n) for n in ((0,), (1,), (2, 3), ())[v % 4]] if 0 <= v < NU - 4 else []

        @block.sync
        def _(sp):
            for w, n in ((wq, "wq"), (wk, "wk"), (wv, "wv")):
                sp.dma_start(w[:, :, :], d[n].rearrange("(c p) n -> p c n", p=P)).then_inc(weights_in, 16)
            sp.dma_start(wo[:, :, :], d["wo"]).then_inc(weights_in, 16)
            sp.dma_start(rope[:, :, :], d["rope"]).then_inc(weights_in, 16)
            sp.dma_start(probt[0][:, 0:2, :, :].rearrange("p a k s -> p (a k s)"), d["rep"]).then_inc(rep_in, 16)
            sp.dma_start(head_gate[:, :, :], d["head_gate"]).then_inc(weights_in, 16)

            def load(b):
                sp.dma_start(cxt[:, :, :], d["ctx_t"][ds(b, 1), :, :].rearrange("o (c p) s -> p (o c) s", p=P)).then_inc(ctx_in, 16)

            def load_mask(b):
                sp.dma_start(mask[:, :, :], d["mask"][ds(b, 1), :, :].rearrange("o (t p) k -> p (o t) k", p=P)).then_inc(mask_in, 16)

            load(0)
            load_mask(0)
            with sp.Fori(1, B) as b:
                sp.wait_ge(av_done, b)
                load(b)
                sp.wait_ge(mask_used, b)
                load_mask(b)

        @block.gpsimd
        def _(pool):
            pool.wait_ge(stats_ready, 1)
            row_rstd(pool, Serial(pool, pool_step, 0, 2), t)
            pool.sem_inc(rstd_ready, 1)
            with pool.Fori(0, B) as b:
                for u in range(NU):
                    pool.wait_ge(norm_ready, b * NU + u + 1)
                    pool.sem_inc(norm_seen, 1)
                    for k in range(4):
                        half = prob[u % NP][:, k % 2, (k // 2) * S:(k // 2 + 1) * S]
                        pool.tensor_scalar(half, half, norm[u % 2][:, k:k + 1], 1.0, ALU.mult, ALU.mult).then_inc(prob_ready, 1)

        @block.scalar
        def _(act):
            act.wait_ge(weights_in, 6 * 16)
            act.activation(head_gate[:, :, 2:4], head_gate[:, :, 2:4], ACT.Tanh).then_inc(gates_ready, 1)

            def prologue(b):
                for s in range(ST):
                    act.wait_ge(xtp_ready, ST * b + s + 1)
                    act.activation(xt[:, :, s * P:(s + 1) * P], score[1][:, s, :].rearrange("p (c s) -> p c s", c=DC), ACT.Copy).then_inc(xt_ready, 1)

            prologue(0)
            def batch(b, first=False, last=False):
                def stack(c):
                    act.wait_ge(stack_done, NR * b + c + 1)
                    act.activation(stack_tiles(c)[3], ring[c % 4].rearrange("p (t s) -> p t s", s=S), ACT.Copy).then_inc(stacked_act, 1)

                def values(k):
                    act.activation(vv[:, k, :, :], score[1 - k // ST][:, k % ST, :].rearrange("p (h d) -> p h d", d=HD), ACT.Copy).then_inc(v_ready, 1)

                for c in range(0, 8, 2):
                    stack(c)
                act.wait_ge(ak_done, b + 1)
                act.wait_ge(stack_done, NR * b + 8)
                act.activation(high[0][:, :, :], score[0][:, :, :].rearrange("p a (m s) -> p (a m) s", s=S), ACT.Copy).then_inc(ak_high, 1)
                act.wait_ge(v_done, b + 1)
                for k in range(ST):
                    values(k)
                for c in range(8, 16, 2):
                    stack(c)
                act.wait_ge(av_done, b + 1)
                for k in range(ST, KT):
                    values(k)
                for c in range(16, NR, 2):
                    stack(c)
                for i in range(NU + LT + 2):
                    if i == NU + LT - 1 and not last:
                        prologue(b + 1)
                    v = i - LT
                    if 0 <= v < NU:
                        act.wait_ge(tps_ready, b * NU + v + 1)
                        g, s, pr, pair = unit(v)
                        if g >= 2 and v % 4 == 0:
                            act.wait_ge(value_done, b * NG + g - 1)
                        act.activation(probt[g % 2][:, 2 * pr + 1, :, s * P:(s + 1) * P], tps[:, 1, :].rearrange("p (n q) -> p n q", q=P), ACT.Copy).then_inc(probt1_ready, 1)
                    for g, n in value_parts(i - 1):
                        if n == KT - 1:
                            act.wait_ge(value_done, b * NG + g + 1)
                            act.activation(ots[:, g, :], ot[:, 0:S], ACT.Copy).then_inc(ot_copied, 1)
                    if i < NU:
                        act.wait_ge(top_ready, b * NU + i + 1)
                        if i >= NP:
                            act.wait_ge(tps_ready, b * NU + i - NP + 1)
                        for k in range(4):
                            src = masked[:, i % 2, k, :] if k < 2 else score[i % 2][:, k - 2, S:2 * S]
                            act.activation(prob[i % NP][:, k % 2, (k // 2) * S:(k // 2 + 1) * S], src, ACT.Exp,
                                           bias=ntop[i % 2][:, k:k + 1], accum_out=total[i % 2][:, k:k + 1]).then_inc(exp_ready, 1)

            batch(0, first=True)
            with act.Fori(1, B - 1) as b:
                batch(b)
            batch(B - 1, last=True)

        @block.vector
        def _(dve):
            row_stats(dve, Serial(dve, dve_step, 0, ROW_STATS), t, stats6)
            dve.sem_inc(stats_ready, 1)
            dve.wait_ge(gates_ready, 1)
            step = Serial(dve, dve_step, ROW_STATS, 1)
            step(dve.memset(head_gate[:, :, 0:2], 1.0))
            dve.wait_ge(rep_in, 16)
            dve.tensor_copy(rep[:, :, :, :, :].rearrange("p a b c q -> p (a b c q)"), probt[0][:, 0:2, :, :].rearrange("p a k s -> p (a k s)")).then_inc(rep_ready, 1)
            dve.wait_ge(rep_ready, 1)
            dve.wait_ge(rstd_ready, 1)
            steps = 2 * 4 + 4 * NU

            def normalise(b):
                for s in range(ST):
                    dve.tensor_scalar(xns[:, s, :], row(t.x, ST * b + s), t.mv_at(ST * b + s, 0), t.rstd_at(ST * b + s),
                                      ALU.subtract, ALU.mult).then_inc(xn_ready, 1)

            def rotary(b, step):
                for n, done, raw_read, split in ((0, q_done, q_turned, q_split), (1, k_done, k_turned, k_split)):
                    dve.wait_ge(done, b + 1)
                    raw = score[n][:, :, :].rearrange("p a (m s) -> p (a m) s", s=S)
                    cos = rope[:, 0, :].unsqueeze(1).to_broadcast([P, NM, S])
                    sin = rope[:, 1, :].unsqueeze(1).to_broadcast([P, NM, S])
                    dve.sem_inc(dve_seen, 1)
                    step(dve.stream_shuffle(turned[n].rearrange("p m s -> p (m s)"), score[n][:, :, :].rearrange("p a f -> p (a f)"), SWAP))
                    dve.tensor_tensor(straight[n], raw, cos, ALU.mult).then_inc(raw_read, 1)
                    step(dve.tensor_tensor(turned[n], turned[n], sin, ALU.mult))
                    step(dve.tensor_tensor(straight[n], straight[n], turned[n], ALU.add))
                    step(dve.tensor_copy(high[n][:, :, :], straight[n]))
                    dve.tensor_tensor(low[n][:, :, :], straight[n], high[n][:, :, :].bitcast(F32), ALU.subtract).then_inc(split, 1)

            normalise(0)
            step = Serial(dve, dve_step, ROW_STATS + 1, 8)
            rotary(0, step)
            step.close()
            def add_output(b, s):
                dve.wait_ge(out_ready, ST * b + s + 1)
                xs = row(t.x, ST * b + s)
                dve.scalar_tensor_tensor(out=xs, in0=out[:, :], scalar=t.gates[:, 2:3], in1=xs, op0=ALU.mult, op1=ALU.add).then_inc(x_added, 1)

            def batch(b, first=False, last=False):
                step = Serial(dve, dve_step, ROW_STATS + 1 + 8 + b * steps, steps - 8 if last else steps)

                def stack(c):
                    dve.wait_ge(stack_done, NR * b + c + 1)
                    dve.tensor_copy(stack_tiles(c)[3], ring[c % 4].rearrange("p (t s) -> p t s", s=S)).then_inc(stacked_dve, 1)

                for c in range(1, 8, 2):
                    stack(c)
                dve.wait_ge(ak_high, b + 1)
                dve.tensor_tensor(low[0][:, :, :], score[0][:, :, :].rearrange("p a (m s) -> p (a m) s", s=S), high[0][:, :, :].bitcast(F32), ALU.subtract).then_inc(ak_split, 1)
                for c in range(9, NR, 2):
                    stack(c)
                dve.wait_ge(mask_in, 16 * (b + 1))
                step(dve.tensor_scalar(mask[:, :, :], mask[:, :, :], FMIN, None, ALU.max))
                for i in range(NU + LT):
                    if i < NU:
                        g, s, pr, pair = unit(i)
                        dve.wait_ge(score_ready, b * NU + i + 1)
                        if i >= 2:
                            dve.wait_ge(exp_ready, 4 * (b * NU + i - 1))
                        if i:
                            dve.wait_ge(top_ready, b * NU + i)
                        dve.sem_inc(dve_seen, 1)
                        for k in range(2):
                            ins = dve.tensor_tensor_reduce(out=masked[:, i % 2, k, :], in0=score[i % 2][:, k, 0:S], in1=mask[:, s, :], scale=1.0,
                                                           scalar=FMIN, op0=ALU.add, op1=ALU.max, accum_out=top[:, k:k + 1])
                            if i == NU - 1 and k == 1:
                                ins.then_inc(mask_used, 1)
                            else:
                                step.later(ins)
                        step.later(dve.reduce_max(top[:, 2:4], score[i % 2][:, :, S:2 * S], axis=AX.X))
                    v = i - 1
                    if 0 <= v < NU:
                        if v >= 2:
                            dve.wait_ge(prob_ready, 4 * (b * NU + v - 1))
                        dve.wait_ge(exp_ready, 4 * (b * NU + v + 1))
                        step.later(dve.reciprocal(share[v % 2][:, :], total[v % 2][:, :]))
                    step.all()
                    if i < NU:
                        if i == NU - 1:
                            dve.wait_ge(mask_used, b + 1)
                        dve.tensor_scalar(ntop[i % 2][:, :], top[:, :], -1.0, None, ALU.mult).then_inc(top_ready, 1)
                    if 0 <= v < NU:
                        dve.tensor_tensor(norm[v % 2][:, :], share[v % 2][:, :], head_gate[:, unit(v)[3], :], ALU.mult).then_inc(norm_ready, 1)
                    if i == NU - 1:
                        dve.wait_ge(top_ready, (b + 1) * NU)
                    if v == NU - 1 and not last:
                        normalise(b + 1)
                    v = i - LT
                    if 0 <= v < NU:
                        dve.wait_ge(tps_ready, b * NU + v + 1)
                        g, s, pr, pair = unit(v)
                        if g >= 2 and v % 4 == 0:
                            dve.wait_ge(value_done, b * NG + g - 1)
                        dve.tensor_copy(probt[g % 2][:, 2 * pr, :, s * P:(s + 1) * P], tps[:, 0, :].rearrange("p (n q) -> p n q", q=P)).then_inc(probt0_ready, 1)
                    if i in (OS - 1, 2 * OS) and not first:
                        add_output(b - 1, i // OS // 2)
                if not last:
                    rotary(b + 1, step)
                step.close()

            batch(0, first=True)
            with dve.Fori(1, B - 1) as b:
                batch(b)
            batch(B - 1, last=True)
            for s in range(ST):
                add_output(B - 1, s)

        @block.tensor
        def _(pe):
            pe.wait_ge(weights_in, 6 * 16)

            def heads_by_position(psum, w, x):
                for m in range(NM):
                    for c in range(DC):
                        mm = pe.matmul(psum[:, m // 2, (m % 2) * S:(m % 2 + 1) * S], w[:, c, m * P:(m + 1) * P], x[:, c, :], start=(c == 0), stop=(c == DC - 1))
                return mm

            def positions_by_head(psum, w, x):
                for s in range(ST):
                    for c in range(DC):
                        mm = pe.matmul(psum[:, s, :], x[:, c, s * P:(s + 1) * P], w[:, c, :], start=(c == 0), stop=(c == DC - 1))
                return mm

            def turn(b):
                for s in range(ST):
                    pe.wait_ge(xn_ready, ST * b + s + 1)
                    transposed_tile(pe, score[1][:, s, :], xns[:, s, :], t).then_inc(xtp_ready, 1)

            def q_product(b):
                pe.wait_ge(xt_ready, ST * b + ST)
                heads_by_position(score[0], wq, xt).then_inc(q_done, 1)

            turn(0)
            q_product(0)
            heads_by_position(score[1], wk, xt).then_inc(k_done, 1)
            def output_part(b, n):
                s, g0 = n // OS, 2 * (n % OS)
                if n == OS:
                    pe.wait_ge(x_added, ST * b + 1)
                for g in (g0, g0 + 1):
                    mm = pe.matmul(out[:, :], ots[:, g, s * P:(s + 1) * P], wo[:, g, :], start=(g == 0), stop=(g == NG - 1))
                if g == NG - 1:
                    mm.then_inc(out_ready, 1)

            def batch(b, first=False, last=False):
                def stack(kind):
                    for c in range(8 * kind, 8 * kind + 8):
                        if c >= 4:
                            pe.wait_ge((stacked_act, stacked_dve)[c % 2], NR // 2 * b + c // 2 - 1)
                        _, m, a, _ = stack_tiles(c)
                        n = kind % 2
                        pe.matmul(ring[c % 4], rep[:, min(kind, 1), 0, a, :], high[n][:, m:m + 2, :].rearrange("p m s -> p (m s)"), start=True, stop=False)
                        pe.matmul(ring[c % 4], rep[:, min(kind, 1), 1, a, :], low[n][:, m:m + 2, :].rearrange("p m s -> p (m s)"), start=False, stop=True).then_inc(stack_done, 1)

                pe.wait_ge(q_turned, b + 1)
                pe.wait_ge(ctx_in, 16 * (b + 1))
                heads_by_position(score[0], wk, cxt).then_inc(ak_done, 1)
                pe.wait_ge(q_split, b + 1)
                stack(0)
                pe.wait_ge(k_turned, b + 1)
                positions_by_head(score[1], wv, xt).then_inc(v_done, 1)
                pe.wait_ge(k_split, b + 1)
                stack(1)
                pe.wait_ge(ak_split, b + 1)
                positions_by_head(score[0], wv, cxt).then_inc(av_done, 1)
                stack(2)
                pe.wait_ge(stacked_act, NR // 2 * (b + 1))
                pe.wait_ge(stacked_dve, NR // 2 * (b + 1))
                pe.wait_ge(v_ready, KT * (b + 1))
                for i in range(NU + LT + 1):
                    if i < NU:
                        g, s, pr, pair = unit(i)
                        if i >= 2:
                            pe.wait_ge(exp_ready, 4 * (b * NU + i - 1))
                        for k in range(2):
                            mm = pe.matmul(score[i % 2][:, k, :], qs[64 * k:64 * k + 64, pair, s * P:(s + 1) * P], ks[64 * k:64 * k + 64, pair, :], start=True, stop=True)
                        mm.then_inc(score_ready, 1)
                    if i == NU + LT - 1 and not last:
                        turn(b + 1)
                    v = i - LT
                    if 0 <= v < NU:
                        pe.wait_ge(prob_ready, 4 * (b * NU + v + 1))
                        if v >= 1:
                            pe.wait_ge(probt0_ready, b * NU + v)
                            pe.wait_ge(probt1_ready, b * NU + v)
                        for k in range(2):
                            mm = transposed_tile(pe, tps[:, k, :], prob[v % NP][:, k, :], t)
                        mm.then_inc(tps_ready, 1)
                    if i < 2 * OS + 1 and i != OS and not first:
                        output_part(b - 1, i if i < OS else i - 1)
                    if i == 2 * OS + 2 and not first:
                        pe.wait_ge(x_added, ST * b)
                    for g, n in value_parts(i):
                        if n == 0:
                            pe.wait_ge(probt0_ready, b * NU + 4 * g + 4)
                            pe.wait_ge(probt1_ready, b * NU + 4 * g + 4)
                            if g:
                                pe.wait_ge(ot_copied, b * NG + g)
                        for c in range(4):
                            mm = pe.matmul(ot[32 * c:32 * c + HD, 0:S], vv[:, n, 4 * g + c, :], probt[g % 2][:, c, n, :], start=(n == 0), stop=(n == KT - 1))
                        if n == KT - 1:
                            mm.then_inc(value_done, 1)
                    if i == NU + LT - 1 and not last:
                        q_product(b + 1)
                if not last:
                    heads_by_position(score[1], wk, xt).then_inc(k_done, 1)
                pe.wait_ge(ot_copied, NG * (b + 1))

            batch(0, first=True)
            with pe.Fori(1, B - 1) as b:
                batch(b)
            batch(B - 1, last=True)
            for n in range(2 * OS):
                output_part(B - 1, n)


def moe1(nc, t, d):
    with ExitStack() as ctx:
        ph = Phase(nc, ctx, "v_")
        t.addr = ph.sb("addr", [P, TT, 8])
        t.weight = ph.sb("weight", [P, TT, K1])
        t.mix = ph.sb("mix", [P, TT, E1])
        t.job_expert = ph.sb("job_expert", [P, NJ], U32)
        t.job_load = ph.sb("job_load", [P, NJ], U32)
        t.jobs = ph.sb("jobs", [P, 4], U32)
        with ExitStack() as inner:
            ph = Phase(nc, inner, "u_")
            t.xn = ph.sb("xn", [P, TT, D])
            route1(nc, t, d)
            experts1(nc, t, d)
        combine_and_store(nc, t, d)


def route1(nc, t, d):
    W = E1 + 8 - K1
    with ExitStack() as ctx:
        ph = Phase(nc, ctx, "w_")
        stats6 = ph.sb("stats6", [P, TT, 6])
        router_t = ph.sb("router_t", [P, DC, E1])
        router_b = ph.sb("router_b", [P, E1])
        job_starts = ph.sb("job_starts", [P, E1, MJ])
        up_to = ph.sb("up_to", [P, E1, E1])
        job_number = ph.sb("job_number", [P, NJ])
        xns = [ph.sb(f"xns{p}", [P, D]) for p in range(2)]
        xts = [ph.sb(f"xts{p}", [P, D]) for p in range(2)]
        logit = ph.sb("logit", [P, TT, W])
        taken = ph.sb("taken", [P, TT, W])
        top = ph.sb("top", [P, TT, 8])
        expd = ph.sb("expd", [P, TT, E1])
        chosen = ph.sb("chosen", [P, TT, E1])
        chosen_before = ph.sb("chosen_before", [P, TT + 1, E1])
        place = ph.sb("place", [P, TT, E1])
        total = ph.sb("total", [P, TT])
        started = ph.sb("started", [P, E1, MJ])
        jobs_of = ph.sb("jobs_of", [P, E1])
        jobs_up_to = ph.sb("jobs_up_to", [P, E1, E1])
        job_end = ph.sb("job_end", [P, E1])
        slot_base = ph.sb("slot_base", [P, E1])
        tokens = ph.sb("tokens", [P, E1])
        tokens_end = ph.sb("tokens_end", [P, E1])
        job_begin = ph.sb("job_begin", [P, E1])
        begun = ph.sb("begun", [P, NJ, E1])
        job_last = ph.sb("job_last", [P, NJ])
        job_first = ph.sb("job_first", [P, NJ])
        ended = ph.sb("ended", [P, NJ, E1])
        job_counts = ph.sb("job_counts", [P, NJ])
        tp = [ph.ps(f"tp{p}", [P, D]) for p in range(2)]
        lg = [ph.ps(f"lg{p}", [P, D]) for p in range(2)]
        counts = ph.ps("counts", [P, D])
        count = counts[:, 0:TT * E1].rearrange("p (i e) -> p i e", e=E1)
        load = counts[:, TT * E1:(TT + 1) * E1]
        weights_in, stats_ready, rstd_ready, xn_ready, xn_copied, tp_ready, xts_ready, logit_ready, logit_out = ph.sems(
            "weights_in stats_ready rstd_ready xn_ready xn_copied tp_ready xts_ready logit_ready logit_out")
        exp_asked, exp_ready, mix_ready, chosen_ready, counted, dve_step, pool_step = ph.sems(
            "exp_asked exp_ready mix_ready chosen_ready counted dve_step pool_step")
        block = ctx.enter_context(nc.Block())

        def over(x, n=E1):
            return x.unsqueeze(2).to_broadcast([P, TT, n])

        @block.sync
        def _(sp):
            sp.dma_start(router_t[:, :, :], d["router_t"].rearrange("(c p) e -> p c e", p=P)).then_inc(weights_in, 16)
            sp.dma_start(router_b[:, :], d["router_b"]).then_inc(weights_in, 16)
            sp.dma_start(job_starts[:, :, :], d["job_starts"]).then_inc(weights_in, 16)
            sp.dma_start(up_to[:, :, :], d["up_to"]).then_inc(weights_in, 16)
            sp.dma_start(job_number[:, :], d["job_number"]).then_inc(weights_in, 16)

        @block.gpsimd
        def _(pool):
            pool.sem_inc(xn_copied, 2)
            pool.wait_ge(stats_ready, 1)
            row_rstd(pool, Serial(pool, pool_step, 0, 2), t)
            pool.sem_inc(rstd_ready, 1)
            with pool.Fori(0, TT // 2) as j:
                for p in range(2):
                    i = 2 * j + p
                    pool.wait_ge(xn_ready, i + 1)
                    pool.tensor_copy(row(t.xn, i), xns[p][:, :]).then_inc(xn_copied, 1)

        @block.scalar
        def _(act):
            def copy_tile(i, p):
                act.wait_ge(tp_ready, 2 + i + 1)
                act.wait_ge(logit_ready, i + 1)
                act.activation(xts[p][:, :], tp[p][:, :], ACT.Copy).then_inc(xts_ready, 1)

            def copy_logits(i, p):
                act.wait_ge(logit_ready, 2 + i + 1)
                act.activation(logit[:, ds(i, 1), 0:E1].rearrange("p o e -> p (o e)"), lg[p][:, 0:E1], ACT.Copy).then_inc(logit_out, 1)

            copy_tile(0, 0)
            with act.Fori(0, TT // 2 - 1) as j:
                for p in range(2):
                    copy_tile(2 * j + p + 1, 1 - p)
                    copy_logits(2 * j + p, p)
            copy_tile(TT - 1, 1)
            copy_logits(TT - 2, 0)
            copy_logits(TT - 1, 1)
            act.wait_ge(exp_asked, 1)
            act.activation(expd[:, :, :], expd[:, :, :], ACT.Exp).then_inc(exp_ready, 1)

        @block.vector
        def _(dve):
            row_stats(dve, Serial(dve, dve_step, 0, ROW_STATS), t, stats6)
            dve.sem_inc(stats_ready, 1)
            dve.wait_ge(rstd_ready, 1)
            with dve.Fori(0, TT // 2) as j:
                for p in range(2):
                    i = 2 * j + p
                    dve.wait_ge(tp_ready, i + 1)
                    dve.wait_ge(xn_copied, i + 1)
                    dve.tensor_scalar(xns[p][:, :], row(t.x, i), t.mv_at(i, 0), t.rstd_at(i), ALU.subtract, ALU.mult).then_inc(xn_ready, 1)
            dve.wait_ge(logit_out, TT)
            dve.wait_ge(weights_in, 5 * 16)
            step = Serial(dve, dve_step, ROW_STATS, 4 + 2 * TT + TT + 3 + 24 + TT + 3 * K1)
            step(dve.tensor_tensor(logit[:, :, 0:E1], logit[:, :, 0:E1], router_b[:, :].unsqueeze(1).to_broadcast([P, TT, E1]), ALU.add))
            step(dve.memset(logit[:, :, E1:W], FMIN))
            for i in range(TT):
                step.later(dve.max(top[:, i, :], logit[:, i, :]))
            step.all()
            dve.tensor_tensor(expd[:, :, :], logit[:, :, 0:E1], over(top[:, :, 0]), ALU.subtract).then_inc(exp_asked, 1)
            step(dve.memset(top[:, :, K1:8], FMIN))
            for i in range(TT):
                step.later(dve.match_replace(taken[:, i, :], top[:, i, :], logit[:, i, :], MARK))
            step.all()
            step(dve.tensor_scalar(chosen[:, :, :], taken[:, :, 0:E1], MARK, None, ALU.is_equal))
            step(dve.memset(chosen_before[:, 0, :], 0.0))
            for i in range(1, TT + 1):
                ins = dve.tensor_tensor(chosen_before[:, i, :], chosen_before[:, i - 1, :], chosen[:, i - 1, :], ALU.add)
                if i == TT:
                    ins.then_inc(chosen_ready, 1)
                else:
                    step(ins)
            dve.wait_ge(exp_ready, 1)
            step(dve.tensor_tensor(expd[:, :, :], expd[:, :, :], chosen[:, :, :], ALU.mult))
            step(dve.reduce_sum(total[:, :], expd[:, :, :], axis=AX.X))
            step(dve.reciprocal(total[:, :], total[:, :]))
            dve.tensor_tensor(t.mix[:, :, :], expd[:, :, :], over(total[:, :]), ALU.mult).then_inc(mix_ready, 1)
            dve.wait_ge(counted, 1)
            step(dve.tensor_copy(tokens[:, :], load))
            step(dve.tensor_tensor(started[:, :, :], tokens[:, :].unsqueeze(2).to_broadcast([P, E1, MJ]), job_starts[:, :, :], ALU.is_gt))
            step(dve.reduce_sum(jobs_of[:, :], started[:, :, :], axis=AX.X))
            step(dve.tensor_tensor(jobs_up_to[:, :, :], jobs_of[:, :].unsqueeze(1).to_broadcast([P, E1, E1]), up_to[:, :, :], ALU.mult))
            step(dve.reduce_sum(job_end[:, :], jobs_up_to[:, :, :], axis=AX.X))
            step(dve.tensor_tensor(job_begin[:, :], job_end[:, :], jobs_of[:, :], ALU.subtract))
            step(dve.tensor_scalar(slot_base[:, :], job_begin[:, :], float(JC), 1.0, ALU.mult, ALU.add))
            step(dve.tensor_tensor(ended[:, :, :], job_end[:, :].unsqueeze(1).to_broadcast([P, NJ, E1]),
                                   job_number[:, :].unsqueeze(2).to_broadcast([P, NJ, E1]), ALU.is_le))
            step(dve.reduce_sum(job_counts[:, :], ended[:, :, :], axis=AX.X))
            step(dve.tensor_scalar(t.job_expert[:, :], job_counts[:, :], float(E1 - 1), None, ALU.min))
            numbers = job_number[:, :].unsqueeze(2).to_broadcast([P, NJ, E1])
            step(dve.tensor_tensor(tokens_end[:, :], slot_base[:, :], tokens[:, :], ALU.add))
            step(dve.tensor_tensor(begun[:, :, :], job_begin[:, :].unsqueeze(1).to_broadcast([P, NJ, E1]), numbers, ALU.is_le))
            step(dve.tensor_tensor(begun[:, :, :], begun[:, :, :], ended[:, :, :], ALU.subtract))
            step(dve.tensor_tensor(begun[:, :, :], begun[:, :, :], tokens_end[:, :].unsqueeze(1).to_broadcast([P, NJ, E1]), ALU.mult))
            step(dve.reduce_sum(job_last[:, :], begun[:, :, :], axis=AX.X))
            step(dve.tensor_scalar(job_first[:, :], job_number[:, :], float(JC), 1.0, ALU.mult, ALU.add))
            step(dve.tensor_tensor(job_last[:, :], job_last[:, :], job_first[:, :], ALU.subtract))
            step(dve.tensor_scalar(t.job_load[:, :], job_last[:, :], 0.0, None, ALU.max))
            step(dve.tensor_copy(t.jobs[:, 0:1], job_end[:, E1 - 1:E1]))
            step(dve.tensor_tensor(job_counts[:, :], job_end[:, E1 - 1:E1].to_broadcast([P, NJ]), job_number[:, :], ALU.is_gt))
            step(dve.reduce_sum(total[:, 0:2], job_counts[:, :].rearrange("p (j two) -> p two j", two=2), axis=AX.X))
            step(dve.tensor_copy(t.jobs[:, 1:3], total[:, 0:2]))
            step(dve.tensor_tensor(place[:, :, :], count, slot_base[:, :].unsqueeze(1).to_broadcast([P, TT, E1]), ALU.add))
            step(dve.tensor_tensor(place[:, :, :], place[:, :, :], chosen[:, :, :], ALU.mult))
            for i in range(TT):
                step.later(dve.max(t.addr[:, i, :], place[:, i, :]))
            step.all()
            dve.wait_ge(mix_ready, 1)
            dve.tensor_scalar(expd[:, :, :], t.mix[:, :, :], t.gates[:, 3:4], None, ALU.mult).then_inc(mix_ready, 1)
            dve.wait_ge(mix_ready, 2)
            for k in range(K1):
                slot = over(t.addr[:, :, k])
                step(dve.tensor_tensor(taken[:, :, 0:E1], place[:, :, :], slot, ALU.is_equal))
                step(dve.tensor_tensor(taken[:, :, 0:E1], taken[:, :, 0:E1], expd[:, :, :], ALU.mult))
                step(dve.reduce_sum(t.weight[:, :, k], taken[:, :, 0:E1], axis=AX.X))
            step.close()

        @block.tensor
        def _(pe):
            pe.sem_inc(tp_ready, 2)
            pe.sem_inc(logit_ready, 2)

            def turn(i, p, first=False):
                pe.wait_ge(xn_ready, i + 1)
                if not first:
                    pe.wait_ge(xts_ready, i - 1)
                transposed_tile(pe, tp[p], xns[p], t).then_inc(tp_ready, 1)

            def logits(i, p, first=False):
                pe.wait_ge(xts_ready, i + 1)
                if not first:
                    pe.wait_ge(logit_out, i - 1)
                for c in range(DC):
                    mm = pe.matmul(lg[p][:, 0:E1], xts[p][:, c * P:(c + 1) * P], router_t[:, c, :], start=(c == 0), stop=(c == DC - 1))
                mm.then_inc(logit_ready, 1)

            pe.wait_ge(weights_in, 5 * 16)
            turn(0, 0, first=True)
            for i in range(2):
                turn(i + 1, 1 - i, first=(i == 0))
                logits(i, i, first=True)
            with pe.Fori(1, TT // 2 - 1) as j:
                for p in range(2):
                    turn(2 * j + p + 1, 1 - p)
                    logits(2 * j + p, p)
            turn(TT - 1, 1)
            logits(TT - 2, 0)
            logits(TT - 1, 1)
            pe.wait_ge(chosen_ready, 1)
            pe.matmul(count, t.before[:, :], chosen[:, :, :], start=True, stop=False)
            pe.matmul(count, t.ones[:, :], chosen_before[:, 0:TT, :], start=False, stop=True)
            pe.matmul(load, t.ones[:, :], chosen_before[:, TT, :], start=True, stop=True).then_inc(counted, 1)


def experts1(nc, t, d):
    NF = I1 // P
    with ExitStack() as ctx:
        ph = Phase(nc, ctx, "x_")
        addr_f = ph.sb("addr_f", [P, TT, 8])
        to = ph.sb("to", [P, TT, 8], U32)
        down_b = ph.sb("down_b", [E1, D])
        mixt = ph.sb("mixt", [E1, T])
        wgu = [ph.sb(f"wgu{p}", [P, DC, 2, I1]) for p in range(2)]
        wd = [ph.sb(f"wd{p}", [P, NF, D]) for p in range(2)]
        bgu = ph.sb("bgu", [P, E1, 2 * NF])
        xs = [ph.sb(f"xs{p}", [P, JT, D]) for p in range(2)]
        xt = [ph.sb(f"xt{p}", [P, DC, JC]) for p in range(2)]
        gate = [ph.sb(f"gate{p}", [P, JC]) for p in range(2)]
        sig = [ph.sb(f"sig{p}", [P, JC]) for p in range(2)]
        up0 = [ph.sb(f"up0{p}", [P, JC]) for p in range(2)]
        up1 = [ph.sb(f"up1{p}", [P, JC]) for p in range(2)]
        h = [ph.sb(f"h{p}", [P, NF, JC]) for p in range(2)]
        eo = [ph.sb(f"eo{p}", [P, JT, D]) for p in range(2)]
        tp = [ph.ps(f"tp{p}", [P, D]) for p in range(2)]
        pg = [ph.ps(f"pg{p}", [P, D]) for p in range(2)]
        pu = [ph.ps(f"pu{p}", [P, D]) for p in range(2)]
        po = [ph.ps(f"po{p}", [P, D]) for p in range(2)]
        mt = [tp[0], tp[1], pg[0], pg[1]]
        weights_in = [ph.sem(f"weights_in{p}") for p in range(2)]
        xs_in = [ph.sem(f"xs_in{p}") for p in range(2)]
        stored = [ph.sem(f"stored{p}") for p in range(2)]
        addr_ready, scattered, down_b_in, mt_ready, mixt_ready, bias_ready, x_added, all_stored, bias_in, tp_ready, xt_ready, gate_done, up_done = ph.sems(
            "addr_ready scattered down_b_in mt_ready mixt_ready bias_ready x_added all_stored bias_in tp_ready xt_ready gate_done up_done")
        gate_ready, up0_ready, sig_ready, up1_ready, glu_ready, h_ready, out_done, eo_ready = ph.sems(
            "gate_ready up0_ready sig_ready up1_ready glu_ready h_ready out_done eo_ready")
        block = ctx.enter_context(nc.Block())

        def job_count(eng):
            return eng.value_load(t.jobs[0:1, 0:1], min_val=FJ, max_val=NJ)

        def expert_of(eng, job):
            return eng.value_load(t.job_expert[0:1, ds(job, 1)], min_val=0, max_val=E1 - 1)

        def slots_of(job, n=JT):
            return d["slots"][ds(job * JC, n * P), :].rearrange("(s p) d -> p s d", p=P)

        def by_load(eng, job, body):
            load = eng.value_load(t.job_load[0:1, ds(job, 1)], min_val=0, max_val=T)

            def choose(n):
                if n == 1:
                    body(1)
                    return
                with eng.If(load > (n - 1) * P):
                    body(n)
                with eng.Else():
                    choose(n - 1)
            choose(JT)

        def rest(n, s):
            return 1 + JT - n if s == n - 1 else 1

        @block.sync
        def _(sp):
            sp.dma_start(down_b[:, :], d["down_b"]).then_inc(down_b_in, 16)
            sp.dma_start(bgu[:, :, :], d["gate_up_b"]).then_inc(bias_in, 16)

            def load_weights(e, p):
                sp.dma_start(wgu[p][:, :, :, :], d["gate_up"][ds(e, 1), :, :, :, :].rearrange("o p c g f -> (o p) c g f")).then_inc(weights_in[p], 16)
                sp.dma_start(wd[p][:, :, :], d["down"][ds(e, 1), :, :].rearrange("o (k p) d -> p (o k) d", p=P)).then_inc(weights_in[p], 16)

            for p in range(2):
                load_weights(expert_of(sp, p), p)
            sp.wait_ge(scattered, 16 * K1 * TT)
            for p in range(2):
                sp.dma_start(xs[p][:, :, :], slots_of(p)).then_inc(xs_in[p], 16)
            n = job_count(sp)
            with sp.Fori(1, NJ // 2) as j:
                for p in range(2):
                    job = 2 * j + p
                    with sp.If(n > job):
                        e = expert_of(sp, job)
                        sp.wait_ge(tp_ready, JT * (job - 1))
                        sp.dma_start(xs[p][:, :, :], slots_of(job)).then_inc(xs_in[p], 16)
                        sp.wait_ge(out_done, JT * (job - 1))
                        load_weights(e, p)

        @block.gpsimd
        def _(pool):
            pool.tensor_scalar(addr_f[:, :, :], t.addr[:, :, :], -1.0, None, ALU.add).then_inc(addr_ready, 1)
            pool.wait_ge(addr_ready, 1)
            pool.tensor_copy(to[:, :, :], addr_f[:, :, :]).then_inc(addr_ready, 1)
            pool.wait_ge(addr_ready, 2)
            pool.sem_inc(addr_ready, 1)
            for i in range(TT):
                for k in range(K1):
                    pool.indirect_dma_start(out=d["slots"], out_offset=bass.IndirectOffsetOnAxis(ap=to[:, i, k:k + 1], axis=0),
                                            in_=t.xn[:, i, :], in_offset=None, bounds_check=SLOTS - 1, oob_is_err=False).then_inc(scattered, 16)

        @block.scalar
        def _(act):
            n = job_count(act)
            for k in range(DC):
                act.wait_ge(mt_ready, k + 1)
                act.activation(mixt[:, k * D:(k + 1) * D], mt[k][0:E1, :], ACT.Copy).then_inc(mixt_ready, 1)

            def copy_rows(job, p):
                for s in range(JT):
                    act.wait_ge(tp_ready, JT * job + s + 1)
                    act.activation(xt[p][:, :, s * P:(s + 1) * P], tp[(JT * p + s) % 2][:, :].rearrange("p (c s) -> p c s", c=DC),
                                   ACT.Copy).then_inc(xt_ready, 1)

            act.sem_inc(glu_ready, 2)
            copy_rows(0, 0)
            with act.Fori(0, NJ // 2) as j:
                for p in range(2):
                    job = 2 * j + p

                    def sigmoids(m):
                        for k in range(NF):
                            u = NF * job + k
                            act.wait_ge(gate_ready, u + 1)
                            act.wait_ge(glu_ready, u + 1)
                            act.activation(sig[k % 2][:, 0:m * P], gate[k % 2][:, 0:m * P], ACT.Sigmoid, scale=ALPHA).then_inc(sig_ready, 1)

                    def store(m):
                        act.wait_ge(eo_ready, 2 + JT * (job + 1))
                        act.dma_start(slots_of(job, m), eo[p][:, 0:m, :]).then_inc(stored[p], 16)

                    with act.If(n > job):
                        by_load(act, job, sigmoids)
                    with act.If(n > job + 1):
                        copy_rows(job + 1, 1 - p)
                    with act.If(n > job):
                        by_load(act, job, store)
            mine = [act.value_load(t.jobs[0:1, 1 + p:2 + p], min_val=FJ // 2, max_val=NJ // 2) for p in range(2)]
            for p in range(2):
                act.wait_ge(stored[p], 16 * mine[p])
                act.sem_inc(all_stored, 1)

        @block.vector
        def _(dve):
            dve.sem_inc(eo_ready, 2)
            dve.sem_inc(up0_ready, 2)
            n = job_count(dve)
            with dve.Fori(0, TT // 2) as j:
                for p in range(2):
                    i = 2 * j + p
                    dve.wait_ge(bias_ready, i + 1)
                    dve.scalar_tensor_tensor(out=row(t.x, i), in0=po[p][:, :], scalar=t.gates[:, 3:4], in1=row(t.x, i),
                                             op0=ALU.mult, op1=ALU.add).then_inc(x_added, 1)
            dve.wait_ge(bias_in, 16)

            def one_job(job, j, p):
                e = expert_of(dve, job)
                by_load(dve, job, lambda m: hidden_and_out(job, j, p, e, m * P, m))

            def hidden_and_out(job, j, p, e, w, m):
                def clamp_gate(k):
                    dve.wait_ge(gate_done, NF * job + k + 1)
                    dve.tensor_scalar(gate[k % 2][:, 0:w], pg[k % 2][:, 0:w], bgu[:, ds(e, 1), k:k + 1].rearrange("p o k -> p (o k)"),
                                      LIMIT, ALU.add, ALU.min).then_inc(gate_ready, 1)

                def clamp_up(k):
                    u = NF * job + k
                    dve.wait_ge(up_done, u + 1)
                    dve.tensor_scalar(up0[k % 2][:, 0:w], pu[k % 2][:, 0:w], bgu[:, ds(e, 1), NF + k:NF + k + 1].rearrange("p o k -> p (o k)"),
                                      LIMIT, ALU.add, ALU.min).then_inc(up0_ready, 1)
                    dve.wait_ge(up0_ready, 2 + u + 1)
                    dve.tensor_scalar(up1[k % 2][:, 0:w], up0[k % 2][:, 0:w], -LIMIT, 1.0, ALU.max, ALU.add).then_inc(up1_ready, 1)

                def glu(k):
                    u = NF * job + k
                    dve.wait_ge(sig_ready, u + 1)
                    dve.tensor_tensor(gate[k % 2][:, 0:w], gate[k % 2][:, 0:w], sig[k % 2][:, 0:w], ALU.mult).then_inc(glu_ready, 1)
                    dve.wait_ge(glu_ready, 2 + u + 1)
                    dve.wait_ge(up1_ready, u + 1)
                    dve.tensor_tensor(h[p][:, k, 0:w], gate[k % 2][:, 0:w], up1[k % 2][:, 0:w], ALU.mult).then_inc(h_ready, 1)
                    dve.wait_ge(h_ready, u + 1)

                for k in range(NF):
                    clamp_gate(k)
                    if k:
                        glu(k - 1)
                    clamp_up(k)
                glu(NF - 1)
                if j is not None:
                    dve.wait_ge(stored[p], 16 * j)
                for s in range(m):
                    dve.wait_ge(out_done, JT * job + s + 1)
                    dve.tensor_copy(eo[p][:, s, :], po[(JT * p + s) % 2][:, :]).then_inc(eo_ready, rest(m, s))

            for p in range(2):
                one_job(p, None, p)
            with dve.Fori(1, NJ // 2) as j:
                for p in range(2):
                    with dve.If(n > 2 * j + p):
                        one_job(2 * j + p, j, p)

        @block.tensor
        def _(pe):
            pe.sem_inc(xt_ready, 2)
            n = job_count(pe)

            def transposes(j, job, p):
                pe.wait_ge(xs_in[p], 16 * (j + 1))
                for s in range(JT):
                    pe.wait_ge(xt_ready, JT * job + s + 1)
                    transposed_tile(pe, tp[(JT * p + s) % 2], xs[p][:, s, :], t).then_inc(tp_ready, 1)

            def up(j, job, p, m):
                pe.wait_ge(weights_in[p], 32 * (j + 1))
                pe.wait_ge(xt_ready, 2 + JT * (job + 1))
                for k in range(NF):
                    pe.wait_ge(up0_ready, NF * job + k + 1)
                    for half, psum, done in ((0, pg, gate_done), (1, pu, up_done)):
                        for c in range(DC):
                            mm = pe.matmul(psum[k % 2][:, 0:m * P], wgu[p][:, c, half, k * P:(k + 1) * P], xt[p][:, c, 0:m * P], start=(c == 0), stop=(c == DC - 1))
                        mm.then_inc(done, 1)

            def down(job, p, m):
                pe.wait_ge(h_ready, NF * (job + 1))
                for s in range(m):
                    pe.wait_ge(eo_ready, JT * job + s + 1)
                    for k in range(NF):
                        mm = pe.matmul(po[(JT * p + s) % 2][:, :], h[p][:, k, s * P:(s + 1) * P], wd[p][:, k, :], start=(k == 0), stop=(k == NF - 1))
                    mm.then_inc(out_done, rest(m, s))

            for k in range(DC):
                for i in range(DC * k, DC * (k + 1)):
                    mm = pe.transpose(mt[k][0:E1, (i % DC) * P:(i % DC + 1) * P], t.mix[:, i, :], t.ident[:, :])
                mm.then_inc(mt_ready, 1)
            pe.wait_ge(down_b_in, 16)
            for i in range(TT):
                if i % DC == 0:
                    pe.wait_ge(mixt_ready, i // DC + 1)
                if i >= 2:
                    pe.wait_ge(x_added, i - 1)
                pe.matmul(po[i % 2][:, :], mixt[:, i * P:(i + 1) * P], down_b[:, :], start=True, stop=True).then_inc(bias_ready, 1)
            pe.wait_ge(x_added, TT)
            transposes(0, 0, 0)
            with pe.Fori(0, NJ // 2) as j:
                for p in range(2):
                    job = 2 * j + p
                    with pe.If(n > job):
                        by_load(pe, job, lambda m: up(j, job, p, m))
                    with pe.If(n > job + 1):
                        transposes(j + p, job + 1, 1 - p)
                    with pe.If(n > job):
                        by_load(pe, job, lambda m: down(job, p, m))


def combine_and_store(nc, t, d):
    with ExitStack() as ctx:
        ph = Phase(nc, ctx, "y_")
        addr_f = ph.sb("addr_f", [P, TT, 8])
        frm = ph.sb("frm", [P, TT, 8], U32)
        y = ph.sb("y", [P, TT, K1, D])
        addr_ready, y_added, tile_done, stored = ph.sems("addr_ready y_added tile_done stored")
        gathered = [ph.sem(f"gathered{i}") for i in range(TT)]
        block = ctx.enter_context(nc.Block())

        @block.gpsimd
        def _(pool):
            pool.tensor_scalar(addr_f[:, :, :], t.addr[:, :, :], -1.0, None, ALU.add).then_inc(addr_ready, 1)
            pool.wait_ge(addr_ready, 1)
            pool.tensor_copy(frm[:, :, :], addr_f[:, :, :]).then_inc(addr_ready, 1)
            pool.wait_ge(addr_ready, 2)
            pool.sem_inc(addr_ready, 1)
            for i in range(TT):
                for k in range(K1):
                    pool.indirect_dma_start(out=y[:, i, k, :], out_offset=None, in_=d["slots"],
                                            in_offset=bass.IndirectOffsetOnAxis(ap=frm[:, i, k:k + 1], axis=0),
                                            bounds_check=SLOTS - 1, oob_is_err=False).then_inc(gathered[i], 16)

        @block.vector
        def _(dve):
            for i in range(TT):
                dve.wait_ge(gathered[i], 16 * K1)
                for k in range(K1):
                    if k:
                        dve.wait_ge(y_added, (K1 - 1) * i + k)
                    ins = dve.scalar_tensor_tensor(out=t.x[:, i, :], in0=y[:, i, k, :], scalar=t.weight[:, i, k:k + 1], in1=t.x[:, i, :],
                                                   op0=ALU.mult, op1=ALU.add)
                    ins.then_inc(tile_done if k == K1 - 1 else y_added, 1)

        @block.sync
        def _(sp):
            for i in range(TT):
                sp.wait_ge(tile_done, i + 1)
                b, s = i // ST, i % ST
                sp.dma_start(d["out"][b, s * P:(s + 1) * P, :], t.x[:, i, :]).then_inc(stored, 16)
            sp.wait_ge(stored, 16 * TT)


def build(nc, d):
    d["slots"] = nc.dram_tensor("expert_slots", (SLOTS, D), F32, kind="Internal").ap()
    with ExitStack() as ctx:
        ph = Phase(nc, ctx, "g_")
        t = Shared()
        t.x = ph.sb("x", [P, TT, D])
        t.mv = ph.sb("mv", [P, TT, 2])
        t.vareps = ph.sb("vareps", [P, TT])
        t.rstd = ph.sb("rstd", [P, TT])
        t.minus_half = ph.sb("minus_half", [P, TT])
        t.gates = ph.sb("gates", [P, 4])
        t.ident = ph.sb("ident", [P, P])
        t.before = ph.sb("before", [P, P])
        t.ones = ph.sb("ones", [P, P])
        t.mv_at = lambda i, k: t.mv[:, ds(i, 1), k:k + 1].rearrange("p o d -> p (o d)")
        t.rstd_at = lambda i: t.rstd[:, ds(i, 1)]
        load_constants(nc, t, d)
        layer0(nc, t, d)
        layer1_attention(nc, t, d)
        moe1(nc, t, d)


def kernel(**inputs):
    import numpy as np
    import concourse.bacc as _bacc
    from concourse.bass_utils import run_bass_kernel_spmd as _run

    a = {k: np.ascontiguousarray(v) for k, v in inputs.items()}

    def chunked(w):
        e, f, dm = w.shape
        return np.ascontiguousarray(w.reshape(e, f, dm // 128, 128).transpose(0, 3, 2, 1))

    wo = np.zeros((128, NH // 4, D), np.float32)
    for h in range(NH):
        wo[32 * (h % 4):32 * (h % 4) + HD, h // 4, :] = a["L1_xattn_Wo"][HD * h:HD * (h + 1), :]
    inv = 1.0 / 10000.0 ** (np.arange(0, HD, 2, dtype=np.float32) / HD)
    angle = np.outer(np.arange(S, dtype=np.float32), inv)
    angle = np.concatenate([angle, angle], -1)
    sign = np.where(np.arange(HD) < HD // 2, -1.0, 1.0).astype(np.float32)
    cos, sin = (np.tile(x.astype(np.float32).T, (128 // HD, 1)) for x in (np.cos(angle), np.sin(angle) * sign))
    rope = np.stack([cos, sin], 1)
    rep = np.zeros((128, 2, 2, 4, 128), np.float32)
    for a1 in range(4):
        for a0 in range(2):
            for j in range(4):
                for r in range(HD):
                    rep[HD * (2 * a1 + a0) + r, 0, j % 2, a1, 64 * a0 + HD * j + r] = HD ** -0.5
                    rep[HD * (2 * a1 + a0) + r, 1, j // 2, a1, 64 * a0 + HD * j + r] = 1
    head_gate = np.zeros((128, NH // 2, 4), np.float32)
    head_gate[:, :, 2:4] = a["L1_xattn_gate"].reshape(NH // 2, 2)

    arrays = {
        "x": a["x"],
        "ctx": a["ctx_2048"],
        "ctx_t": np.ascontiguousarray(a["ctx_2048"].transpose(0, 2, 1)),
        "gates": np.ascontiguousarray(np.broadcast_to(np.concatenate([a["g_xattn"][0:1], a["g_ffn"][0:1], a["g_xattn"][1:2], a["g_ffn"][1:2]]), (128, 4))),
        "ident": np.eye(128, dtype=np.float32),
        "gate_wt": np.ascontiguousarray(a["L0_ffn_gate_w"].T),
        "slot_base": np.broadcast_to(np.arange(64, dtype=np.float32) * CAP + 1, (128, 64)).copy(),
        "sh_gate": np.ascontiguousarray(a["L0_ffn_sh_gate"].T),
        "sh_up": np.ascontiguousarray(a["L0_ffn_sh_up"].T),
        "sh_down": np.ascontiguousarray(a["L0_ffn_sh_down"].T),
        "w_gate": chunked(a["L0_ffn_w_gate"]),
        "w_up": chunked(a["L0_ffn_w_up"]),
        "w_down": np.ascontiguousarray(a["L0_ffn_w_down"].transpose(0, 2, 1)),
        "mask": a["mask_Bx1xSxS_fk0"].reshape(B, S, S),
        "wq": a["L1_xattn_Wq"], "wk": a["L1_xattn_Wk"], "wv": a["L1_xattn_Wv"],
        "wo": wo, "rope": rope, "rep": rep.reshape(128, -1), "head_gate": head_gate,
        "router_t": np.ascontiguousarray(a["L1_ffn_router_weight"].T),
        "router_b": np.broadcast_to(a["L1_ffn_router_bias"], (128, E1)).copy(),
        "gate_up": np.ascontiguousarray(a["L1_ffn_gate_up_proj"].reshape(E1, DC, 128, I1, 2).transpose(0, 2, 1, 4, 3)),
        "gate_up_b": np.ascontiguousarray(a["L1_ffn_gate_up_proj_bias"].reshape(E1, I1 // 128, 128, 2).transpose(2, 0, 3, 1)).reshape(128, E1, 2 * I1 // 128),
        "down": a["L1_ffn_down_proj"],
        "down_b": a["L1_ffn_down_proj_bias"],
        "job_starts": np.broadcast_to(np.arange(MJ, dtype=np.float32) * JC, (128, E1, MJ)).copy(),
        "up_to": np.broadcast_to(np.tril(np.ones((E1, E1), np.float32)), (128, E1, E1)).copy(),
        "job_number": np.broadcast_to(np.arange(NJ, dtype=np.float32), (128, NJ)).copy(),
        "before": np.triu(np.ones((128, 128), np.float32), 1),
    }
    nc = _bacc.Bacc("TRN2", target_bir_lowering=False, num_devices=1)
    d = {n: nc.dram_tensor("in_" + n, v.shape, mybir.dt.from_np(v.dtype), kind="ExternalInput").ap() for n, v in arrays.items()}
    d["out"] = nc.dram_tensor("out_0", a["x"].shape, F32, kind="ExternalOutput").ap()
    build(nc, d)
    r = _run(nc, [{"in_" + n: v for n, v in arrays.items()}], core_ids=[0])
    return r.results[0]["out_0"]
```
